# Optimizing a Trainium2 kernel written in Bass

```python
import numpy as np
import jax
import jax.numpy as jnp

def _softmax(x, axis=-1):
    return jax.nn.softmax(x, axis=axis)

def _gelu(x):
    return jax.nn.gelu(x, approximate=True)

def _silu(x):
    return jax.nn.silu(x)

def _sigmoid(x):
    return jax.nn.sigmoid(x)

def _layernorm(x, axis=-1, eps=1e-05):
    m = jnp.mean(x, axis=axis, keepdims=True)
    v = jnp.var(x, axis=axis, keepdims=True)
    return (x - m) / jnp.sqrt(v + eps)

def _scatter_add(tgt, idx, src, axis=0):
    return tgt.at[idx].add(src)

def _segment_sum(src, seg, n):
    return jax.ops.segment_sum(src, seg, n)
kernel_name = 'mk_seq_postln_d4_jaxref_r8_20bae8'

def setup_inputs(seed: int=0):
    np.random.seed(seed)
    _w = jnp.asarray

    def _L0_attn_setup():
        import jax, jax.numpy as jnp
        import numpy as np
        from jax import lax
        B, T, HID, H, DK, DV, K = (2, 256, 128, 16, 64, 64, 4)
        SCALE = float(DK) ** (-0.5)
        EPS = 1e-05

        def _causal_dwconv_silu(z, w, b):
            zc = z.transpose(0, 2, 1)
            y = lax.conv_general_dilated(zc, w, (1,), [(K - 1, 0)], dimension_numbers=('NCH', 'OIH', 'NCH'), feature_group_count=zc.shape[1])
            return jax.nn.silu((y + b[None, :, None]).transpose(0, 2, 1))
        key = jax.random.key(seed)
        ks = jax.random.split(key, 12)
        n = lambda k, sh, s=0.02: jax.random.normal(k, sh, jnp.float32) * s
        return {'x': jax.random.normal(ks[0], (B, T, HID), jnp.float32), 'Wq': n(ks[1], (H * DK, HID)), 'Wk': n(ks[2], (H * DK, HID)), 'Wv': n(ks[3], (H * DV, HID)), 'Wa': n(ks[4], (H * DV, HID)), 'ba': jnp.zeros((H * DV,), jnp.float32), 'Wb': n(ks[5], (H, HID)), 'bb': jnp.zeros((H,), jnp.float32), 'Wg': n(ks[6], (H * DV, HID)), 'Wo': n(ks[7], (HID, H * DV)), 'qcw': n(ks[8], (H * DK, 1, K), 0.3), 'qcb': jnp.zeros((H * DK,), jnp.float32), 'kcw': n(ks[9], (H * DK, 1, K), 0.3), 'kcb': jnp.zeros((H * DK,), jnp.float32), 'vcw': n(ks[10], (H * DV, 1, K), 0.3), 'vcb': jnp.zeros((H * DV,), jnp.float32), 'ln_w': jnp.ones((DV,), jnp.float32), 'ln_b': jnp.zeros((DV,), jnp.float32)}
    _L0_attn_in = _L0_attn_setup()

    def _L0_ffn_setup():
        import jax, jax.numpy as jnp
        import numpy as np
        D_IN, D_HID = (128, 512)

        def _ternary(key, shape):
            return jax.random.randint(key, shape, -1, 2).astype(jnp.float32)

        def _tlin(x, w, s):
            return jnp.einsum('bsi,oi->bso', x, w) * s
        key = jax.random.key(seed)
        ks = jax.random.split(key, 12)
        inv = lambda fan: 1.0 / np.sqrt(fan).astype(np.float32)
        return {'x': jax.random.normal(ks[0], (4, 256, D_IN), dtype=jnp.float32), 'w1_w': _ternary(ks[1], (D_HID, D_IN)), 'w1_s': jax.random.uniform(ks[2], (D_HID,), dtype=jnp.float32) * inv(D_IN), 'w2_w': _ternary(ks[3], (D_HID, D_IN)), 'w2_s': jax.random.uniform(ks[4], (D_HID,), dtype=jnp.float32) * inv(D_IN), 'h1_w': _ternary(ks[5], (D_HID, D_HID)), 'h1_s': jax.random.uniform(ks[6], (D_HID,), dtype=jnp.float32) * inv(D_HID), 'h2_w': _ternary(ks[7], (D_HID, D_HID)), 'h2_s': jax.random.uniform(ks[8], (D_HID,), dtype=jnp.float32) * inv(D_HID), 'w3_w': _ternary(ks[9], (D_IN, D_HID)), 'w3_s': jax.random.uniform(ks[10], (D_IN,), dtype=jnp.float32) * inv(D_HID)}
    _L0_ffn_in = _L0_ffn_setup()

    def _L1_attn_setup():
        import jax, jax.numpy as jnp
        import numpy as np
        D_MODEL = 128
        N_HEADS = 16
        D_K = D_MODEL // N_HEADS
        MAX_POS = 64
        ATT_SPAN = MAX_POS
        B, T = (4, 128)
        SCALE_FACTOR = 3

        def _heads(y):
            b, t, _ = y.shape
            return y.reshape(b, t, N_HEADS, D_K).transpose(0, 2, 1, 3)
        key = jax.random.key(seed)
        ks = jax.random.split(key, 16)
        init = lambda k, shape: jax.random.normal(k, shape, dtype=jnp.float32) * 0.02
        inp = {'x': jax.random.normal(ks[0], (B, T, D_MODEL), dtype=jnp.float32), 'Wq': init(ks[1], (D_MODEL, D_MODEL)), 'bq': jnp.zeros((D_MODEL,), jnp.float32), 'Wk': init(ks[2], (D_MODEL, D_MODEL)), 'bk': jnp.zeros((D_MODEL,), jnp.float32), 'Wv': init(ks[3], (D_MODEL, D_MODEL)), 'bv': jnp.zeros((D_MODEL,), jnp.float32), 'Wo': init(ks[4], (D_MODEL, D_MODEL)), 'bo': jnp.zeros((D_MODEL,), jnp.float32), 'Wpk': init(ks[5], (D_MODEL, D_MODEL)), 'bpk': jnp.zeros((D_MODEL,), jnp.float32), 'Wpq': init(ks[6], (D_MODEL, D_MODEL)), 'bpq': jnp.zeros((D_MODEL,), jnp.float32), 'rel_emb': init(ks[7], (2 * ATT_SPAN, D_MODEL))}
        return inp
    _L1_attn_in = _L1_attn_setup()

    def _L1_ffn_setup():
        import jax, jax.numpy as jnp
        import numpy as np
        E = 8
        TOPK = 2
        PRIME = 11
        HASH_OFF = 7919
        N_SHARED = 1
        key = jax.random.key(seed)
        ks = jax.random.split(key, 8)
        B, T, C, Hs, Hr = (4, 1024, 128, 256, 128)
        sc = lambda k, shape, fan: jax.random.normal(k, shape, jnp.float32) * fan ** (-0.5)
        return {'x': jax.random.normal(ks[0], (B, T, C), jnp.float32), 't_emb': jax.random.normal(ks[1], (B, C), jnp.float32), 'sw1': sc(ks[2], (C, Hs), C), 'sb1': jnp.zeros((Hs,), jnp.float32), 'sw3': sc(ks[3], (C, Hs), C), 'sb3': jnp.zeros((Hs,), jnp.float32), 'sw2': sc(ks[4], (Hs, C), Hs), 'sb2': jnp.zeros((C,), jnp.float32), 'w1': sc(ks[5], (E, C, Hr), C), 'b1': jnp.zeros((E, Hr), jnp.float32), 'w2': sc(ks[6], (E, Hr, C), Hr), 'b2': jnp.zeros((E, C), jnp.float32)}
    _L1_ffn_in = _L1_ffn_setup()

    def _L2_attn_setup():
        import jax, jax.numpy as jnp
        import numpy as np
        B, T, C, HS = (4, 256, 128, 16)
        H = C // HS
        LAYER_ID, N_LAYER = (2, 24)
        D_MIX, D_DECAY = (32, 64)
        LN_EPS = 1e-05

        def _wkv6(r, k, v, w, u):
            wd = jnp.exp(-jnp.exp(w))
            rT, kT, vT, wT = (a.transpose(1, 0, 2, 3) for a in (r, k, v, wd))

            def step(S, ins):
                r_t, k_t, v_t, w_t = ins
                kv = jnp.einsum('bhi,bhj->bhij', k_t, v_t)
                y_t = jnp.einsum('bhi,bhij->bhj', r_t, S + u[None, :, :, None] * kv)
                return (w_t[..., None] * S + kv, y_t)
            S0 = jnp.zeros((r.shape[0], H, HS, HS), r.dtype)
            _, ys = jax.lax.scan(step, S0, (rT, kT, vT, wT))
            return ys.transpose(1, 0, 2, 3)
        key = jax.random.key(seed)
        ks = jax.random.split(key, 8)
        r01 = LAYER_ID / (N_LAYER - 1)
        r10 = 1.0 - LAYER_ID / N_LAYER
        ddd = np.arange(C, dtype=np.float64) / C
        tm = lambda p: (1.0 - ddd ** p).reshape(1, 1, C).astype(np.float32)
        time_maa_x = tm(r10)
        time_maa_w = tm(r10)
        time_maa_k = tm(r10)
        time_maa_v = (1.0 - (ddd ** r10 + 0.3 * r01)).reshape(1, 1, C).astype(np.float32)
        time_maa_r = tm(0.5 * r10)
        n = np.arange(C, dtype=np.float64)
        decay = (-6.0 + 5.0 * (n / (C - 1)) ** (0.7 + 1.3 * r01)).reshape(1, 1, C).astype(np.float32)
        zig = ((n + 1) % 3 - 1) * 0.1
        faaaa = (r01 * (1.0 - n / (C - 1)) + zig).reshape(H, HS).astype(np.float32)
        u01 = lambda k, s: jax.random.uniform(k, s, jnp.float32, -0.01, 0.01)
        return {'x': jax.random.normal(ks[0], (B, T, C), jnp.float32), 'time_maa_x': jnp.asarray(time_maa_x), 'time_maa_w': jnp.asarray(time_maa_w), 'time_maa_k': jnp.asarray(time_maa_k), 'time_maa_v': jnp.asarray(time_maa_v), 'time_maa_r': jnp.asarray(time_maa_r), 'time_maa_w1': u01(ks[1], (C, D_MIX * 4)), 'time_maa_w2': u01(ks[2], (4, D_MIX, C)), 'time_decay': jnp.asarray(decay), 'time_decay_w1': u01(ks[3], (C, D_DECAY)), 'time_decay_w2': u01(ks[4], (D_DECAY, C)), 'time_faaaa': jnp.asarray(faaaa), 'W_r': jax.random.normal(ks[5], (C, C), jnp.float32) * 0.02, 'W_k': jax.random.normal(ks[6], (C, C), jnp.float32) * 0.02, 'W_v': jax.random.normal(ks[7], (C, C), jnp.float32) * 0.02, 'W_o': jax.random.normal(jax.random.fold_in(key, 99), (C, C), jnp.float32) * 0.02, 'ln_g': jnp.ones((C,), jnp.float32), 'ln_b': jnp.zeros((C,), jnp.float32)}
    _L2_attn_in = _L2_attn_setup()

    def _L2_ffn_setup():
        import jax, jax.numpy as jnp
        import numpy as np
        key = jax.random.key(seed)
        k1, k2, k3, k4, k5 = jax.random.split(key, 5)
        d_in, d_out, r = (128, 128, 32)
        x = jax.random.normal(k1, (8, 1024, d_in), dtype=jnp.float32)
        W = jax.random.normal(k2, (d_out, d_in), dtype=jnp.float32) * (1.0 / np.sqrt(d_in))
        b = jax.random.normal(k3, (d_out,), dtype=jnp.float32) * 0.01
        V_r = jax.random.normal(k4, (d_in, r), dtype=jnp.float32) * (1.0 / np.sqrt(d_in))
        C = jax.random.normal(k5, (d_out, r), dtype=jnp.float32) * (1.0 / np.sqrt(r))
        return {'x': x, 'W': W, 'b': b, 'V_r': V_r, 'C': C}
    _L2_ffn_in = _L2_ffn_setup()

    def _L3_attn_setup():
        import jax, jax.numpy as jnp
        import numpy as np
        HIDDEN = 128
        N_HEAD = 16
        HEAD_DIM = HIDDEN // N_HEAD
        BATCH = 1
        SEQ = 512
        THETA = 10000.0

        def _rope_cos_sin(seq_len, head_dim, dtype=jnp.float32):
            inv_freq = 1.0 / THETA ** (jnp.arange(0, head_dim, 2, dtype=dtype) / head_dim)
            t = jnp.arange(seq_len, dtype=dtype)
            freqs = jnp.outer(t, inv_freq)
            return (jnp.cos(freqs), jnp.sin(freqs))

        def _apply_rope(x, cos, sin):
            x2 = x.reshape(*x.shape[:-1], -1, 2)
            x_re, x_im = (x2[..., 0], x2[..., 1])
            c = cos[None, :, None, :]
            s = sin[None, :, None, :]
            out_re = x_re * c - x_im * s
            out_im = x_re * s + x_im * c
            out = jnp.stack([out_re, out_im], axis=-1)
            return out.reshape(x.shape)
        key = jax.random.key(seed)
        kx, kq, kk, kv = jax.random.split(key, 4)
        scale = 1.0 / np.sqrt(HIDDEN)
        return {'x': jax.random.normal(kx, (BATCH, SEQ, HIDDEN), dtype=jnp.float32), 'wq': jax.random.normal(kq, (HIDDEN, HIDDEN), dtype=jnp.float32) * scale, 'wk': jax.random.normal(kk, (HIDDEN, HIDDEN), dtype=jnp.float32) * scale, 'wv': jax.random.normal(kv, (HIDDEN, HIDDEN), dtype=jnp.float32) * scale}
    _L3_attn_in = _L3_attn_setup()

    def _L3_ffn_setup():
        import jax, jax.numpy as jnp
        import numpy as np
        D = 128
        E = 12
        HS = 2 * D
        HR = 3 * D
        TAU = 1.5

        def _geglu(h):
            a, g = jnp.split(h, 2, axis=-1)
            return a * jax.nn.gelu(g, approximate=False)
        key = jax.random.key(seed)
        ks = jax.random.split(key, 12)

        def xavier(k, shape):
            fan_in, fan_out = (shape[-2], shape[-1])
            lim = jnp.sqrt(6.0 / (fan_in + fan_out))
            return jax.random.uniform(k, shape, jnp.float32, -lim, lim)
        x = jax.random.normal(ks[0], (2, 128, D), jnp.float32)
        Ws1 = xavier(ks[1], (D, 2 * HS))
        bs1 = jnp.zeros((2 * HS,), jnp.float32)
        Ws2 = xavier(ks[2], (HS, D))
        bs2 = jnp.zeros((D,), jnp.float32)
        We1 = xavier(ks[3], (E, D, 2 * HR))
        be1 = jnp.zeros((E, 2 * HR), jnp.float32)
        We2 = xavier(ks[4], (E, HR, D))
        be2 = jnp.zeros((E, D), jnp.float32)
        Wr = xavier(ks[5], (D, E))
        br = jnp.zeros((E,), jnp.float32)
        return {'x': x, 'Ws1': Ws1, 'bs1': bs1, 'Ws2': Ws2, 'bs2': bs2, 'We1': We1, 'be1': be1, 'We2': We2, 'be2': be2, 'Wr': Wr, 'br': br}
    _L3_ffn_in = _L3_ffn_setup()
    _d = {'L0_attn_x': _L0_attn_in['x'], 'L0_attn_Wq': _L0_attn_in['Wq'], 'L0_attn_Wk': _L0_attn_in['Wk'], 'L0_attn_Wv': _L0_attn_in['Wv'], 'L0_attn_Wa': _L0_attn_in['Wa'], 'L0_attn_ba': _L0_attn_in['ba'], 'L0_attn_Wb': _L0_attn_in['Wb'], 'L0_attn_bb': _L0_attn_in['bb'], 'L0_attn_Wg': _L0_attn_in['Wg'], 'L0_attn_Wo': _L0_attn_in['Wo'], 'L0_attn_qcw': _L0_attn_in['qcw'], 'L0_attn_qcb': _L0_attn_in['qcb'], 'L0_attn_kcw': _L0_attn_in['kcw'], 'L0_attn_kcb': _L0_attn_in['kcb'], 'L0_attn_vcw': _L0_attn_in['vcw'], 'L0_attn_vcb': _L0_attn_in['vcb'], 'L0_attn_ln_w': _L0_attn_in['ln_w'], 'L0_attn_ln_b': _L0_attn_in['ln_b'], 'L0_ffn_w1_w': _L0_ffn_in['w1_w'], 'L0_ffn_w1_s': _L0_ffn_in['w1_s'], 'L0_ffn_w2_w': _L0_ffn_in['w2_w'], 'L0_ffn_w2_s': _L0_ffn_in['w2_s'], 'L0_ffn_h1_w': _L0_ffn_in['h1_w'], 'L0_ffn_h1_s': _L0_ffn_in['h1_s'], 'L0_ffn_h2_w': _L0_ffn_in['h2_w'], 'L0_ffn_h2_s': _L0_ffn_in['h2_s'], 'L0_ffn_w3_w': _L0_ffn_in['w3_w'], 'L0_ffn_w3_s': _L0_ffn_in['w3_s'], 'L1_attn_Wq': _L1_attn_in['Wq'], 'L1_attn_bq': _L1_attn_in['bq'], 'L1_attn_Wk': _L1_attn_in['Wk'], 'L1_attn_bk': _L1_attn_in['bk'], 'L1_attn_Wv': _L1_attn_in['Wv'], 'L1_attn_bv': _L1_attn_in['bv'], 'L1_attn_Wo': _L1_attn_in['Wo'], 'L1_attn_bo': _L1_attn_in['bo'], 'L1_attn_Wpk': _L1_attn_in['Wpk'], 'L1_attn_bpk': _L1_attn_in['bpk'], 'L1_attn_Wpq': _L1_attn_in['Wpq'], 'L1_attn_bpq': _L1_attn_in['bpq'], 'L1_attn_rel_emb': _L1_attn_in['rel_emb'], 'L1_ffn_t_emb': _L1_ffn_in['t_emb'], 'L1_ffn_sw1': _L1_ffn_in['sw1'], 'L1_ffn_sb1': _L1_ffn_in['sb1'], 'L1_ffn_sw3': _L1_ffn_in['sw3'], 'L1_ffn_sb3': _L1_ffn_in['sb3'], 'L1_ffn_sw2': _L1_ffn_in['sw2'], 'L1_ffn_sb2': _L1_ffn_in['sb2'], 'L1_ffn_w1': _L1_ffn_in['w1'], 'L1_ffn_b1': _L1_ffn_in['b1'], 'L1_ffn_w2': _L1_ffn_in['w2'], 'L1_ffn_b2': _L1_ffn_in['b2'], 'L2_attn_time_maa_x': _L2_attn_in['time_maa_x'], 'L2_attn_time_maa_w': _L2_attn_in['time_maa_w'], 'L2_attn_time_maa_k': _L2_attn_in['time_maa_k'], 'L2_attn_time_maa_v': _L2_attn_in['time_maa_v'], 'L2_attn_time_maa_r': _L2_attn_in['time_maa_r'], 'L2_attn_time_maa_w1': _L2_attn_in['time_maa_w1'], 'L2_attn_time_maa_w2': _L2_attn_in['time_maa_w2'], 'L2_attn_time_decay': _L2_attn_in['time_decay'], 'L2_attn_time_decay_w1': _L2_attn_in['time_decay_w1'], 'L2_attn_time_decay_w2': _L2_attn_in['time_decay_w2'], 'L2_attn_time_faaaa': _L2_attn_in['time_faaaa'], 'L2_attn_W_r': _L2_attn_in['W_r'], 'L2_attn_W_k': _L2_attn_in['W_k'], 'L2_attn_W_v': _L2_attn_in['W_v'], 'L2_attn_W_o': _L2_attn_in['W_o'], 'L2_attn_ln_g': _L2_attn_in['ln_g'], 'L2_attn_ln_b': _L2_attn_in['ln_b'], 'L2_ffn_W': _L2_ffn_in['W'], 'L2_ffn_b': _L2_ffn_in['b'], 'L2_ffn_V_r': _L2_ffn_in['V_r'], 'L2_ffn_C': _L2_ffn_in['C'], 'L3_attn_wq': _L3_attn_in['wq'], 'L3_attn_wk': _L3_attn_in['wk'], 'L3_attn_wv': _L3_attn_in['wv'], 'L3_ffn_Ws1': _L3_ffn_in['Ws1'], 'L3_ffn_bs1': _L3_ffn_in['bs1'], 'L3_ffn_Ws2': _L3_ffn_in['Ws2'], 'L3_ffn_bs2': _L3_ffn_in['bs2'], 'L3_ffn_We1': _L3_ffn_in['We1'], 'L3_ffn_be1': _L3_ffn_in['be1'], 'L3_ffn_We2': _L3_ffn_in['We2'], 'L3_ffn_be2': _L3_ffn_in['be2'], 'L3_ffn_Wr': _L3_ffn_in['Wr'], 'L3_ffn_br': _L3_ffn_in['br']}
    _x0 = _d['L0_attn_x']
    _d['L0_attn_x'] = jax.random.normal(jax.random.fold_in(jax.random.key(seed), 1), (4, 512, 128), dtype=_x0.dtype)
    del _x0
    return _d

def reference(L0_attn_x, L0_attn_Wq, L0_attn_Wk, L0_attn_Wv, L0_attn_Wa, L0_attn_ba, L0_attn_Wb, L0_attn_bb, L0_attn_Wg, L0_attn_Wo, L0_attn_qcw, L0_attn_qcb, L0_attn_kcw, L0_attn_kcb, L0_attn_vcw, L0_attn_vcb, L0_attn_ln_w, L0_attn_ln_b, L0_ffn_w1_w, L0_ffn_w1_s, L0_ffn_w2_w, L0_ffn_w2_s, L0_ffn_h1_w, L0_ffn_h1_s, L0_ffn_h2_w, L0_ffn_h2_s, L0_ffn_w3_w, L0_ffn_w3_s, L1_attn_Wq, L1_attn_bq, L1_attn_Wk, L1_attn_bk, L1_attn_Wv, L1_attn_bv, L1_attn_Wo, L1_attn_bo, L1_attn_Wpk, L1_attn_bpk, L1_attn_Wpq, L1_attn_bpq, L1_attn_rel_emb, L1_ffn_t_emb, L1_ffn_sw1, L1_ffn_sb1, L1_ffn_sw3, L1_ffn_sb3, L1_ffn_sw2, L1_ffn_sb2, L1_ffn_w1, L1_ffn_b1, L1_ffn_w2, L1_ffn_b2, L2_attn_time_maa_x, L2_attn_time_maa_w, L2_attn_time_maa_k, L2_attn_time_maa_v, L2_attn_time_maa_r, L2_attn_time_maa_w1, L2_attn_time_maa_w2, L2_attn_time_decay, L2_attn_time_decay_w1, L2_attn_time_decay_w2, L2_attn_time_faaaa, L2_attn_W_r, L2_attn_W_k, L2_attn_W_v, L2_attn_W_o, L2_attn_ln_g, L2_attn_ln_b, L2_ffn_W, L2_ffn_b, L2_ffn_V_r, L2_ffn_C, L3_attn_wq, L3_attn_wk, L3_attn_wv, L3_ffn_Ws1, L3_ffn_bs1, L3_ffn_Ws2, L3_ffn_bs2, L3_ffn_We1, L3_ffn_be1, L3_ffn_We2, L3_ffn_be2, L3_ffn_Wr, L3_ffn_br):

    def _L0_attn_ref(x, Wq, Wk, Wv, Wa, ba, Wb, bb, Wg, Wo, qcw, qcb, kcw, kcb, vcw, vcb, ln_w, ln_b):
        import jax, jax.numpy as jnp
        import numpy as np
        from jax import lax
        B, T, HID, H, DK, DV, K = (2, 256, 128, 16, 64, 64, 4)
        SCALE = float(DK) ** (-0.5)
        EPS = 1e-05

        def _causal_dwconv_silu(z, w, b):
            zc = z.transpose(0, 2, 1)
            y = lax.conv_general_dilated(zc, w, (1,), [(K - 1, 0)], dimension_numbers=('NCH', 'OIH', 'NCH'), feature_group_count=zc.shape[1])
            return jax.nn.silu((y + b[None, :, None]).transpose(0, 2, 1))
        Bb, Tt, _ = x.shape
        q = _causal_dwconv_silu(x @ Wq.T, qcw, qcb).reshape(Bb, Tt, H, DK)
        k = _causal_dwconv_silu(x @ Wk.T, kcw, kcb).reshape(Bb, Tt, H, DK) * SCALE
        v = _causal_dwconv_silu(x @ Wv.T, vcw, vcb).reshape(Bb, Tt, H, DV)
        a = jax.nn.sigmoid(x @ Wa.T + ba).reshape(Bb, Tt, H, DV)
        beta = jax.nn.sigmoid(x @ Wb.T + bb)

        def step(S, inp):
            qt, kt, vt, at, bt = inp
            err = jnp.einsum('bhij,bhj->bhi', S, kt) - vt
            S = at[..., None] * S - bt[..., None, None] * (err[..., None] * kt[:, :, None, :])
            o = jnp.einsum('bhij,bhj->bhi', S, qt)
            return (S, o)
        xs = tuple((jnp.moveaxis(t, 1, 0) for t in (q, k, v, a, beta)))
        S0 = jnp.zeros((Bb, H, DV, DK), x.dtype)
        _, o = lax.scan(step, S0, xs)
        o = jnp.moveaxis(o, 0, 1)
        mu = o.mean(-1, keepdims=True)
        var = ((o - mu) ** 2).mean(-1, keepdims=True)
        o = (o - mu) / jnp.sqrt(var + EPS) * ln_w + ln_b
        g = jax.nn.sigmoid(x @ Wg.T).reshape(Bb, Tt, H, DV)
        o = (o * g).reshape(Bb, Tt, H * DV)
        return o @ Wo.T

    def _L0_ffn_ref(x, w1_w, w1_s, w2_w, w2_s, h1_w, h1_s, h2_w, h2_s, w3_w, w3_s):
        import jax, jax.numpy as jnp
        import numpy as np
        D_IN, D_HID = (128, 512)

        def _ternary(key, shape):
            return jax.random.randint(key, shape, -1, 2).astype(jnp.float32)

        def _tlin(x, w, s):
            return jnp.einsum('bsi,oi->bso', x, w) * s
        h = jax.nn.silu(_tlin(x, w1_w, w1_s)) * _tlin(x, w2_w, w2_s)
        h = jax.nn.gelu(_tlin(h, h1_w, h1_s), approximate=False)
        h = jax.nn.gelu(_tlin(h, h2_w, h2_s), approximate=False)
        return _tlin(h, w3_w, w3_s)

    def _L1_attn_ref(x, Wq, bq, Wk, bk, Wv, bv, Wo, bo, Wpk, bpk, Wpq, bpq, rel_emb):
        import jax, jax.numpy as jnp
        import numpy as np
        D_MODEL = 128
        N_HEADS = 16
        D_K = D_MODEL // N_HEADS
        MAX_POS = 64
        ATT_SPAN = MAX_POS
        B, T = (4, 128)
        SCALE_FACTOR = 3

        def _heads(y):
            b, t, _ = y.shape
            return y.reshape(b, t, N_HEADS, D_K).transpose(0, 2, 1, 3)
        b, t, c = x.shape
        scale = 1.0 / jnp.sqrt(jnp.asarray(D_K * SCALE_FACTOR, x.dtype))
        Q = _heads(x @ Wq.T + bq)
        K = _heads(x @ Wk.T + bk)
        V = _heads(x @ Wv.T + bv)
        rel = jnp.arange(t)[None, :] - jnp.arange(t)[:, None]
        rel_pos = jnp.clip(rel + ATT_SPAN, 0, 2 * ATT_SPAN - 1)
        p2c_pos = jnp.clip(-rel + ATT_SPAN, 0, 2 * ATT_SPAN - 1)
        scores = jnp.einsum('bhqd,bhkd->bhqk', Q, K) * scale
        pos_key = (rel_emb @ Wpk.T + bpk).reshape(2 * ATT_SPAN, N_HEADS, D_K)
        c2p = jnp.einsum('bhqd,shd->bhqs', Q, pos_key) * scale
        c2p = jnp.take_along_axis(c2p, rel_pos[None, None, :, :], axis=-1)
        pos_query = (rel_emb @ Wpq.T + bpq).reshape(2 * ATT_SPAN, N_HEADS, D_K)
        p2c = jnp.einsum('bhkd,shd->bhks', K, pos_query) * scale
        p2c = jnp.take_along_axis(p2c, p2c_pos[None, None, :, :], axis=-1)
        p2c = jnp.swapaxes(p2c, -1, -2)
        scores = scores + c2p + p2c
        probs = jax.nn.softmax(scores, axis=-1)
        ctx = jnp.einsum('bhqk,bhkd->bhqd', probs, V)
        ctx = ctx.transpose(0, 2, 1, 3).reshape(b, t, c)
        return ctx @ Wo.T + bo

    def _L1_ffn_ref(x, t_emb, sw1, sb1, sw3, sb3, sw2, sb2, w1, b1, w2, b2):
        import jax, jax.numpy as jnp
        import numpy as np
        E = 8
        TOPK = 2
        PRIME = 11
        HASH_OFF = 7919
        N_SHARED = 1
        B, T, C = x.shape
        N = B * T
        xf = x.reshape(N, C)
        shared = jax.nn.silu(xf @ sw1 + sb1) * (xf @ sw3 + sb3) @ sw2 + sb2
        tok = jnp.arange(N)
        out = jnp.zeros((N, C), x.dtype)
        for k in range(TOPK):
            exp_ids = (tok * PRIME + k * HASH_OFF) % E
            sort_idx = jnp.argsort(exp_ids)
            xs = xf[sort_idx].reshape(E, N // E, C)
            h = jax.nn.gelu(jnp.einsum('enc,ech->enh', xs, w1) + b1[:, None, :], approximate=False)
            y = jnp.einsum('enh,ehc->enc', h, w2) + b2[:, None, :]
            out = out.at[sort_idx].add(y.reshape(N, C))
        out = out / TOPK
        return ((shared + out) / (N_SHARED + 1)).reshape(B, T, C)

    def _L2_attn_ref(x, time_maa_x, time_maa_w, time_maa_k, time_maa_v, time_maa_r, time_maa_w1, time_maa_w2, time_decay, time_decay_w1, time_decay_w2, time_faaaa, W_r, W_k, W_v, W_o, ln_g, ln_b):
        import jax, jax.numpy as jnp
        import numpy as np
        B, T, C, HS = (4, 256, 128, 16)
        H = C // HS
        LAYER_ID, N_LAYER = (2, 24)
        D_MIX, D_DECAY = (32, 64)
        LN_EPS = 1e-05

        def _wkv6(r, k, v, w, u):
            wd = jnp.exp(-jnp.exp(w))
            rT, kT, vT, wT = (a.transpose(1, 0, 2, 3) for a in (r, k, v, wd))

            def step(S, ins):
                r_t, k_t, v_t, w_t = ins
                kv = jnp.einsum('bhi,bhj->bhij', k_t, v_t)
                y_t = jnp.einsum('bhi,bhij->bhj', r_t, S + u[None, :, :, None] * kv)
                return (w_t[..., None] * S + kv, y_t)
            S0 = jnp.zeros((r.shape[0], H, HS, HS), r.dtype)
            _, ys = jax.lax.scan(step, S0, (rT, kT, vT, wT))
            return ys.transpose(1, 0, 2, 3)
        b, t, c = x.shape
        xx = jnp.concatenate([jnp.zeros_like(x[:, :1]), x[:, :-1]], axis=1) - x
        xxx = x + xx * time_maa_x
        m = jnp.tanh(xxx @ time_maa_w1).reshape(b, t, 4, D_MIX)
        m = jnp.einsum('btfd,fdc->fbtc', m, time_maa_w2)
        mw, mk, mv, mr = (m[0], m[1], m[2], m[3])
        xw = x + xx * (time_maa_w + mw)
        xk = x + xx * (time_maa_k + mk)
        xv = x + xx * (time_maa_v + mv)
        xr = x + xx * (time_maa_r + mr)
        r = (xr @ W_r).reshape(b, t, H, HS)
        k = (xk @ W_k).reshape(b, t, H, HS)
        v = (xv @ W_v).reshape(b, t, H, HS)
        ww = jnp.tanh(xw @ time_decay_w1) @ time_decay_w2
        w = (time_decay + ww).reshape(b, t, H, HS)
        y = _wkv6(r, k, v, w, time_faaaa).reshape(b, t, c)
        mu = jnp.mean(y, axis=-1, keepdims=True)
        var = jnp.mean(jnp.square(y - mu), axis=-1, keepdims=True)
        y = (y - mu) * jax.lax.rsqrt(var + LN_EPS) * ln_g + ln_b
        return y @ W_o

    def _L2_ffn_ref(x, W, b, V_r, C):
        import jax, jax.numpy as jnp
        import numpy as np
        base = jnp.einsum('bsd,od->bso', x, W) + b
        correction = jnp.einsum('bsr,or->bso', jnp.einsum('bsd,dr->bsr', x, V_r), C)
        return base + correction

    def _L3_attn_ref(x, wq, wk, wv):
        import jax, jax.numpy as jnp
        import numpy as np
        HIDDEN = 128
        N_HEAD = 16
        HEAD_DIM = HIDDEN // N_HEAD
        BATCH = 1
        SEQ = 512
        THETA = 10000.0

        def _rope_cos_sin(seq_len, head_dim, dtype=jnp.float32):
            inv_freq = 1.0 / THETA ** (jnp.arange(0, head_dim, 2, dtype=dtype) / head_dim)
            t = jnp.arange(seq_len, dtype=dtype)
            freqs = jnp.outer(t, inv_freq)
            return (jnp.cos(freqs), jnp.sin(freqs))

        def _apply_rope(x, cos, sin):
            x2 = x.reshape(*x.shape[:-1], -1, 2)
            x_re, x_im = (x2[..., 0], x2[..., 1])
            c = cos[None, :, None, :]
            s = sin[None, :, None, :]
            out_re = x_re * c - x_im * s
            out_im = x_re * s + x_im * c
            out = jnp.stack([out_re, out_im], axis=-1)
            return out.reshape(x.shape)
        B, S, _ = x.shape
        xq = (x @ wq.T).reshape(B, S, N_HEAD, HEAD_DIM).astype(jnp.float32)
        xk = (x @ wk.T).reshape(B, S, N_HEAD, HEAD_DIM).astype(jnp.float32)
        xv = (x @ wv.T).reshape(B, S, N_HEAD, HEAD_DIM).astype(jnp.float32)
        cos, sin = _rope_cos_sin(S, HEAD_DIM)
        q = _apply_rope(xq, cos, sin)
        k = _apply_rope(xk, cos, sin)
        scores = jnp.einsum('bqhd,bkhd->bhqk', q, k) / jnp.sqrt(jnp.asarray(HEAD_DIM, dtype=q.dtype))
        attn = jax.nn.softmax(scores, axis=-1)
        out = jnp.einsum('bhqk,bkhd->bqhd', attn, xv)
        return out.reshape(B, S, N_HEAD * HEAD_DIM)

    def _L3_ffn_ref(x, Ws1, bs1, Ws2, bs2, We1, be1, We2, be2, Wr, br):
        import jax, jax.numpy as jnp
        import numpy as np
        D = 128
        E = 12
        HS = 2 * D
        HR = 3 * D
        TAU = 1.5

        def _geglu(h):
            a, g = jnp.split(h, 2, axis=-1)
            return a * jax.nn.gelu(g, approximate=False)
        B, T, Dm = x.shape
        xf = x.reshape(-1, Dm)
        ys = _geglu(xf @ Ws1 + bs1) @ Ws2 + bs2
        logits = (xf @ Wr + br) / TAU
        top_val, top_idx = jax.lax.top_k(logits, 2)
        top_w = jax.nn.softmax(top_val, axis=-1)
        onehot = jax.nn.one_hot(top_idx, E, dtype=x.dtype)
        w = jnp.einsum('nke,nk->ne', onehot, top_w)
        h = jnp.einsum('nd,edh->enh', xf, We1) + be1[:, None, :]
        act = _geglu(h)
        yE = jnp.einsum('enh,ehd->end', act, We2) + be2[:, None, :]
        yr = jnp.einsum('end,ne->nd', yE, w)
        return (ys + yr).reshape(B, T, Dm)
    x = L0_attn_x
    x = _layernorm(x + _L0_attn_ref(x, L0_attn_Wq, L0_attn_Wk, L0_attn_Wv, L0_attn_Wa, L0_attn_ba, L0_attn_Wb, L0_attn_bb, L0_attn_Wg, L0_attn_Wo, L0_attn_qcw, L0_attn_qcb, L0_attn_kcw, L0_attn_kcb, L0_attn_vcw, L0_attn_vcb, L0_attn_ln_w, L0_attn_ln_b), axis=-1)
    x = _layernorm(x + _L0_ffn_ref(x, L0_ffn_w1_w, L0_ffn_w1_s, L0_ffn_w2_w, L0_ffn_w2_s, L0_ffn_h1_w, L0_ffn_h1_s, L0_ffn_h2_w, L0_ffn_h2_s, L0_ffn_w3_w, L0_ffn_w3_s), axis=-1)
    x = _layernorm(x + _L1_attn_ref(x, L1_attn_Wq, L1_attn_bq, L1_attn_Wk, L1_attn_bk, L1_attn_Wv, L1_attn_bv, L1_attn_Wo, L1_attn_bo, L1_attn_Wpk, L1_attn_bpk, L1_attn_Wpq, L1_attn_bpq, L1_attn_rel_emb), axis=-1)
    x = _layernorm(x + _L1_ffn_ref(x, L1_ffn_t_emb, L1_ffn_sw1, L1_ffn_sb1, L1_ffn_sw3, L1_ffn_sb3, L1_ffn_sw2, L1_ffn_sb2, L1_ffn_w1, L1_ffn_b1, L1_ffn_w2, L1_ffn_b2), axis=-1)
    x = _layernorm(x + _L2_attn_ref(x, L2_attn_time_maa_x, L2_attn_time_maa_w, L2_attn_time_maa_k, L2_attn_time_maa_v, L2_attn_time_maa_r, L2_attn_time_maa_w1, L2_attn_time_maa_w2, L2_attn_time_decay, L2_attn_time_decay_w1, L2_attn_time_decay_w2, L2_attn_time_faaaa, L2_attn_W_r, L2_attn_W_k, L2_attn_W_v, L2_attn_W_o, L2_attn_ln_g, L2_attn_ln_b), axis=-1)
    x = _layernorm(x + _L2_ffn_ref(x, L2_ffn_W, L2_ffn_b, L2_ffn_V_r, L2_ffn_C), axis=-1)
    x = _layernorm(x + _L3_attn_ref(x, L3_attn_wq, L3_attn_wk, L3_attn_wv), axis=-1)
    x = _layernorm(x + _L3_ffn_ref(x, L3_ffn_Ws1, L3_ffn_bs1, L3_ffn_Ws2, L3_ffn_bs2, L3_ffn_We1, L3_ffn_be1, L3_ffn_We2, L3_ffn_be2, L3_ffn_Wr, L3_ffn_br), axis=-1)
    return x

_drawn_inputs = setup_inputs


def setup_inputs(seed=0):
    import zlib

    import numpy as np

    out = dict(_drawn_inputs(seed))
    spreads = {'L0_attn_ba': (0.0, 0.8),
     'L0_attn_bb': (0.0, 0.784),
     'L0_attn_qcb': (0.0, 0.1),
     'L0_attn_kcb': (0.0, 0.1),
     'L0_attn_vcb': (0.0, 0.1),
     'L0_attn_ln_w': (1.0, 0.6),
     'L0_attn_ln_b': (0.0, 0.1),
     'L1_attn_bq': (0.0, 0.8),
     'L1_attn_bk': (0.0, 2.0),
     'L1_attn_bv': (0.0, 0.1),
     'L1_attn_bo': (0.0, 0.1),
     'L1_attn_bpk': (0.0, 2.0),
     'L1_attn_bpq': (0.0, 0.8),
     'L1_ffn_sb1': (0.0, 0.1),
     'L1_ffn_sb3': (0.0, 0.1),
     'L1_ffn_sb2': (0.0, 0.1),
     'L1_ffn_b1': (0.0, 0.1),
     'L1_ffn_b2': (0.0, 0.1),
     'L2_attn_ln_g': (1.0, 0.2),
     'L2_attn_ln_b': (0.0, 0.1),
     'L3_ffn_bs1': (0.0, 0.1),
     'L3_ffn_bs2': (0.0, 0.1),
     'L3_ffn_be1': (0.0, 0.1),
     'L3_ffn_be2': (0.0, 0.1),
     'L3_ffn_br': (0.0, 0.1)}
    factors = {'L0_attn_Wa': 8.0,
     'L0_attn_Wb': 6.261,
     'L0_attn_Wg': 4.711,
     'L0_ffn_w1_w': 8.0,
     'L0_ffn_w1_s': 8.0,
     'L0_ffn_w2_w': 7.402,
     'L0_ffn_w2_s': 8.0,
     'L0_ffn_h1_w': 7.482,
     'L0_ffn_h1_s': 8.0,
     'L0_ffn_h2_w': 7.42,
     'L0_ffn_h2_s': 8.0,
     'L0_ffn_w3_w': 7.253,
     'L0_ffn_w3_s': 8.0,
     'L1_attn_Wq': 8.0,
     'L1_attn_Wk': 8.0,
     'L1_attn_Wv': 5.715,
     'L1_attn_Wpk': 26.261,
     'L1_attn_Wpq': 23.705,
     'L1_attn_rel_emb': 8.0,
     'L2_attn_time_maa_x': 8.0,
     'L2_attn_time_maa_w': 64.0,
     'L2_attn_time_maa_w1': 8.0,
     'L2_attn_time_maa_w2': 8.0,
     'L2_attn_time_decay_w1': 34.941,
     'L2_attn_time_decay_w2': 34.817,
     'L2_attn_time_faaaa': 6.638,
     'L2_ffn_b': 3.738}
    for name, (base, spread) in spreads.items():
        noise = np.random.default_rng([zlib.crc32(name.encode()), seed]).standard_normal(out[name].shape)
        drawn = base * np.exp(spread * noise) if base else spread * noise
        out[name] = jnp.asarray(drawn.astype(out[name].dtype))
    for name, factor in factors.items():
        out[name] = (out[name] * factor).astype(out[name].dtype)
    return out
```

```python
from contextlib import ExitStack

import numpy as np
import concourse.bass as bass
from concourse import mybir

F32 = mybir.dt.float32
ALU = mybir.AluOpType
ACT = mybir.ActivationFunctionType
AXX = mybir.AxisListType.X

P = 128
B, T = 4, 512
N = B * T
PAD = 3
TAIL = 32
EPS = 1e-5


class Chip:

    def __init__(self, nc, ctx, dram):
        self.nc, self.ctx, self.dram = nc, ctx, dram
        self.X = self.sb("X", [P, B, PAD + T + TAIL])
        self.R = self.sb("R", [P, B, T])
        self.ones_mean = self.sb("ones_mean", [P, P])
        self.ident = self.sb("ident", [P, P])
        self.eps = self.sb("eps", [P, 1])
        self.ps = ctx.enter_context(nc.psum_tensor("ps", [P, 8, 512], F32))
        self.norms = 0

    def sb(self, name, shape, ctx=None):
        return (ctx or self.ctx).enter_context(self.nc.sbuf_tensor(name, shape, F32))

    def sem(self, name):
        return self.ctx.enter_context(self.nc.semaphore(name))

    def block(self, ctx):
        return ctx.enter_context(self.nc.Block())


def load_start(c):
    loaded = c.sem("start_loaded")
    zeroed = c.sem("start_zeroed")
    with ExitStack() as ctx:
        block = c.block(ctx)

        @block.sync
        def _(eng):
            eng.wait_ge(zeroed, 1)
            for b in range(B):
                eng.dma_start(c.X[:, b, PAD:PAD + T], c.dram["xT"][:, b, :]).then_inc(loaded, 16)
            eng.dma_start(c.ident[:, :], c.dram["identity"]).then_inc(loaded, 16)
            eng.wait_ge(loaded, 16 * (B + 1))

        @block.vector
        def _(eng):
            eng.memset(c.X[:, :, PAD + T:], 0.0)
            eng.memset(c.X[:, :, 0:PAD], 0.0).then_inc(zeroed, 1)
            eng.memset(c.ones_mean[:, :], 1.0 / P)
            eng.memset(c.eps[:, :], EPS)


def layernorm(c):
    base = B * c.norms
    c.norms += 1
    mean, centred, squared, var, log, rstd = (c.ln[n] for n in (
        "ln_mean", "ln_centred", "ln_squared", "ln_var", "ln_log", "ln_rstd"))
    with ExitStack() as ctx:
        D = c.sb(f"ln_D{base}", [P, B, T], ctx)
        Q = c.sb(f"ln_Q{base}", [P, B, T], ctx)
        block = c.block(ctx)

        @block.tensor
        def _(eng):
            for b in range(B):
                eng.matmul(c.ps[:, b, :], c.ones_mean[:, :], c.R[:, b, :], start=True, stop=True).then_inc(mean, 1)
            for b in range(B):
                eng.wait_ge(squared, base + b + 1)
                eng.matmul(c.ps[:, 4 + b, :], c.ones_mean[:, :], Q[:, b, :], start=True, stop=True).then_inc(var, 1)

        @block.vector
        def _(eng):
            for b in range(B):
                eng.wait_ge(mean, base + b + 1)
                eng.tensor_tensor(D[:, b, :], c.R[:, b, :], c.ps[:, b, :], ALU.subtract).then_inc(centred, 1)
            for b in range(B):
                eng.wait_ge(rstd, base + b + 1)
                eng.wait_ge(centred, base + b + 1)
                eng.tensor_tensor(c.X[:, b, PAD:PAD + T], D[:, b, :], Q[:, b, :], ALU.mult)

        @block.scalar
        def _(eng):
            for b in range(B):
                eng.wait_ge(centred, base + b + 1)
                eng.activation(Q[:, b, :], D[:, b, :], ACT.Square).then_inc(squared, 1)
            for b in range(B):
                eng.wait_ge(var, base + b + 1)
                eng.activation(Q[:, b, :], c.ps[:, 4 + b, :], ACT.Ln, bias=c.eps[:, 0:1]).then_inc(log, 1)
            for b in range(B):
                eng.wait_ge(log, base + b + 1)
                eng.activation(Q[:, b, :], Q[:, b, :], ACT.Exp, scale=-0.5).then_inc(rstd, 1)


def store_end(c):
    stored = c.sem("stored")
    with ExitStack() as ctx:
        block = c.block(ctx)

        @block.sync
        def _(eng):
            for b in range(B):
                eng.dma_start(c.dram["outT"][:, b, :], c.X[:, b, PAD:PAD + T]).then_inc(stored, 16)
            eng.wait_ge(stored, 16 * B)


def load_all(eng, sem, pairs):
    for dst, src in pairs:
        eng.dma_start(dst, src).then_inc(sem, 16)
    return 16 * len(pairs)


def ternary_ffn(c):
    d = c.dram
    H = 512
    HT = H // P
    loaded, tiles = c.sem("tf_loaded"), c.sem("tf_tiles")
    act_done, dve_done = c.sem("tf_act_done"), c.sem("tf_dve_done")
    TILES, ACTS, DVES = 2 * HT + 2 * HT + 1, 3 * HT, HT + 1
    with ExitStack() as ctx:
        w1 = c.sb("tf_w1", [P, H], ctx)
        w2 = c.sb("tf_w2", [P, H], ctx)
        h1 = c.sb("tf_h1", [P, HT, H], ctx)
        h2 = c.sb("tf_h2", [P, HT, H], ctx)
        w3 = c.sb("tf_w3", [P, HT, P], ctx)
        s = c.sb("tf_s", [P, 4 * HT + 1], ctx)
        G = c.sb("tf_G", [P, HT, T], ctx)
        H1 = c.sb("tf_H1", [P, HT, T], ctx)
        H2 = c.sb("tf_H2", [P, HT, T], ctx)
        H3 = c.sb("tf_H3", [P, HT, T], ctx)
        pairs = [(w1[:, :], d["tf_w1"]), (w2[:, :], d["tf_w2"]), (s[:, :], d["tf_s"]), (h1[:, :, :], d["tf_h1"]),
                 (h2[:, :, :], d["tf_h2"]), (w3[:, :, :], d["tf_w3"])]
        block = c.block(ctx)

        @block.sync
        def _(eng):
            load_all(eng, loaded, pairs)

        @block.tensor
        def _(eng):
            eng.wait_ge(loaded, 16 * len(pairs))
            with eng.Fori(0, B) as b:
                x = c.X[:, b, PAD:PAD + T]
                eng.wait_ge(dve_done, b * DVES + 1)
                for m in range(HT):
                    cols = slice(m * P, (m + 1) * P)
                    eng.matmul(c.ps[:, 2 * m, :], w1[:, cols], x, start=True, stop=True).then_inc(tiles, 1)
                    eng.matmul(c.ps[:, 2 * m + 1, :], w2[:, cols], x, start=True, stop=True).then_inc(tiles, 1)
                eng.wait_ge(dve_done, b * DVES + HT + 1)
                for layer, (w, hid) in enumerate(((h1, H1), (h2, H2))):
                    if layer:
                        eng.wait_ge(act_done, b * ACTS + 2 * HT)
                    for m in range(HT):
                        for k in range(HT):
                            mm = eng.matmul(c.ps[:, 4 * layer + m, :], w[:, k, m * P:(m + 1) * P], hid[:, k, :],
                                            start=k == 0, stop=k == HT - 1)
                        mm.then_inc(tiles, 1)
                eng.wait_ge(act_done, b * ACTS + 3 * HT)
                for k in range(HT):
                    mm = eng.matmul(c.ps[:, 0, :], w3[:, k, :], H3[:, k, :], start=k == 0, stop=k == HT - 1)
                mm.then_inc(tiles, 1)

        @block.scalar
        def _(eng):
            eng.wait_ge(loaded, 16 * len(pairs))
            with eng.Fori(0, B) as b:
                for m in range(HT):
                    eng.wait_ge(tiles, b * TILES + 2 * m + 1)
                    eng.activation(G[:, m, :], c.ps[:, 2 * m, :], ACT.Silu, scale=s[:, m:m + 1]).then_inc(act_done, 1)
                for layer, out in enumerate((H2, H3)):
                    for m in range(HT):
                        eng.wait_ge(tiles, b * TILES + 2 * HT + layer * HT + m + 1)
                        k = (2 + layer) * HT + m
                        eng.activation(out[:, m, :], c.ps[:, 4 * layer + m, :], ACT.Gelu, scale=s[:, k:k + 1])\
                           .then_inc(act_done, 1)

        @block.vector
        def _(eng):
            eng.sem_inc(dve_done, 1)
            eng.wait_ge(loaded, 16 * len(pairs))
            with eng.Fori(0, B) as b:
                for m in range(HT):
                    eng.wait_ge(tiles, b * TILES + 2 * m + 2)
                    eng.wait_ge(act_done, b * ACTS + m + 1)
                    eng.scalar_tensor_tensor(H1[:, m, :], c.ps[:, 2 * m + 1, :], s[:, HT + m:HT + m + 1], G[:, m, :],
                                             ALU.mult, ALU.mult).then_inc(dve_done, 1)
                eng.wait_ge(tiles, b * TILES + TILES)
                eng.scalar_tensor_tensor(c.R[:, b, :], c.ps[:, 0, :], s[:, 4 * HT:4 * HT + 1], c.X[:, b, PAD:PAD + T],
                                         ALU.mult, ALU.add).then_inc(dve_done, 1)


def hashed_ffn(c):
    d = c.dram
    E, HS = 8, 2
    first = [(r * 11) % E for r in range(E)]
    second = [(r * 11 + 7919) % E for r in range(E)]
    C = T // E
    loaded, tiles, outs = c.sem("hf_loaded"), c.sem("hf_tiles"), c.sem("hf_outs")
    silus, gelus, gated = c.sem("hf_silus"), c.sem("hf_gelus"), c.sem("hf_gated")
    prepared, scaled, chain = c.sem("hf_prepared"), c.sem("hf_scaled"), c.sem("hf_chain")
    with ExitStack() as ctx:
        sw1 = c.sb("hf_sw1", [P, HS * P], ctx)
        sw3 = c.sb("hf_sw3", [P, HS * P], ctx)
        sw2 = c.sb("hf_sw2", [P, HS, P], ctx)
        sw2x2 = c.sb("hf_sw2x2", [P, HS, P], ctx)
        w1 = c.sb("hf_w1", [P, E, P], ctx)
        w2 = c.sb("hf_w2", [P, E, P], ctx)
        bias = c.sb("hf_bias", [P, 2 * HS + 1 + 2 * E], ctx)
        b_out = c.sb("hf_b_out", [P, 3 * E], ctx)
        G = c.sb("hf_G", [P, B, HS, T], ctx)
        SH = c.sb("hf_SH", [P, HS, B, T], ctx)
        EH = c.sb("hf_EH", [P, E, 2, B * C], ctx)
        O = c.sb("hf_O", [P, E, B * C], ctx)
        pairs = [(sw1[:, :], d["hf_sw1"]), (sw3[:, :], d["hf_sw3"]), (sw2[:, :, :], d["hf_sw2"]), (w1[:, :, :], d["hf_w1"]),
                 (w2[:, :, :], d["hf_w2"]), (bias[:, :], d["hf_bias"])]
        SB2, B1, B2 = 2 * HS, 2 * HS + 1, 2 * HS + 1 + E
        block = c.block(ctx)

        def residue(buf, r, pad):
            return buf[:, :, pad + r:pad + r + (C - 1) * E + 1:E]

        @block.sync
        def _(eng):
            load_all(eng, loaded, pairs)

        @block.tensor
        def _(eng):
            eng.wait_ge(loaded, 16 * len(pairs))
            for b in range(B):
                if b >= 2:
                    eng.wait_ge(gated, HS * (b - 1))
                for m in range(HS):
                    for k, w in enumerate((sw1, sw3)):
                        eng.matmul(c.ps[:, 4 * (b % 2) + 2 * m + k, :], w[:, m * P:(m + 1) * P], c.X[:, b, PAD:PAD + T],
                                   start=True, stop=True).then_inc(tiles, 1)
            eng.wait_ge(gated, HS * B)
            for r in range(E):
                for j, e in enumerate((first[r], second[r])):
                    n = 2 * r + j
                    if n >= 8:
                        eng.wait_ge(gelus, n - 7)
                    eng.matmul(c.ps[:, n % 8, 0:B * C], w1[:, e, :], residue(c.X, r, PAD), start=True, stop=True)\
                       .then_inc(tiles, 1)
            eng.wait_ge(prepared, 1)
            eng.wait_ge(gelus, 2 * E)
            for r in range(E):
                eng.matmul(c.ps[:, r, 0:B * C], w2[:, first[r], :], EH[:, r, 0, :], start=True, stop=False)
                eng.matmul(c.ps[:, r, 0:B * C], w2[:, second[r], :], EH[:, r, 1, :], start=False, stop=False)
                for k in range(HS):
                    mm = eng.matmul(c.ps[:, r, 0:B * C], sw2x2[:, k, :], residue(SH[:, k, :, :], r, 0),
                                    start=False, stop=k == HS - 1)
                mm.then_inc(outs, 1)

        @block.scalar
        def _(eng):
            eng.wait_ge(loaded, 16 * len(pairs))
            for b in range(B):
                for m in range(HS):
                    eng.wait_ge(tiles, 4 * b + 2 * m + 1)
                    eng.activation(G[:, b, m, :], c.ps[:, 4 * (b % 2) + 2 * m, :], ACT.Silu,
                                   bias=bias[:, m:m + 1]).then_inc(silus, 1)
            for r in range(E):
                for j, e in enumerate((first[r], second[r])):
                    n = 2 * r + j
                    eng.wait_ge(tiles, 4 * B + n + 1)
                    eng.activation(EH[:, r, j, :], c.ps[:, n % 8, 0:B * C], ACT.Gelu,
                                   bias=bias[:, B1 + e:B1 + e + 1]).then_inc(gelus, 1)
            eng.wait_ge(prepared, 1)
            for r in range(E):
                eng.wait_ge(outs, r + 1)
                eng.activation(O[:, r, :], c.ps[:, r, 0:B * C], ACT.Identity, scale=0.25,
                               bias=b_out[:, 2 * E + r:2 * E + r + 1]).then_inc(scaled, 1)

        @block.vector
        def _(eng):
            eng.wait_ge(loaded, 16 * len(pairs))
            for b in range(B):
                for m in range(HS):
                    eng.wait_ge(tiles, 4 * b + 2 * m + 2)
                    eng.wait_ge(silus, HS * b + m + 1)
                    eng.scalar_tensor_tensor(SH[:, m, b, :], c.ps[:, 4 * (b % 2) + 2 * m + 1, :],
                                             bias[:, HS + m:HS + m + 1], G[:, b, m, :], ALU.add, ALU.mult)\
                       .then_inc(gated, 1)
            for r in range(E):
                eng.tensor_tensor(b_out[:, r:r + 1], bias[:, B2 + first[r]:B2 + first[r] + 1],
                                  bias[:, B2 + second[r]:B2 + second[r] + 1], ALU.add).then_inc(chain, 1)
            eng.tensor_scalar(b_out[:, E:2 * E], bias[:, SB2:SB2 + 1].to_broadcast([P, E]), 0.5, None, ALU.mult).then_inc(chain, 1)
            eng.wait_ge(chain, E + 1)
            eng.scalar_tensor_tensor(b_out[:, 2 * E:3 * E], b_out[:, 0:E], 0.25, b_out[:, E:2 * E],
                                     ALU.mult, ALU.add).then_inc(chain, 1)
            eng.wait_ge(chain, E + 2)
            eng.tensor_scalar(sw2x2[:, :, :], sw2[:, :, :], 2.0, None, ALU.mult).then_inc(prepared, 1)
            for r in range(E):
                eng.wait_ge(scaled, r + 1)
                eng.tensor_tensor(residue(c.R, r, 0), O[:, r, :].rearrange("p (b t) -> p b t", b=B),
                                  residue(c.X, r, PAD), ALU.add)


def lowrank_ffn(c):
    d = c.dram
    RANK = 32
    loaded, merged, weight, tiles = c.sem("lf_loaded"), c.sem("lf_merged"), c.sem("lf_weight"), c.sem("lf_tiles")
    with ExitStack() as ctx:
        W = c.sb("lf_W", [P, P], ctx)
        V = c.sb("lf_V", [RANK, P], ctx)
        C = c.sb("lf_C", [RANK, P], ctx)
        bias = c.sb("lf_b", [P, 1], ctx)
        M = c.sb("lf_M", [P, P], ctx)
        pairs = [(W[:, :], d["lf_W"]), (V[:, :], d["lf_V"]), (C[:, :], d["lf_C"]), (bias[:, :], d["lf_b"])]
        block = c.block(ctx)

        @block.sync
        def _(eng):
            load_all(eng, loaded, pairs)

        @block.tensor
        def _(eng):
            eng.wait_ge(loaded, 16 * len(pairs))
            eng.matmul(c.ps[:, 0, 0:P], V[:, :], C[:, :], start=True, stop=True).then_inc(merged, 1)
            eng.wait_ge(weight, 1)
            for b in range(B):
                eng.matmul(c.ps[:, 1 + b, :], M[:, :], c.X[:, b, PAD:PAD + T], start=True, stop=True).then_inc(tiles, 1)

        @block.vector
        def _(eng):
            eng.wait_ge(loaded, 16 * len(pairs))
            eng.wait_ge(merged, 1)
            eng.tensor_tensor(M[:, :], W[:, :], c.ps[:, 0, 0:P], ALU.add).then_inc(weight, 1)
            for b in range(B):
                eng.wait_ge(tiles, b + 1)
                eng.scalar_tensor_tensor(c.R[:, b, :], c.ps[:, 1 + b, :], bias[:, 0:1], c.X[:, b, PAD:PAD + T],
                                         ALU.add, ALU.add)


def routed_ffn(c):
    d = c.dram
    E, HR, HS = 12, 3, 2
    NT = N // P
    TAU = 1.5
    loaded, logits_done, chain = c.sem("rf_loaded"), c.sem("rf_logits"), c.sem("rf_chain")
    gap, sigmoids = c.sem("rf_gap"), c.sem("rf_sigmoids")
    weights_t, weights_c = c.sem("rf_weights_transposed"), c.sem("rf_weights_copied")
    wide, tiles, outs = c.sem("rf_wide"), c.sem("rf_tiles"), c.sem("rf_outs")
    wide_copied, gelus, weighted, acts, stored = (c.sem("rf_" + n) for n in (
        "wide_copied", "gelus", "weighted", "acts", "residual"))
    with ExitStack() as ctx:
        We1 = c.sb("rf_We1", [P, E, 2 * HR, P], ctx)
        We2 = c.sb("rf_We2", [P, E, HR, P], ctx)
        Ws1 = c.sb("rf_Ws1", [P, 2 * HS, P], ctx)
        Ws2 = c.sb("rf_Ws2", [P, HS, P], ctx)
        Wr = c.sb("rf_Wr", [P, E], ctx)
        br = c.sb("rf_br", [P, E], ctx)
        be2 = c.sb("rf_be2", [P, P], ctx)
        bias = c.sb("rf_bias", [P, E * 2 * HR + 2 * HS + 1], ctx)
        pick = c.sb("rf_pick", [P, E, P], ctx)
        order = c.sb("rf_order", [P, E], ctx)
        logits = c.sb("rf_logits", [P, NT, E], ctx)
        rest = c.sb("rf_rest", [P, NT, E], ctx)
        key = c.sb("rf_key", [P, NT, E], ctx)
        hot = c.sb("rf_hot", [P, 2, NT, E], ctx)
        top = c.sb("rf_top", [P, 2, NT], ctx)
        kmax = c.sb("rf_kmax", [P, 2, NT], ctx)
        part = c.sb("rf_part", [P, 3, NT], ctx)
        weights = c.sb("rf_weights", [P, NT, E], ctx)
        WT = c.sb("rf_WT", [P, B, T], ctx)
        WB = c.sb("rf_WB", [P, 2, T], ctx)
        G = c.sb("rf_G", [P, 2, HR, T], ctx)
        A = c.sb("rf_A", [P, 2, HR, T], ctx)
        pairs = [(Wr[:, :], d["rf_Wr"]), (br[:, :], d["rf_br"]), (order[:, :], d["rf_order"]), (pick[:, :, :], d["rf_pick"]),
                 (be2[:, :], d["rf_be2"]), (bias[:, :], d["rf_bias"]), (Ws1[:, :, :], d["rf_Ws1"]), (Ws2[:, :, :], d["rf_Ws2"]),
                 (We1[:, :, :, :], d["rf_We1"]), (We2[:, :, :, :], d["rf_We2"])]
        BS2 = E * 2 * HR + 2 * HS
        with ExitStack() as inner:
            block = c.block(inner)

            @block.sync
            def _(eng):
                load_all(eng, loaded, pairs)

            @block.tensor
            def _(eng):
                eng.wait_ge(loaded, 16 * len(pairs))
                for t in range(NT):
                    b, q = t // (T // P), t % (T // P)
                    mm = eng.matmul(c.ps[:, 0, t * E:(t + 1) * E], c.X[:, b, PAD + q * P:PAD + (q + 1) * P], Wr[:, :],
                                    start=True, stop=True)
                mm.then_inc(logits_done, 1)
                eng.wait_ge(chain, 14)
                for t in range(NT):
                    mm = eng.transpose(c.ps[0:E, 1 + t // 4, (t % 4) * P:(t % 4 + 1) * P], weights[:, t, :], c.ident[:, :])
                    if t % 4 == 3:
                        mm.then_inc(weights_t, 1)

            @block.vector
            def _(eng):
                steps = [0]

                def step(ins):
                    steps[0] += 1
                    ins.then_inc(chain, 1)
                    eng.wait_ge(chain, steps[0])

                def wide_of(x):
                    return x.unsqueeze(2).to_broadcast([P, NT, E])

                def per_expert(x):
                    return x.unsqueeze(1).to_broadcast([P, NT, E])

                eng.wait_ge(loaded, 16 * len(pairs))
                eng.wait_ge(logits_done, 1)
                step(eng.tensor_tensor(logits[:, :, :], c.ps[:, 0, 0:NT * E].rearrange("p (t e) -> p t e", e=E),
                                       per_expert(br[:, :]), ALU.add))
                values = logits
                for k in range(2):
                    step(eng.tensor_reduce(top[:, k, :], values[:, :, :], AXX, ALU.max))
                    step(eng.tensor_tensor(key[:, :, :], values[:, :, :], wide_of(top[:, k, :]), ALU.is_equal))
                    step(eng.tensor_tensor(key[:, :, :], key[:, :, :], per_expert(order[:, :]), ALU.mult))
                    step(eng.tensor_reduce(kmax[:, k, :], key[:, :, :], AXX, ALU.max))
                    step(eng.tensor_tensor(hot[:, k, :, :], key[:, :, :], wide_of(kmax[:, k, :]), ALU.is_equal))
                    if k == 0:
                        step(eng.scalar_tensor_tensor(rest[:, :, :], hot[:, 0, :, :], -3e38, logits[:, :, :], ALU.mult, ALU.add))
                        values = rest
                eng.tensor_tensor(part[:, 0, :], top[:, 1, :], top[:, 0, :], ALU.subtract).then_inc(gap, 1)
                eng.wait_ge(sigmoids, 2)
                step(eng.tensor_tensor(rest[:, :, :], hot[:, 0, :, :], wide_of(part[:, 1, :]), ALU.mult))
                eng.tensor_tensor(key[:, :, :], hot[:, 1, :, :], wide_of(part[:, 2, :]), ALU.mult).then_inc(gap, 1)
                eng.wait_ge(gap, 2)
                step(eng.tensor_tensor(weights[:, :, :], rest[:, :, :], key[:, :, :], ALU.add))
                step(eng.memset(WT[:, :, :], 0.0))
                for b in range(B):
                    eng.wait_ge(weights_t, b + 1)
                    eng.tensor_copy(WT[0:E, b, :], c.ps[0:E, 1 + b, :]).then_inc(weights_c, 1)

            @block.scalar
            def _(eng):
                eng.wait_ge(gap, 1)
                eng.activation(part[:, 1, :], part[:, 0, :], ACT.Sigmoid, scale=-1.0 / TAU).then_inc(sigmoids, 1)
                eng.activation(part[:, 2, :], part[:, 0, :], ACT.Sigmoid, scale=1.0 / TAU).then_inc(sigmoids, 1)

        experts = [(HR, E > 0)] * E + [(HS, False)]
        before = [sum(h for h, _ in experts[:e]) for e in range(E + 2)]
        HB = before[E + 1]
        block = c.block(ctx)

        def w_in(e):
            return (We1[:, e, :, :], We2[:, e, :, :], e * 2 * HR) if e < E else (Ws1[:, :, :], Ws2[:, :, :], E * 2 * HR)

        @block.tensor
        def _(eng):
            with eng.Fori(0, B) as b:
                x = c.X[:, b, PAD:PAD + T]

                def second(e):
                    h, w2 = experts[e][0], w_in(e)[1]
                    for m in range(h):
                        eng.wait_ge(acts, b * HB + before[e] + m + 2)
                        mm = eng.matmul(c.ps[:, 7, :], w2[:, m, :], A[:, e % 2, m, :], start=False,
                                        stop=e == E and m == h - 1)
                    mm.then_inc(outs, 1)

                eng.wait_ge(stored, b + 1)
                eng.matmul(c.ps[:, 7, :], be2[:, :], WT[:, b, :], start=True, stop=False)
                for e in range(E + 1):
                    h, _ = experts[e]
                    w1 = w_in(e)[0]
                    if e < E:
                        eng.wait_ge(wide_copied, b * E + e + 1)
                        eng.matmul(c.ps[:, 6, :], pick[:, e, :], WT[:, b, :], start=True, stop=True).then_inc(wide, 1)
                    for m in range(h):
                        seen = before[e - 1] + min(m + 1, experts[e - 1][0]) if e else 0
                        eng.wait_ge(gelus, b * HB + seen + 1)
                        eng.matmul(c.ps[:, m, :], w1[:, h + m, :], x, start=True, stop=True).then_inc(tiles, 1)
                        eng.wait_ge(acts, b * HB + seen + 1)
                        eng.matmul(c.ps[:, 3 + m, :], w1[:, m, :], x, start=True, stop=True).then_inc(tiles, 1)
                    if e:
                        second(e - 1)
                second(E)

        @block.scalar
        def _(eng):
            eng.sem_inc(wide_copied, 1)
            eng.sem_inc(gelus, 1)
            with eng.Fori(0, B) as b:
                for e in range(E + 1):
                    h, _ = experts[e]
                    at = w_in(e)[2]
                    if e < E:
                        eng.wait_ge(wide, b * E + e + 1)
                        if e >= 2:
                            eng.wait_ge(weighted, b * E * HR + (e - 1) * HR)
                        eng.activation(WB[:, e % 2, :], c.ps[:, 6, :], ACT.Copy).then_inc(wide_copied, 1)
                    for m in range(h):
                        eng.wait_ge(tiles, 2 * (b * HB + before[e] + m) + 1)
                        if e >= 2:
                            eng.wait_ge(acts, b * HB + before[e - 2] + m + 2)
                        eng.activation(G[:, e % 2, m, :], c.ps[:, m, :], ACT.Gelu, bias=bias[:, at + h + m:at + h + m + 1])\
                           .then_inc(gelus, 1)

        @block.gpsimd
        def _(eng):
            with eng.Fori(0, B) as b:
                for e in range(E):
                    eng.wait_ge(wide_copied, b * E + e + 2)
                    for m in range(HR):
                        eng.wait_ge(gelus, b * HB + before[e] + m + 2)
                        eng.tensor_tensor(G[:, e % 2, m, :], G[:, e % 2, m, :], WB[:, e % 2, :], ALU.mult).then_inc(weighted, 1)

        @block.vector
        def _(eng):
            eng.sem_inc(acts, 1)
            eng.sem_inc(stored, 1)
            with eng.Fori(0, B) as b:
                for e in range(E + 1):
                    h, _ = experts[e]
                    at = w_in(e)[2]
                    for m in range(h):
                        eng.wait_ge(tiles, 2 * (b * HB + before[e] + m) + 2)
                        if e < E:
                            eng.wait_ge(weighted, b * E * HR + e * HR + m + 1)
                        else:
                            eng.wait_ge(gelus, b * HB + before[e] + m + 2)
                        if e >= 2:
                            eng.wait_ge(outs, b * (E + 1) + e - 1)
                        eng.scalar_tensor_tensor(A[:, e % 2, m, :], c.ps[:, 3 + m, :], bias[:, at + m:at + m + 1],
                                                 G[:, e % 2, m, :], ALU.add, ALU.mult).then_inc(acts, 1)
                eng.wait_ge(outs, (b + 1) * (E + 1))
                eng.scalar_tensor_tensor(c.R[:, b, :], c.ps[:, 7, :], bias[:, BS2:BS2 + 1], c.X[:, b, PAD:PAD + T],
                                         ALU.add, ALU.add).then_inc(stored, 1)


def rwkv_attention(c):
    d = c.dram
    HS = 16
    loaded, chain = c.sem("rw_loaded"), c.sem("rw_chain")
    pe_done, act_done = c.sem("rw_pe"), c.sem("rw_act")
    vb_ready, kv_ready, scanned, read, summed = (c.sem("rw_" + n) for n in ("vb", "kv", "scanned", "read", "summed"))
    ym, yc, ys, yv, yl, yr, yn, yo = (c.sem("rw_y" + n) for n in "mcsvlrno")
    with ExitStack() as ctx:
        maa = c.sb("rw_maa", [P, 9], ctx)
        w1 = c.sb("rw_w1", [P, P], ctx)
        w2 = c.sb("rw_w2", [P, P], ctx)
        dw1 = c.sb("rw_dw1", [P, 64], ctx)
        dw2 = c.sb("rw_dw2", [64, P], ctx)
        Wrkv = c.sb("rw_Wrkv", [P, 3, P], ctx)
        Wo = c.sb("rw_Wo", [P, P], ctx)
        spread = c.sb("rw_spread", [P, HS, P], ctx)
        gather = c.sb("rw_gather", [P, HS, P], ctx)
        heads = c.sb("rw_heads", [P, P], ctx)
        xx = c.sb("rw_xx", [P, T], ctx)
        xxx = c.sb("rw_xxx", [P, T], ctx)
        m = c.sb("rw_m", [P, T], ctx)
        mix = c.sb("rw_mix", [P, 4, T], ctx)
        rkv = c.sb("rw_rkv", [P, 3, T], ctx)
        wd = c.sb("rw_wd", [P, T], ctx)
        wt = c.sb("rw_wt", [64, T], ctx)
        we = c.sb("rw_we", [P, T], ctx)
        ruk = c.sb("rw_ruk", [P, T], ctx)
        own = c.sb("rw_own", [P, T], ctx)
        kv = c.sb("rw_kv", [P, 2, T], ctx)
        S = c.sb("rw_S", [P, 2, 1 + T], ctx)
        rS = c.sb("rw_rS", [P, 2, T], ctx)
        Y = c.sb("rw_Y", [P, T], ctx)
        Q = c.sb("rw_Q", [P, 2, T], ctx)
        pairs = [(maa[:, :], d["rw_maa"]), (w1[:, :], d["rw_w1"]), (w2[:, :], d["rw_w2"]), (dw1[:, :], d["rw_dw1"]),
                 (dw2[:, :], d["rw_dw2"]), (Wrkv[:, :, :], d["rw_Wrkv"]), (Wo[:, :], d["rw_Wo"]),
                 (spread[:, :, :], d["rw_spread"]), (gather[:, :, :], d["rw_gather"]), (heads[:, :], d["rw_heads"])]
        block = c.block(ctx)
        PES, ACTS, STEPS = 10, 7, 12

        @block.sync
        def _(eng):
            load_all(eng, loaded, pairs)

        @block.tensor
        def _(eng):
            eng.wait_ge(loaded, 16 * len(pairs))
            with eng.Fori(0, B) as b:
                pe, dv, ac = b * PES, b * STEPS, b * ACTS
                eng.wait_ge(chain, dv + 2)
                eng.matmul(c.ps[:, 7, :], w1[:, :], xxx[:, :], start=True, stop=True).then_inc(pe_done, 1)
                eng.wait_ge(act_done, ac + 1)
                for f in range(4):
                    eng.matmul(c.ps[:, f, :], w2[32 * f:32 * f + 32, :], m[32 * f:32 * f + 32, :], start=True, stop=True)\
                       .then_inc(pe_done, 1)
                eng.wait_ge(chain, dv + 10)
                eng.matmul(c.ps[0:64, 7, :], dw1[:, :], mix[:, 0, :], start=True, stop=True).then_inc(pe_done, 1)
                for n in range(3):
                    mm = eng.matmul(c.ps[:, 4 + n, :], Wrkv[:, n, :], mix[:, 1 + n, :], start=True, stop=True)
                mm.then_inc(pe_done, 1)
                eng.wait_ge(act_done, ac + 2)
                eng.matmul(c.ps[:, 7, :], dw2[:, :], wt[:, :], start=True, stop=True).then_inc(pe_done, 1)
                eng.wait_ge(chain, dv + 11)
                eng.wait_ge(act_done, ac + 4)
                eng.matmul(c.ps[:, 7, :], heads[:, :], ruk[:, :], start=True, stop=True).then_inc(pe_done, 1)
                for j in range(HS + 1):
                    if j < HS:
                        if j >= 2:
                            eng.wait_ge(kv_ready, b * HS + j - 1)
                        eng.matmul(c.ps[:, j % 2, :], spread[:, j, :], rkv[:, 1, :], start=True, stop=True).then_inc(vb_ready, 1)
                    if j >= 1:
                        eng.wait_ge(read, b * HS + j)
                        eng.matmul(c.ps[:, 2, :], gather[:, j - 1, :], rS[:, (j - 1) % 2, :], start=j == 1, stop=j == HS)\
                           .then_inc(summed, 1)
                eng.wait_ge(yo, 2 * b + 1)
                eng.matmul(c.ps[:, 3, :], c.ones_mean[:, :], Y[:, :], start=True, stop=True).then_inc(ym, 1)
                eng.wait_ge(ys, b + 1)
                eng.matmul(c.ps[:, 4, :], c.ones_mean[:, :], Q[:, 0, :], start=True, stop=True).then_inc(yv, 1)
                eng.wait_ge(yn, 2 * b + 2)
                eng.matmul(c.ps[:, 5, :], Wo[:, :], Y[:, :], start=True, stop=True).then_inc(pe_done, 1)
                eng.wait_ge(yo, 2 * b + 2)

        @block.scalar
        def _(eng):
            eng.wait_ge(loaded, 16 * len(pairs))
            with eng.Fori(0, B) as b:
                pe, dv, ac = b * PES, b * STEPS, b * ACTS
                eng.wait_ge(pe_done, pe + 1)
                eng.activation(m[:, :], c.ps[:, 7, :], ACT.Tanh).then_inc(act_done, 1)
                eng.wait_ge(pe_done, pe + 6)
                eng.activation(wt[:, :], c.ps[0:64, 7, :], ACT.Tanh).then_inc(act_done, 1)
                eng.wait_ge(pe_done, pe + 7)
                for n in range(3):
                    mm = eng.activation(rkv[:, n, :], c.ps[:, 4 + n, :], ACT.Copy)
                mm.then_inc(act_done, 1)
                eng.wait_ge(pe_done, pe + 8)
                eng.activation(we[:, :], c.ps[:, 7, :], ACT.Exp, bias=maa[:, 5:6]).then_inc(act_done, 1)
                eng.wait_ge(act_done, ac + 4)
                eng.activation(wd[:, :], we[:, :], ACT.Exp, scale=-1.0).then_inc(act_done, 1)
                eng.wait_ge(yc, b + 1)
                eng.activation(Q[:, 0, :], xx[:, :], ACT.Square).then_inc(ys, 1)
                eng.wait_ge(yv, b + 1)
                eng.activation(Q[:, 1, :], c.ps[:, 4, :], ACT.Ln, bias=c.eps[:, 0:1]).then_inc(act_done, 1)
                eng.wait_ge(act_done, ac + 6)
                eng.activation(Q[:, 1, :], Q[:, 1, :], ACT.Exp, scale=-0.5).then_inc(act_done, 1)

        @block.gpsimd
        def _(eng):
            with eng.Fori(0, B) as b:
                for j in range(HS):
                    eng.wait_ge(scanned, b * HS + j + 1)
                    if j >= 2:
                        eng.wait_ge(summed, b * HS + j - 1)
                    eng.tensor_tensor(rS[:, j % 2, :], rkv[:, 2, :], S[:, j % 2, 0:T], ALU.mult).then_inc(read, 1)

        @block.vector
        def _(eng):
            for n in range(2):
                eng.memset(S[:, n, 0:1], 0.0)
            eng.wait_ge(loaded, 16 * len(pairs))
            with eng.Fori(0, B) as b:
                pe, dv, ac = b * PES, b * STEPS, b * ACTS
                steps = [0]

                def step(ins):
                    steps[0] += 1
                    ins.then_inc(chain, 1)

                def after():
                    eng.wait_ge(chain, dv + steps[0])

                x = c.X[:, b, PAD:PAD + T]
                step(eng.tensor_tensor(xx[:, :], c.X[:, b, PAD - 1:PAD + T - 1], x, ALU.subtract))
                after()
                step(eng.scalar_tensor_tensor(xxx[:, :], xx[:, :], maa[:, 0:1], x, ALU.mult, ALU.add))
                for f in range(4):
                    eng.wait_ge(pe_done, pe + 2 + f)
                    step(eng.scalar_tensor_tensor(mix[:, f, :], c.ps[:, f, :], maa[:, 1 + f:2 + f], xx[:, :], ALU.add, ALU.mult))
                after()
                for f in range(4):
                    step(eng.tensor_tensor(mix[:, f, :], mix[:, f, :], x, ALU.add))
                eng.wait_ge(act_done, ac + 3)
                step(eng.scalar_tensor_tensor(ruk[:, :], rkv[:, 2, :], maa[:, 6:7], rkv[:, 0, :], ALU.mult, ALU.mult))
                eng.wait_ge(act_done, ac + 5)
                eng.wait_ge(pe_done, pe + 9)
                step(eng.tensor_tensor(we[:, :], rkv[:, 1, :], c.ps[:, 7, :], ALU.mult))
                for j in range(HS + 1):
                    if j < HS:
                        eng.wait_ge(vb_ready, b * HS + j + 1)
                        if j >= 2:
                            eng.wait_ge(scanned, b * HS + j - 1)
                        eng.tensor_tensor(kv[:, j % 2, :], rkv[:, 0, :], c.ps[:, j % 2, :], ALU.mult).then_inc(kv_ready, 1)
                    if j >= 1:
                        eng.wait_ge(kv_ready, b * HS + j)
                        if j >= 3:
                            eng.wait_ge(read, b * HS + j - 2)
                        eng.tensor_tensor_scan(S[:, (j - 1) % 2, 1:], wd[:, :], kv[:, (j - 1) % 2, :], 0.0,
                                               ALU.mult, ALU.add).then_inc(scanned, 1)
                eng.wait_ge(summed, (b + 1) * HS)
                after()
                eng.tensor_tensor(Y[:, :], we[:, :], c.ps[:, 2, :], ALU.add).then_inc(yo, 1)
                eng.wait_ge(ym, b + 1)
                eng.wait_ge(yo, 2 * b + 1)
                eng.tensor_tensor(xx[:, :], Y[:, :], c.ps[:, 3, :], ALU.subtract).then_inc(yc, 1)
                eng.wait_ge(act_done, ac + 7)
                eng.wait_ge(yc, b + 1)
                eng.scalar_tensor_tensor(own[:, :], xx[:, :], maa[:, 7:8], Q[:, 1, :], ALU.mult, ALU.mult).then_inc(yn, 1)
                eng.wait_ge(yn, 2 * b + 1)
                eng.tensor_scalar(Y[:, :], own[:, :], maa[:, 8:9], None, ALU.add).then_inc(yn, 1)
                eng.wait_ge(pe_done, pe + 10)
                eng.tensor_tensor(c.R[:, b, :], x, c.ps[:, 5, :], ALU.add).then_inc(yo, 1)
                assert steps[0] == STEPS


HEADS = 16
DH = P // HEADS
QUAD = 4
GROUPS = HEADS // QUAD
QT = T // P
UNITS = QT * QUAD


def rotary_attention(c):
    d = c.dram
    NW = 5
    names = ("loaded", "weights", "projected", "roped", "kept", "values_t", "scores", "maxima", "exps",
             "probs_t", "probs_c", "mixed", "inverted", "normed", "placed", "out_t")
    s = {n: c.sem("ra_" + n) for n in names}
    with ExitStack() as ctx:
        W = c.sb("ra_W", [P, NW, P], ctx)
        rope = c.sb("ra_rope", [P, 4, T], ctx)
        QK = c.sb("ra_QK", [P, 2, 2, T], ctx)
        tmp = c.sb("ra_tmp", [P, 4, T], ctx)
        VC = c.sb("ra_VC", [P, T], ctx)
        V = c.sb("ra_V", [P, 2, QT, P], ctx)
        bias = c.sb("ra_bias", [P, UNITS], ctx)
        E = c.sb("ra_E", [P, 2, T], ctx)
        PT = c.sb("ra_PT", [P, 2, T], ctx)
        total = c.sb("ra_total", [P, UNITS], ctx)
        inverse = c.sb("ra_inverse", [P, UNITS], ctx)
        O = c.sb("ra_O", [P, B, QT, P], ctx)
        OG = c.sb("ra_OG", [P, B, QT, QUAD * DH], ctx)
        block = c.block(ctx)
        NB = GROUPS * B

        @block.sync
        def _(eng):
            eng.dma_start(rope[:, :, :], d["ra_rope"]).then_inc(s["loaded"], 16)
            eng.dma_start(W[:, :, :], d["ra_W"][:, 0, :, :]).then_inc(s["weights"], 16)
            with eng.Fori(1, GROUPS) as g:
                eng.wait_ge(s["projected"], g * B * NW)
                eng.dma_start(W[:, :, :], d["ra_W"][:, g, :, :]).then_inc(s["weights"], 16)

        @block.tensor
        def _(eng):
            with eng.Fori(0, GROUPS) as g:
                eng.wait_ge(s["weights"], 16 * g + 16)
                for b in range(B):
                    n = g * B + b
                    x = c.X[:, b, PAD:PAD + T]
                    for w in range(NW):
                        eng.matmul(c.ps[:, (5 + w) % 8, :], W[:, w, :], x, start=True, stop=True).then_inc(s["projected"], 1)
                    eng.wait_ge(s["kept"], n + 1)
                    for t in range(QT):
                        mm = eng.transpose(c.ps[:, 2, t * P:(t + 1) * P], VC[:, t * P:(t + 1) * P], c.ident[:, :])
                    mm.then_inc(s["values_t"], 1)
                    eng.wait_ge(s["roped"], 6 * n + 6)

                    def scores(u):
                        t, h = u // QUAD, u % QUAD
                        rows = slice(32 * h, 32 * h + 32)
                        if u >= 2:
                            eng.wait_ge(s["exps"], n * UNITS + u - 1)
                        eng.matmul(c.ps[:, u % 2, :], QK[rows, b % 2, 0, t * P:(t + 1) * P], QK[rows, b % 2, 1, :],
                                   start=True, stop=True).then_inc(s["scores"], 1)

                    def transposes(u):
                        eng.wait_ge(s["exps"], n * UNITS + u + 1)
                        if u >= 2:
                            eng.wait_ge(s["probs_c"], n * UNITS + u - 1)
                        for k in range(QT):
                            mm = eng.transpose(c.ps[:, 2 + u % 2, k * P:(k + 1) * P], E[:, u % 2, k * P:(k + 1) * P], c.ident[:, :])
                        mm.then_inc(s["probs_t"], 1)

                    def mixes(u):
                        h = u % QUAD
                        if u == 0:
                            eng.wait_ge(s["normed"], n + 1)
                        eng.wait_ge(s["probs_c"], n * UNITS + u + 1)
                        for k in range(QT):
                            mm = eng.matmul(c.ps[:, 4, u * DH:(u + 1) * DH], PT[:, u % 2, k * P:(k + 1) * P],
                                            V[:, b % 2, k, 32 * h:32 * h + DH], start=k == 0, stop=k == QT - 1)
                        mm.then_inc(s["mixed"], 1)

                    scores(0)
                    for u in range(UNITS):
                        if u + 1 < UNITS:
                            scores(u + 1)
                        transposes(u)
                        if u:
                            mixes(u - 1)
                    mixes(UNITS - 1)
            eng.wait_ge(s["placed"], GROUPS)
            for b in range(B):
                for t in range(QT):
                    mm = eng.transpose(c.ps[:, b, t * P:(t + 1) * P], O[:, b, t, :], c.ident[:, :])
                mm.then_inc(s["out_t"], 1)

        @block.scalar
        def _(eng):
            with eng.Fori(0, GROUPS) as g:
                for b in range(B):
                    n = g * B + b
                    eng.wait_ge(s["projected"], NW * n + 5)
                    eng.activation(VC[:, :], c.ps[:, 1, :], ACT.Copy).then_inc(s["kept"], 1)
                    eng.wait_ge(s["values_t"], n + 1)
                    eng.activation(V[:, b % 2, :, :], c.ps[:, 2, :].rearrange("p (t c) -> p t c", t=QT), ACT.Copy).then_inc(s["roped"], 1)
                    for u in range(UNITS):
                        eng.wait_ge(s["maxima"], n * UNITS + u + 1)
                        if u >= 2:
                            eng.wait_ge(s["probs_t"], n * UNITS + u - 1)
                        eng.activation(E[:, u % 2, :], c.ps[:, u % 2, :], ACT.Exp, bias=bias[:, u:u + 1],
                                       accum_out=total[:, u:u + 1]).then_inc(s["exps"], 1)

        @block.vector
        def _(eng):
            eng.sem_inc(s["normed"], 1)
            eng.wait_ge(s["loaded"], 16)
            with eng.Fori(0, GROUPS) as g:
                for b in range(B):
                    n = g * B + b
                    for w in range(4):
                        eng.wait_ge(s["projected"], NW * n + w + 1)
                        eng.tensor_tensor(tmp[:, w, :], rope[:, w, :], c.ps[:, (5 + w) % 8, :], ALU.mult).then_inc(s["roped"], 1)
                    eng.wait_ge(s["roped"], 6 * n + 5)
                    eng.tensor_tensor(QK[:, b % 2, 0, :], tmp[:, 0, :], tmp[:, 1, :], ALU.add)
                    eng.tensor_tensor(QK[:, b % 2, 1, :], tmp[:, 2, :], tmp[:, 3, :], ALU.add).then_inc(s["roped"], 1)
                    for u in range(UNITS + 1):
                        if u < UNITS:
                            eng.wait_ge(s["scores"], n * UNITS + u + 1)
                            eng.tensor_reduce(bias[:, u:u + 1], c.ps[:, u % 2, :], AXX, ALU.max, negate=True).then_inc(s["maxima"], 1)
                        if u:
                            eng.wait_ge(s["probs_t"], n * UNITS + u)
                            if u >= 3:
                                eng.wait_ge(s["mixed"], n * UNITS + u - 2)
                            eng.tensor_copy(PT[:, (u - 1) % 2, :], c.ps[:, 2 + (u - 1) % 2, :]).then_inc(s["probs_c"], 1)
                    eng.wait_ge(s["exps"], (n + 1) * UNITS)
                    eng.reciprocal(inverse[:, :], total[:, :]).then_inc(s["inverted"], 1)
                    eng.wait_ge(s["mixed"], (n + 1) * UNITS)
                    eng.wait_ge(s["inverted"], n + 1)
                    eng.tensor_tensor(OG[:, b, :, :].rearrange("p t (h c) -> p (t h) c", h=QUAD),
                                      c.ps[:, 4, 0:UNITS * DH].rearrange("p (u c) -> p u c", c=DH),
                                      inverse[:, :].unsqueeze(2).to_broadcast([P, UNITS, DH]), ALU.mult).then_inc(s["normed"], 1)
                eng.wait_ge(s["normed"], g * B + B + 1)
                eng.tensor_copy(O[:, :, :, bass.ds(g * QUAD * DH, QUAD * DH)], OG[:, :, :, :]).then_inc(s["placed"], 1)
                eng.wait_ge(s["placed"], g + 1)
            for b in range(B):
                eng.wait_ge(s["out_t"], b + 1)
                eng.tensor_tensor(c.R[:, b, :], c.X[:, b, PAD:PAD + T], c.ps[:, b, :], ALU.add)


def relative_attention(c):
    d, nc = c.dram, c.nc
    SPAN, LOW, UP = 64, 192, 64
    BAND = LOW + UP
    ROW = SPAN + BAND
    names = ("loaded", "zeros", "padded", "weights", "tables_ps", "tables", "projected", "kept", "values_t", "qk", "ab",
             "ab_copied", "wrote", "windows", "scores", "maxima", "exps", "probs_t", "probs_c", "mixed", "inverted",
             "normed", "placed", "out_t", "out_c", "out")
    s = {n: c.sem("da_" + n) for n in names}
    scale = (DH * 3) ** -0.5
    Wq, Wk, Wv, Wpk, Wpq = range(5)
    Q_LOW, Q_UP, K_LOW, K_UP = range(4)
    scratch = [[nc.dram_tensor(f"da_scratch{i}{j}", (UNITS * P * ROW + SPAN,), F32).ap() for j in range(2)] for i in range(2)]

    def rows_of(buf, offset, row, first, count, width):
        return bass.AP(buf.tensor, buf.offset + offset + first * row, [[row, count], [P * ROW, UNITS], [1, width]])

    with ExitStack() as ctx:
        W = c.sb("da_W", [P, 5, P], ctx)
        Wo = c.sb("da_Wo", [P, P], ctx)
        rel = c.sb("da_rel", [P, 2, P], ctx)
        bias = c.sb("da_bias", [P, GROUPS, 5], ctx)
        bo = c.sb("da_bo", [P, 1], ctx)
        half = c.sb("da_half", [P, 2, P], ctx)
        zeros = c.sb("da_zeros", [P, UNITS, SPAN], ctx)
        pk = c.sb("da_pk", [P, P], ctx)
        pq = c.sb("da_pq", [P, P], ctx)
        A_table = c.sb("da_A_table", [P, BAND], ctx)
        B_table = c.sb("da_B_table", [P, BAND], ctx)
        ends = c.sb("da_ends", [P, 5], ctx)
        QK = c.sb("da_QK", [P, 2, 4, T], ctx)
        VC = c.sb("da_VC", [P, T], ctx)
        V = c.sb("da_V", [P, 2, QT, P], ctx)
        AB = c.sb("da_AB", [P, UNITS, 2, BAND], ctx)
        diag = c.sb("da_diag", [P, 2, 2, UNITS, P], ctx)
        corner = c.sb("da_corner", [P, 2, 2, UNITS, SPAN], ctx)
        top = c.sb("da_top", [P, UNITS], ctx)
        E = c.sb("da_E", [P, 2, T], ctx)
        PT = c.sb("da_PT", [P, 2, T], ctx)
        total = c.sb("da_total", [P, UNITS], ctx)
        inverse = c.sb("da_inverse", [P, UNITS], ctx)
        OG = c.sb("da_OG", [P, B, QT, QUAD * DH], ctx)
        O = c.sb("da_O", [P, B, QT, P], ctx)
        OC = AB[:, 0:B, :, :].rearrange("p b k c -> p b (k c)")
        pairs = [(Wo[:, :], d["da_Wo"]), (rel[:, :, :], d["da_rel"]), (bias[:, :, :], d["da_bias"]), (bo[:, :], d["da_bo"]),
                 (half[:, :, :], d["da_half"])]
        COPIES = UNITS + 1
        ORDER = [(1, 0), (1, 1), (2, 0), (1, 2), (2, 1), (1, 3), (2, 2), (2, 3)]
        block = c.block(ctx)

        @block.sync
        def _(eng):
            load_all(eng, s["loaded"], pairs)
            eng.dma_start(W[:, :, :], d["da_W"][:, 0, :, :]).then_inc(s["weights"], 16)
            eng.sem_inc(s["wrote"], 1)
            eng.wait_ge(s["zeros"], 1)
            for pair in scratch:
                for buf in pair:
                    eng.dma_start(rows_of(buf, 0, ROW, 0, P, SPAN), zeros[:, :, :]).then_inc(s["padded"], 16)
                    eng.dma_start(bass.AP(buf.tensor, buf.offset + UNITS * P * ROW, [[SPAN, 1], [1, SPAN]]), zeros[0:1, 0, :])\
                       .then_inc(s["padded"], 16)
            eng.wait_ge(s["padded"], 8 * 16)
            with eng.Fori(0, GROUPS) as g:
                for kind, b in ORDER:
                    if kind == 2:
                        continue
                    n = g * B + b
                    for t in range(QT):
                        eng.wait_ge(s["ab_copied"], n * COPIES + 2 + (t + 1) * QUAD)
                        for side in range(2):
                            buf = scratch[b % 2][side]
                            dst = bass.AP(buf.tensor, buf.offset + t * QUAD * P * ROW + SPAN, [[ROW, P], [P * ROW, QUAD], [1, BAND]])
                            eng.dma_start(dst, AB[:, t * QUAD:(t + 1) * QUAD, side, :]).then_inc(s["wrote"], 16)
                    eng.wait_ge(s["wrote"], (n + 1) * 16 * 2 * QT + 1)
                    A, Bk = scratch[b % 2]
                    par = b % 2
                    for dst, src in (
                            (diag[:, par, 0, :, :], rows_of(A, 2 * SPAN, ROW - 1, 0, P, P)),
                            (corner[0:64, par, 0, :, :], rows_of(A, SPAN, ROW - 1, 0, 64, SPAN)),
                            (corner[64:128, par, 0, :, :], rows_of(A, SPAN + LOW + 2 * SPAN, ROW - 1, 64, 64, SPAN)),
                            (diag[:, par, 1, :, :], rows_of(Bk, SPAN + UP + P, ROW - 1, 0, P, P)),
                            (corner[0:64, par, 1, :, :], rows_of(Bk, SPAN, ROW - 1, 0, 64, SPAN)),
                            (corner[64:128, par, 1, :, :], rows_of(Bk, SPAN + UP + 2 * P, ROW - 1, 64, 64, SPAN))):
                        eng.dma_start(dst, src).then_inc(s["windows"], 16)
                eng.wait_ge(s["projected"], (g + 1) * B)
                eng.dma_start(W[:, :, :], d["da_W"][:, g + 1, :, :]).then_inc(s["weights"], 16)
            eng.wait_ge(s["weights"], 16 * (GROUPS + 1))

        @block.tensor
        def _(eng):
            eng.wait_ge(s["loaded"], 16 * len(pairs))
            with eng.Fori(0, GROUPS) as g:
                def bands(b):
                    n = g * B + b
                    x = c.X[:, b, PAD:PAD + T]
                    eng.wait_ge(s["ab_copied"], n * COPIES + 1)
                    for w in (Wq, Wk, Wv):
                        mm = eng.matmul(c.ps[:, 5 + w, :], W[:, w, :], x, start=True, stop=True)
                    mm.then_inc(s["projected"], 1)
                    eng.wait_ge(s["kept"], n + 1)
                    eng.wait_ge(s["qk"], n + 1)
                    for t in range(QT):
                        mm = eng.transpose(c.ps[:, 5, t * P:(t + 1) * P], VC[:, t * P:(t + 1) * P], c.ident[:, :])
                    mm.then_inc(s["values_t"], 1)
                    for u in range(UNITS):
                        t, h = u // QUAD, u % QUAD
                        rows = slice(32 * h, 32 * h + 32)
                        if u >= 2:
                            eng.wait_ge(s["ab_copied"], n * COPIES + 1 + u)
                        eng.matmul(c.ps[:, 6 + u % 2, 0:BAND], QK[rows, b % 2, Q_LOW, t * P:(t + 1) * P], A_table[rows, :],
                                   start=True, stop=True)
                        eng.matmul(c.ps[:, 6 + u % 2, BAND:2 * BAND], QK[rows, b % 2, K_LOW, t * P:(t + 1) * P], B_table[rows, :],
                                   start=True, stop=True).then_inc(s["ab"], 1)

                def scores(b, u):
                    n = g * B + b
                    t, h = u // QUAD, u % QUAD
                    rows = slice(32 * h, 32 * h + 32)
                    par, ps = b % 2, c.ps[:, u % 2, :]
                    lo, hi = c.ps[0:64, u % 2, :], c.ps[64:128, u % 2, :]
                    at = slice(t * P, (t + 1) * P)
                    if u >= 2:
                        eng.wait_ge(s["exps"], n * UNITS + u - 1)
                    eng.matmul(ps[:, 0:(t + 1) * P], QK[rows, par, Q_LOW, at], QK[rows, par, K_LOW, 0:(t + 1) * P], start=True, stop=False)
                    if t < QT - 1:
                        eng.matmul(ps[:, (t + 1) * P:], QK[rows, par, Q_UP, at], QK[rows, par, K_UP, (t + 1) * P:], start=False, stop=False)
                    eng.matmul(ps[:, at], c.ident[:, :], diag[:, par, 0, u, :], start=False, stop=False)
                    if t > 0:
                        eng.matmul(ps[:, t * P - SPAN:t * P], half[:, 0, :], corner[:, par, 0, u, :], start=False, stop=False)
                        eng.matmul(lo[:, t * P - SPAN:t * P], corner[:, par, 1, u - QUAD, :], c.ident[:, 64:128],
                                   start=False, stop=False)
                    if t < QT - 1:
                        eng.matmul(ps[:, (t + 1) * P:(t + 1) * P + SPAN], half[:, 1, :], corner[:, par, 0, u, :],
                                   start=False, stop=False)
                        eng.matmul(hi[:, (t + 1) * P:(t + 1) * P + SPAN], corner[:, par, 1, u + QUAD, :], c.ident[:, 0:64],
                                   start=False, stop=False)
                    eng.matmul(ps[:, at], diag[:, par, 1, u, :], c.ident[:, :], start=False, stop=True).then_inc(s["scores"], 1)

                def transposes(b, u):
                    n = g * B + b
                    eng.wait_ge(s["exps"], n * UNITS + u + 1)
                    if u >= 2:
                        eng.wait_ge(s["probs_c"], n * UNITS + u - 1)
                    for k in range(QT):
                        mm = eng.transpose(c.ps[:, 2 + u % 2, k * P:(k + 1) * P], E[:, u % 2, k * P:(k + 1) * P], c.ident[:, :])
                    mm.then_inc(s["probs_t"], 1)

                def mixes(b, u):
                    n = g * B + b
                    h = u % QUAD
                    if u == 0:
                        eng.wait_ge(s["normed"], n + 1)
                    eng.wait_ge(s["probs_c"], n * UNITS + u + 1)
                    for k in range(QT):
                        mm = eng.matmul(c.ps[:, 4, u * DH:(u + 1) * DH], PT[:, u % 2, k * P:(k + 1) * P],
                                        V[:, b % 2, k, 32 * h:32 * h + DH], start=k == 0, stop=k == QT - 1)
                    mm.then_inc(s["mixed"], 1)

                eng.wait_ge(s["weights"], 16 * g + 16)
                eng.wait_ge(s["ab_copied"], g * B * COPIES + 1)
                eng.matmul(c.ps[:, 5, 0:P], W[:, Wpk, :], rel[:, 0, :], start=True, stop=True)
                eng.matmul(c.ps[:, 6, 0:P], W[:, Wpq, :], rel[:, 1, :], start=True, stop=True).then_inc(s["tables_ps"], 1)
                eng.wait_ge(s["tables"], g * 9 + 9)
                for kind, b in ORDER:
                    if kind == 1:
                        bands(b)
                        continue
                    eng.wait_ge(s["windows"], (g * B + b + 1) * 6 * 16)
                    scores(b, 0)
                    for u in range(UNITS):
                        if u + 1 < UNITS:
                            scores(b, u + 1)
                        transposes(b, u)
                        if u:
                            mixes(b, u - 1)
                    mixes(b, UNITS - 1)
            eng.wait_ge(s["placed"], GROUPS)
            for b in range(B):
                for t in range(QT):
                    mm = eng.transpose(c.ps[:, b, t * P:(t + 1) * P], O[:, b, t, :], c.ident[:, :])
                mm.then_inc(s["out_t"], 1)
            for b in range(B):
                eng.wait_ge(s["out_c"], b + 1)
                eng.matmul(c.ps[:, 4 + b, :], Wo[:, :], OC[:, b, :], start=True, stop=True).then_inc(s["out"], 1)

        @block.scalar
        def _(eng):
            eng.sem_inc(s["ab_copied"], 1)
            eng.wait_ge(s["loaded"], 16 * len(pairs))
            with eng.Fori(0, GROUPS) as g:
                for kind, b in ORDER:
                    n = g * B + b
                    if kind == 1:
                        eng.wait_ge(s["projected"], n + 1)
                        eng.activation(VC[:, :], c.ps[:, 5 + Wv, :], ACT.Identity, bias=ends[:, 4:5]).then_inc(s["kept"], 1)
                        eng.wait_ge(s["values_t"], n + 1)
                        eng.activation(V[:, b % 2, :, :], c.ps[:, 5, :].rearrange("p (t c) -> p t c", t=QT), ACT.Copy)\
                           .then_inc(s["ab_copied"], 1)
                        eng.wait_ge(s["wrote"], n * 16 * 2 * QT + 1)
                        for u in range(UNITS):
                            eng.wait_ge(s["ab"], n * UNITS + u + 1)
                            eng.activation(AB[:, u, :, :], c.ps[:, 6 + u % 2, :].rearrange("p (k c) -> p k c", k=2), ACT.Copy)\
                               .then_inc(s["ab_copied"], 1)
                        continue
                    for u in range(UNITS):
                        eng.wait_ge(s["maxima"], n * UNITS + u + 1)
                        if u >= 2:
                            eng.wait_ge(s["probs_t"], n * UNITS + u - 1)
                        eng.activation(E[:, u % 2, :], c.ps[:, u % 2, :], ACT.Exp, bias=top[:, u:u + 1],
                                       accum_out=total[:, u:u + 1]).then_inc(s["exps"], 1)

        @block.vector
        def _(eng):
            eng.memset(zeros[:, :, :], 0.0).then_inc(s["zeros"], 1)
            eng.memset(B_table[:, 0:1], 0.0)
            eng.sem_inc(s["normed"], 1)
            eng.wait_ge(s["loaded"], 16 * len(pairs))
            with eng.Fori(0, GROUPS) as g:
                def table(ins):
                    ins.then_inc(s["tables"], 1)

                def group_bias(i):
                    return bias[:, bass.ds(g, 1), i]

                eng.wait_ge(s["tables_ps"], g + 1)
                table(eng.tensor_scalar(pk[:, :], c.ps[:, 5, 0:P], group_bias(Wpk), None, ALU.add))
                table(eng.tensor_scalar(pq[:, :], c.ps[:, 6, 0:P], group_bias(Wpq), None, ALU.add))
                eng.wait_ge(s["tables"], g * 9 + 2)
                pk_low, pk_up, pq_low, pq_up = pk[:, 0:1], pk[:, P - 1:P], pq[:, P - 1:P], pq[:, 0:1]
                table(eng.tensor_scalar(A_table[:, 0:P], pk[:, :], pk_low, None, ALU.subtract))
                table(eng.tensor_scalar(A_table[:, P:LOW], pk_up.to_broadcast([P, LOW - P]), pk_low, None, ALU.subtract))
                table(eng.tensor_scalar(A_table[:, LOW:], pk[:, SPAN:], pk_up, None, ALU.subtract))
                table(eng.tensor_scalar(B_table[:, 1:UP], pq[:, 0:UP - 1], pq_up, scale, ALU.subtract, ALU.mult))
                table(eng.tensor_scalar(B_table[:, UP:2 * UP + 1], pq_up.to_broadcast([P, UP + 1]), pq_low, scale,
                                        ALU.subtract, ALU.mult))
                table(eng.tensor_scalar(B_table[:, 2 * UP + 1:], pq[:, 0:P - 1], pq_low, scale, ALU.subtract, ALU.mult))
                for i, (w, end) in enumerate(((Wq, pq_low), (Wq, pq_up), (Wk, pk_low), (Wk, pk_up))):
                    eng.tensor_tensor(ends[:, i:i + 1], group_bias(w), end, ALU.add)
                table(eng.tensor_copy(ends[:, 4:5], group_bias(Wv)))
                eng.wait_ge(s["tables"], g * 9 + 9)
                for kind, b in ORDER:
                    n = g * B + b
                    if kind == 1:
                        eng.wait_ge(s["projected"], n + 1)
                        for i in (Q_LOW, Q_UP):
                            eng.tensor_scalar(QK[:, b % 2, i, :], c.ps[:, 5 + Wq, :], ends[:, i:i + 1], scale, ALU.add, ALU.mult)
                        for i in (K_LOW, K_UP):
                            last = eng.tensor_scalar(QK[:, b % 2, i, :], c.ps[:, 5 + Wk, :], ends[:, i:i + 1], None, ALU.add)
                        last.then_inc(s["qk"], 1)
                        continue
                    for u in range(UNITS + 1):
                        if u < UNITS:
                            eng.wait_ge(s["scores"], n * UNITS + u + 1)
                            eng.tensor_reduce(top[:, u:u + 1], c.ps[:, u % 2, :], AXX, ALU.max, negate=True).then_inc(s["maxima"], 1)
                        if u:
                            eng.wait_ge(s["probs_t"], n * UNITS + u)
                            if u >= 3:
                                eng.wait_ge(s["mixed"], n * UNITS + u - 2)
                            eng.tensor_copy(PT[:, (u - 1) % 2, :], c.ps[:, 2 + (u - 1) % 2, :]).then_inc(s["probs_c"], 1)
                    eng.wait_ge(s["exps"], (n + 1) * UNITS)
                    eng.reciprocal(inverse[:, :], total[:, :]).then_inc(s["inverted"], 1)
                    eng.wait_ge(s["mixed"], (n + 1) * UNITS)
                    eng.wait_ge(s["inverted"], n + 1)
                    eng.tensor_tensor(OG[:, b, :, :].rearrange("p t (h c) -> p (t h) c", h=QUAD),
                                      c.ps[:, 4, 0:UNITS * DH].rearrange("p (u c) -> p u c", c=DH),
                                      inverse[:, :].unsqueeze(2).to_broadcast([P, UNITS, DH]), ALU.mult).then_inc(s["normed"], 1)
                eng.wait_ge(s["normed"], g * B + B + 1)
                eng.tensor_copy(O[:, :, :, bass.ds(g * QUAD * DH, QUAD * DH)], OG[:, :, :, :]).then_inc(s["placed"], 1)
                eng.wait_ge(s["placed"], g + 1)
            for b in range(B):
                eng.wait_ge(s["out_t"], b + 1)
                eng.tensor_copy(OC[:, b, :], c.ps[:, b, :]).then_inc(s["out_c"], 1)
            for b in range(B):
                eng.wait_ge(s["out"], b + 1)
                eng.scalar_tensor_tensor(c.R[:, b, :], c.ps[:, 4 + b, :], bo[:, 0:1], c.X[:, b, PAD:PAD + T], ALU.add, ALU.add)


def delta_attention(c):
    d = c.dram
    CH = 32
    NC = T // CH
    M = 8
    NP = B * M
    DK = 64
    X2 = 2 * CH
    TAPS = PAD + 1
    I = 32
    ID = 21
    GR, GP = 8, NP // 8
    names = ("loaded", "staged", "scaled_w", "zeroed", "beta_ps", "beta", "proj", "evac", "kq", "d0", "g", "gt", "chain",
             "handled", "y", "yt", "pool_chain", "dve_done", "o", "w", "pd", "t", "wc", "ktc", "upd", "decayed",
             "state", "kc", "centred", "gate_ps", "squared", "gate", "var", "log", "rstd", "pool_out", "normed", "wo",
             "wo_copied", "pe_past", "pool_past")
    s = {n: c.sem("dl_" + n) for n in names}
    with ExitStack() as ctx:
        taps = [c.sb(f"dl_taps_{n}", [P, TAPS, M * P], ctx) for n in "kqv"]
        Wa = c.sb("dl_Wa", [P, M * P], ctx)
        Wg = c.sb("dl_Wg", [P, M * P], ctx)
        Wo = c.sb("dl_Wo", [P, M, P], ctx)
        Wb = c.sb("dl_Wb", [P, B, P], ctx)
        vec = c.sb("dl_vec", [P, 4 * M + 3], ctx)
        sums = c.sb("dl_sums", [P, 3, P], ctx)
        eye = c.sb("dl_eye", [P, DK], ctx)
        beta = c.sb("dl_beta", [P, T + CH], ctx)
        bc = c.sb("dl_bc", [P, 2, CH], ctx)
        kkN = c.sb("dl_kkN", [P, NP, 2, CH], ctx)
        kqN = c.sb("dl_kqN", [P, NP, CH, 2], ctx)
        vN = c.sb("dl_vN", [P, NP, CH], ctx)
        aN = c.sb("dl_aN", [P, NP, CH], ctx)
        kc = c.sb("dl_kc", [P, NP, CH], ctx)
        d0 = c.sb("dl_d0", [P, NP, CH], ctx)
        d1 = c.sb("dl_d1", [P, NP, CH], ctx)
        F = c.sb("dl_F", [P, NP, CH], ctx)
        whole = c.sb("dl_whole", [P, NP], ctx)
        Pd = c.sb("dl_Pd", [P, NP, DK], ctx)
        aT = c.sb("dl_aT", [P, CH, I], ctx)
        bv = c.sb("dl_bv", [P, CH, I], ctx)
        G = c.sb("dl_G", [P, X2, CH], ctx)
        Y = c.sb("dl_Y", [P, X2, I], ctx)
        tmp = c.sb("dl_tmp", [P, X2, I], ctx)
        U = c.sb("dl_U", [P, CH, I], ctx)
        UT = tmp[:, CH:, :]
        W = c.sb("dl_W", [P, NP, CH], ctx)
        WT = c.sb("dl_WT", [CH, 2, GP * P], ctx)
        KT = c.sb("dl_KT", [CH, 2, GP * P], ctx)
        ST = c.sb("dl_ST", [P, NP, DK], ctx)
        O = c.sb("dl_O", [P, CH, NP], ctx)
        D = c.sb("dl_D", [P, CH, NP], ctx)
        Q = c.sb("dl_Q", [P, CH * NP], ctx)
        gate = c.sb("dl_gate", [P, CH, NP], ctx)
        back = c.sb("dl_back", [P, B, CH], ctx)
        BB, LW, LB = 4 * M, 4 * M + 1, 4 * M + 2
        pairs = [(taps[i][:, :, :], d["dl_cw"][:, i]) for i in range(3)] + [
            (Wa[:, :], d["dl_Wa"]), (Wg[:, :], d["dl_Wg"]), (Wo[:, :, :], d["dl_Wo"]), (Wb[:, :, :], d["dl_Wb"]),
            (vec[:, :], d["dl_vec"]), (sums[:, :, :], d["dl_sums"]), (eye[:, :], d["dl_eye"])]
        flat = (tmp[:, :, :].rearrange("p x i -> p (x i)"), Y[:, :, :].rearrange("p x i -> p (x i)"))
        plain = [flat[0][:, 0:M * P], flat[0][:, M * P:2 * M * P], flat[1][:, 0:M * P]]
        PROJ = 8
        K, QQ, V, A = range(4)
        ps = c.ps
        state_ps = ps[:, 2:6, :].rearrange("p k (n x) -> p (k n) x", x=X2)
        block = c.block(ctx)

        def chunk_of(buf, n, first=0):
            return buf[:, :, bass.ds(n * CH + first, CH)] if not isinstance(n, int) else buf[:, :, n * CH + first:n * CH + first + CH]


        @block.sync
        def _(eng):
            load_all(eng, s["loaded"], pairs)
            for dst, name in zip(plain, "kqv"):
                eng.dma_start(dst, d[f"dl_W{name}"]).then_inc(s["staged"], 16)

        @block.tensor
        def _(eng):
            def project(n, first):
                if not first:
                    eng.wait_ge(s["handled"], n)
                for i in range(PROJ):
                    if i >= 2 or not first:
                        eng.wait_ge(s["evac"], n * PROJ + i - 1)
                    w, half = i // 2, i % 2
                    for m in range(4 * half, 4 * half + 4):
                        out = ps[:, i % 2, (m % 4) * P:(m % 4 + 1) * P]
                        cols = slice(m * P, (m + 1) * P)
                        if w == A:
                            mm = eng.matmul(out, Wa[:, cols], chunk_of(c.X, n, PAD), start=True, stop=True)
                        else:
                            for tap in range(TAPS):
                                mm = eng.matmul(out, taps[w][:, tap, cols], chunk_of(c.X, n, tap),
                                                start=tap == 0, stop=tap == TAPS - 1)
                    mm.then_inc(s["proj"], 1)

            def products_of_keys(n, first):
                eng.wait_ge(s["kq"], 2 * n + 2)
                if not first:
                    eng.wait_ge(s["yt"], n)
                eng.sem_inc(s["pe_past"], 1)
                for pair in range(NP):
                    for h in range(2):
                        rows = slice(DK * h, DK * h + DK)
                        mm = eng.matmul(state_ps[rows, pair, :], kkN[rows, pair, :, :].rearrange("p k t -> p (k t)"), kqN[rows, pair, :, :].rearrange("p t k -> p (t k)"),
                                        start=True, stop=True)
                mm.then_inc(s["g"], 1)

            def start(n, first):
                if not first:
                    eng.wait_ge(s["state"], GR * n)
                eng.wait_ge(s["gt"], n + 1)
                eng.sem_inc(s["pe_past"], 1)
                for pair in range(NP):
                    for h in range(2):
                        rows = slice(DK * h, DK * h + DK)
                        mm = eng.matmul(state_ps[rows, pair, :], ST[rows, pair, :], kqN[rows, pair, :, :].rearrange("p t k -> p (t k)"),
                                        start=True, stop=True)
                mm.then_inc(s["y"], 1)

            def end(n):
                def update(g):
                    at = GR * n + g + 1
                    eng.wait_ge(s["wc"], at)
                    eng.wait_ge(s["ktc"], at)
                    if g >= 2:
                        eng.wait_ge(s["state"], at - 2)
                    bank = ps[:, 6 + g % 2, :]
                    eng.matmul(bank[:, GP * DK:2 * GP * DK], sums[:, 0, :],
                               Pd[:, g * GP:(g + 1) * GP, :].rearrange("p n i -> p (n i)"), start=True, stop=True)
                    for j in range(GP):
                        for h in range(2):
                            cols = slice(j * P + DK * h, j * P + DK * h + DK)
                            mm = eng.matmul(bank[DK * h:DK * h + DK, j * DK:(j + 1) * DK], KT[:, g % 2, cols], WT[:, g % 2, cols],
                                            start=True, stop=True)
                    mm.then_inc(s["upd"], 1)

                eng.wait_ge(s["pd"], n + 1)
                eng.wait_ge(s["kc"], n + 1)
                eng.wait_ge(s["w"], n + 1)
                eng.wait_ge(s["evac"], (n + 2) * PROJ)
                for g in range(GR):
                    if g:
                        eng.wait_ge(s["wc"], GR * n + g)
                        eng.wait_ge(s["ktc"], GR * n + g)
                    for bank, src in ((0, W), (1, kc)):
                        for j in range(GP):
                            mm = eng.transpose(ps[0:CH, bank, j * P:(j + 1) * P], src[:, g * GP + j, :], c.ident[:, :])
                    mm.then_inc(s["t"], 1)
                    if g:
                        update(g - 1)
                update(GR - 1)

            def output(n):
                eng.wait_ge(s["o"], n + 1)
                Of = O[:, :, :].rearrange("p t n -> p (t n)")
                for k in range(2):
                    mm = eng.matmul(ps[:, k, :], sums[:, 2, :], Of[:, k * 512:(k + 1) * 512], start=True, stop=True)
                mm.then_inc(s["centred"], 1)
                for m in range(M):
                    mm = eng.matmul(ps[:, 6 + m // 4, (m % 4) * P:(m % 4 + 1) * P], Wg[:, m * P:(m + 1) * P], chunk_of(c.X, n, PAD),
                                    start=True, stop=True)
                mm.then_inc(s["gate_ps"], 1)
                eng.wait_ge(s["squared"], n + 1)
                eng.wait_ge(s["gate"], n + 1)
                for k in range(2):
                    mm = eng.matmul(ps[:, 6 + k, :], sums[:, 1, :], Q[:, k * 512:(k + 1) * 512], start=True, stop=True)
                mm.then_inc(s["var"], 1)
                eng.wait_ge(s["normed"], n + 1)
                Dv = D[:, :, :].rearrange("p t (b m) -> p m b t", m=M)
                for m in range(M):
                    mm = eng.matmul(ps[:, 0, 0:P], Wo[:, m, :], Dv[:, m, :, :], start=m == 0, stop=m == M - 1)
                mm.then_inc(s["wo"], 1)
                eng.wait_ge(s["wo_copied"], n + 1)

            def one_pass(n, first):
                if not first:
                    output(n - 1)
                project(n + 1, False)
                products_of_keys(n + 1, False)
                end(n)
                start(n + 1, False)

            eng.wait_ge(s["loaded"], 16 * len(pairs))
            for b in range(B):
                mm = eng.matmul(ps[:, 7, :], Wb[:, b, :], c.X[:, b, PAD:PAD + T], start=b == 0, stop=b == B - 1)
            mm.then_inc(s["beta_ps"], 1)
            eng.wait_ge(s["scaled_w"], 3)
            eng.wait_ge(s["zeroed"], 1)
            project(0, True)
            products_of_keys(0, True)
            start(0, True)
            one_pass(0, True)
            with eng.Fori(1, NC) as n:
                one_pass(n, False)
            output(NC - 1)

        @block.scalar
        def _(eng):
            def project(n, first):
                if not first:
                    eng.wait_ge(s["y"], n)
                    eng.wait_ge(s["handled"], n)
                    eng.wait_ge(s["kc"], n)
                for i in range(PROJ):
                    w, half = i // 2, i % 2
                    eng.wait_ge(s["proj"], n * PROJ + i + 1)
                    dst = (kkN[:, :, 0, :], kqN[:, :, :, 1], vN[:, :, :], aN[:, :, :])[w]
                    for m in range(4 * half, 4 * half + 4):
                        ins = eng.activation(dst[:, m:NP:M, :], ps[:, i % 2, (m % 4) * P:(m % 4 + 1) * P].rearrange("p (b t) -> p b t", b=B),
                                             ACT.Sigmoid if w == A else ACT.Silu, bias=vec[:, w * M + m:w * M + m + 1])
                    ins.then_inc(s["evac"], 1)
                    if w == QQ and half == 1:
                        eng.wait_ge(s["evac"], n * PROJ + i + 1)
                        raw, scale = kkN[:, :, 0, :], float(DK) ** -0.5
                        eng.activation(kqN[:, :, :, 0], raw, ACT.Copy, scale=scale)
                        eng.activation(kkN[:, :, 1, :], raw, ACT.Copy, scale=scale).then_inc(s["kq"], 1)
                        eng.wait_ge(s["kq"], 2 * n + 1)
                        eng.activation(raw, raw, ACT.Copy, scale=scale).then_inc(s["kq"], 1)
                eng.wait_ge(s["evac"], (n + 1) * PROJ)
                eng.activation(d0[:, :, 0:CH - 1], aN[:, :, 1:CH], ACT.Copy).then_inc(s["d0"], 1)

            def keep_keys(n):
                eng.wait_ge(s["kq"], 2 * n + 2)
                eng.activation(kc[:, :, :], kqN[:, :, :, 0], ACT.Copy).then_inc(s["kc"], 1)

            def end(n):
                for g in range(GR):
                    at = GR * n + g + 1
                    eng.wait_ge(s["t"], at)
                    if g >= 2:
                        eng.wait_ge(s["upd"], at - 2)
                    eng.activation(KT[:, g % 2, :], ps[0:CH, 1, :], ACT.Copy).then_inc(s["ktc"], 1)
                keep_keys(n + 1)

            def output(n):
                eng.wait_ge(s["centred"], n + 1)
                Df = D[:, :, :].rearrange("p t n -> p (t n)")
                for k in range(2):
                    eng.activation(Df[:, k * 512:(k + 1) * 512], ps[:, k, :], ACT.Copy)
                for k in range(2):
                    ins = eng.activation(Q[:, k * 512:(k + 1) * 512], ps[:, k, :], ACT.Square)
                ins.then_inc(s["squared"], 1)
                eng.wait_ge(s["gate_ps"], n + 1)
                gv = gate[:, :, :].rearrange("p t (b m) -> p m b t", m=M)
                for m in range(M):
                    ins = eng.activation(gv[:, m, :, :], ps[:, 6 + m // 4, (m % 4) * P:(m % 4 + 1) * P].rearrange("p (b t) -> p b t", b=B),
                                         ACT.Sigmoid)
                ins.then_inc(s["gate"], 1)
                eng.wait_ge(s["var"], n + 1)
                for k in range(2):
                    ins = eng.activation(Q[:, k * 512:(k + 1) * 512], ps[:, 6 + k, :], ACT.Ln, bias=c.eps[:, 0:1])
                ins.then_inc(s["log"], 1)
                eng.wait_ge(s["log"], n + 1)
                eng.activation(Q[:, :], Q[:, :], ACT.Exp, scale=-0.5).then_inc(s["rstd"], 1)
                eng.wait_ge(s["wo"], n + 1)
                eng.activation(back[:, :, :], ps[:, 0, 0:P].rearrange("p (b t) -> p b t", b=B), ACT.Copy).then_inc(s["wo_copied"], 1)

            def one_pass(n, first):
                if not first:
                    output(n - 1)
                project(n + 1, False)
                end(n)

            eng.wait_ge(s["loaded"], 16 * len(pairs))
            eng.wait_ge(s["zeroed"], 1)
            eng.wait_ge(s["beta_ps"], 1)
            eng.activation(beta[:, 0:T], ps[:, 7, :], ACT.Sigmoid, bias=vec[:, BB:BB + 1]).then_inc(s["beta"], 1)
            project(0, True)
            keep_keys(0)
            one_pass(0, True)
            with eng.Fori(1, NC) as n:
                one_pass(n, False)
            output(NC - 1)

        def steps(eng, lo, hi, chain, base, fused, midway):
            count = [0]

            def link(ins):
                count[0] += 1
                ins.then_inc(chain, 1)

            def before(k=0):
                eng.wait_ge(chain, base + count[0] - k)

            n = hi - lo
            for t in range(CH):
                rest = X2 - 1 - 2 * t
                if t:
                    before()
                if fused:
                    link(eng.scalar_tensor_tensor(U[:, t, lo:hi], Y[:, 2 * t, lo:hi], bc[:, 1, t:t + 1], bv[:, t, lo:hi], ALU.mult, ALU.add))
                else:
                    link(eng.tensor_tensor(U[:, t, lo:hi], Y[:, 2 * t, lo:hi], bc[:, 1, t:t + 1].to_broadcast([P, n]), ALU.mult))
                    before()
                    link(eng.tensor_tensor(U[:, t, lo:hi], U[:, t, lo:hi], bv[:, t, lo:hi], ALU.add))
                y = Y[:, 2 * t + 1:, lo:hi]
                link(eng.tensor_tensor(y, y, aT[:, t, lo:hi].unsqueeze(1).to_broadcast([P, rest, n]), ALU.mult))
                before(1)
                link(eng.tensor_tensor(tmp[:, 2 * t + 1:, lo:hi], G[:, 2 * t + 1:, t].unsqueeze(2).to_broadcast([P, rest, n]),
                                       U[:, t, lo:hi].unsqueeze(1).to_broadcast([P, rest, n]), ALU.mult))
                before()
                link(eng.tensor_tensor(y, y, tmp[:, 2 * t + 1:, lo:hi], ALU.add))
                if t in midway:
                    midway[t]()
            return count[0]

        POOL_LINKS, DVE_LINKS = 5 * CH, 4 * CH

        @block.gpsimd
        def _(eng):
            def diagonal(n, first):
                eng.wait_ge(s["handled"], n + 1)
                if not first:
                    eng.wait_ge(s["upd"], GR * n)
                eng.tensor_tensor(Pd[:, :, :], whole[:, :].unsqueeze(2).to_broadcast([P, NP, DK]),
                                  eye[:, :].unsqueeze(1).to_broadcast([P, NP, DK]), ALU.mult).then_inc(s["pd"], 1)

            def norm(n):
                eng.wait_ge(s["rstd"], n + 1)
                Df = D[:, :, :].rearrange("p t n -> p (t n)")
                at = 3 * n
                eng.tensor_tensor(Df, Df, Q[:, :], ALU.mult).then_inc(s["pool_out"], 1)
                eng.wait_ge(s["pool_out"], at + 1)
                eng.sem_inc(s["pool_past"], 1)
                eng.tensor_scalar(Df, Df, vec[:, LW:LW + 1], vec[:, LB:LB + 1], ALU.mult, ALU.add).then_inc(s["pool_out"], 1)
                eng.wait_ge(s["pool_out"], at + 2)
                eng.tensor_tensor(D[:, :, :], D[:, :, :], gate[:, :, :], ALU.mult).then_inc(s["normed"], 1)

            def residual(n):
                eng.wait_ge(s["wo_copied"], n + 1)
                eng.tensor_tensor(chunk_of(c.R, n), chunk_of(c.X, n, PAD), back[:, :, :], ALU.add).then_inc(s["pool_out"], 1)

            def one_pass(n, first):
                eng.wait_ge(s["yt"], n + 1)
                midway = {} if first else {6: lambda: norm(n - 1), 14: lambda: residual(n - 1)}
                assert steps(eng, ID, I, s["pool_chain"], n * POOL_LINKS, False, midway) == POOL_LINKS
                eng.wait_ge(s["pool_chain"], (n + 1) * POOL_LINKS)
                diagonal(n + 1, False)

            eng.wait_ge(s["loaded"], 16 * len(pairs))
            diagonal(0, True)
            one_pass(0, True)
            with eng.Fori(1, NC) as n:
                one_pass(n, False)
            norm(NC - 1)
            residual(NC - 1)

        @block.vector
        def _(eng):
            HANDLES = 3

            def handle(n, first):
                at = HANDLES * n
                eng.tensor_copy(bc[:, 0, :], beta_chunk(n))
                eng.tensor_scalar(bc[:, 1, :], beta_chunk(n), -1.0, None, ALU.mult).then_inc(s["chain"], 1)
                eng.wait_ge(s["g"], n + 1)
                eng.transpose(G[:, :, :], state_ps.rearrange("p n x -> p x n")).then_inc(s["gt"], 1)
                eng.wait_ge(s["evac"], (n + 1) * PROJ)
                vT = tmp[:, 0:CH, :]
                eng.transpose(vT, vN[:, :, :].rearrange("p n t -> p t n")).then_inc(s["chain"], 1)
                eng.transpose(aT[:, :, :], aN[:, :, :].rearrange("p n t -> p t n"))
                eng.wait_ge(s["chain"], at + 2)
                eng.tensor_tensor(bv[:, :, :], vT, bc[:, 0, :].unsqueeze(2).to_broadcast([P, CH, I]), ALU.mult)
                eng.wait_ge(s["d0"], n + 1)
                eng.tensor_tensor_scan(F[:, :, :].rearrange("p n t -> p (n t)")[:, ::-1], d0[:, :, :].rearrange("p n t -> p (n t)")[:, ::-1],
                                       d1[:, :, :].rearrange("p n t -> p (n t)")[:, ::-1], 0.0, ALU.mult, ALU.add).then_inc(s["chain"], 1)
                eng.wait_ge(s["chain"], at + 3)
                eng.tensor_tensor(whole[:, :], F[:, :, 0], aN[:, :, 0], ALU.mult).then_inc(s["handled"], 1)

            def beta_chunk(n):
                return beta[:, n * CH:(n + 1) * CH] if isinstance(n, int) else beta[:, bass.ds(n * CH, CH)]

            def start(n):
                eng.wait_ge(s["y"], n + 1)
                eng.transpose(Y[:, :, :], state_ps.rearrange("p n x -> p x n")).then_inc(s["yt"], 1)

            def end(n, first):
                eng.wait_ge(s["pool_chain"], (n + 1) * POOL_LINKS)
                eng.wait_ge(s["dve_done"], (n + 1) * DVE_LINKS)
                if not first:
                    eng.wait_ge(s["centred"], n)
                eng.transpose(O[:, :, :], Y[:, 1::2, :]).then_inc(s["o"], 1)
                eng.transpose(UT, U[:, :, :]).then_inc(s["decayed"], 1)
                eng.wait_ge(s["decayed"], (n + 1) * (GR + 1) - GR)
                eng.tensor_tensor(W[:, :, :], UT.rearrange("p t n -> p n t"), F[:, :, :], ALU.mult).then_inc(s["w"], 1)

                def update(g):
                    at = GR * n + g + 1
                    eng.wait_ge(s["upd"], at)
                    mine = ST[:, g * GP:(g + 1) * GP, :]
                    bank = ps[:, 6 + g % 2, :].rearrange("p (k n i) -> p k n i", k=2, i=DK)
                    eng.tensor_tensor(mine, mine, bank[:, 1, :, :], ALU.mult).then_inc(s["decayed"], 1)
                    eng.wait_ge(s["decayed"], (n + 1) * (GR + 1) - GR + g + 1)
                    eng.tensor_tensor(mine, mine, bank[:, 0, :, :], ALU.add).then_inc(s["state"], 1)

                for g in range(GR):
                    at = GR * n + g + 1
                    eng.wait_ge(s["t"], at)
                    if g >= 2:
                        eng.wait_ge(s["upd"], at - 2)
                    eng.tensor_copy(WT[:, g % 2, :], ps[0:CH, 0, :]).then_inc(s["wc"], 1)
                    if g:
                        update(g - 1)
                update(GR - 1)

            def one_pass(n, first):
                assert steps(eng, 0, ID, s["dve_done"], n * DVE_LINKS, True, {}) == DVE_LINKS
                end(n, first)
                handle(n + 1, False)
                start(n + 1)

            for i in range(3):
                eng.wait_ge(s["loaded"], 16 * len(pairs))
                eng.wait_ge(s["staged"], 16 * 3)
                eng.tensor_tensor(taps[i][:, :, :], taps[i][:, :, :], plain[i].unsqueeze(1).to_broadcast([P, TAPS, M * P]), ALU.mult)\
                   .then_inc(s["scaled_w"], 1)
            eng.memset(ST[:, :, :], 0.0)
            eng.memset(beta[:, T:], 0.0)
            eng.memset(d0[:, :, CH - 1:], 0.0)
            eng.memset(d1[:, :, 0:CH - 1], 0.0)
            eng.memset(d1[:, :, CH - 1:], 1.0).then_inc(s["zeroed"], 1)
            eng.wait_ge(s["scaled_w"], 3)
            eng.wait_ge(s["zeroed"], 1)
            eng.wait_ge(s["beta"], 1)
            handle(0, True)
            start(0)
            eng.wait_ge(s["yt"], 1)
            one_pass(0, True)
            with eng.Fori(1, NC) as n:
                eng.wait_ge(s["yt"], n + 1)
                one_pass(n, False)


LAYERS = [delta_attention, ternary_ffn, relative_attention, hashed_ffn, rwkv_attention, lowrank_ffn, rotary_attention, routed_ffn]


def build(nc, dram):
    with ExitStack() as ctx:
        c = Chip(nc, ctx, dram)
        c.ln = {n: c.sem(n) for n in ("ln_mean", "ln_centred", "ln_squared", "ln_var", "ln_log", "ln_rstd")}
        load_start(c)
        for layer in LAYERS:
            layer(c)
            layernorm(c)
        store_end(c)


def columns(*vectors):
    return np.concatenate([np.asarray(v).reshape(-1, P).T for v in vectors], axis=1)


def rows_in(w):
    w = np.asarray(w)
    return w.reshape(-1, P, w.shape[1]).transpose(1, 0, 2)


def quads(w, *at):
    w = np.asarray(w)
    w = w.reshape(GROUPS, QUAD, DH, w.size // P)
    out = np.zeros((w.shape[3], GROUPS, QUAD, 32), w.dtype)
    for offset in at or (0,):
        out[..., offset:offset + DH] = w.transpose(3, 0, 1, 2)
    return out.reshape(w.shape[3], GROUPS, P)


def laid_out(a):
    g = {k: np.asarray(v) for k, v in a.items()}
    L0, L1 = "L0_ffn_", "L1_ffn_"
    o = {
        "xT": g["L0_attn_x"].transpose(2, 0, 1),
        "identity": np.eye(P, dtype=np.float32),
        "tf_w1": g[L0 + "w1_w"].T, "tf_w2": g[L0 + "w2_w"].T, "tf_h1": rows_in(g[L0 + "h1_w"].T),
        "tf_h2": rows_in(g[L0 + "h2_w"].T), "tf_w3": rows_in(g[L0 + "w3_w"].T),
        "tf_s": columns(*(g[L0 + n] for n in ("w1_s", "w2_s", "h1_s", "h2_s", "w3_s"))),
        "hf_sw1": g[L1 + "sw1"], "hf_sw3": g[L1 + "sw3"], "hf_sw2": rows_in(g[L1 + "sw2"]),
        "hf_w1": g[L1 + "w1"].transpose(1, 0, 2), "hf_w2": g[L1 + "w2"].transpose(1, 0, 2),
        "hf_bias": columns(*(g[L1 + n] for n in ("sb1", "sb3", "sb2", "b1", "b2"))),
        "lf_W": g["L2_ffn_W"].T, "lf_V": g["L2_ffn_V_r"].T, "lf_C": g["L2_ffn_C"].T, "lf_b": columns(g["L2_ffn_b"]),
    }
    L3, R6 = "L3_ffn_", "L2_attn_"
    E = 12
    o |= {
        "rf_Wr": g[L3 + "Wr"], "rf_br": np.broadcast_to(g[L3 + "br"], (P, E)),
        "rf_order": np.broadcast_to(100.0 - np.arange(E, dtype=np.float32), (P, E)),
        "rf_pick": np.broadcast_to(np.eye(P, E, dtype=np.float32)[:, :, None], (P, E, P)),
        "rf_be2": np.concatenate([g[L3 + "be2"], np.zeros((P - E, P), np.float32)]), "rf_bias": columns(*(g[L3 + n] for n in ("be1", "bs1", "bs2"))),
        "rf_Ws1": g[L3 + "Ws1"].reshape(P, -1, P), "rf_Ws2": rows_in(g[L3 + "Ws2"]),
        "rf_We1": g[L3 + "We1"].reshape(E, P, -1, P).transpose(1, 0, 2, 3),
        "rf_We2": g[L3 + "We2"].reshape(E, -1, P, P).transpose(2, 0, 1, 3),
        "rw_maa": columns(*(g[R6 + n] for n in ("time_maa_x", "time_maa_w", "time_maa_k", "time_maa_v", "time_maa_r",
                                                "time_decay", "time_faaaa", "ln_g", "ln_b"))),
        "rw_w1": g[R6 + "time_maa_w1"], "rw_w2": g[R6 + "time_maa_w2"].reshape(P, P),
        "rw_dw1": g[R6 + "time_decay_w1"], "rw_dw2": g[R6 + "time_decay_w2"],
        "rw_Wrkv": np.stack([g[R6 + n] for n in ("W_k", "W_v", "W_r")], axis=1), "rw_Wo": g[R6 + "W_o"],
    }
    swap = np.arange(P) ^ 1
    wq, wk, wv = (g["L3_attn_" + n] for n in ("wq", "wk", "wv"))
    o["ra_W"] = np.stack([quads(w) for w in (wq, wq[swap], wk, wk[swap], wv)], axis=2)
    inverse = (1.0 / np.float32(10000.0) ** (np.arange(0, DH, 2, dtype=np.float32) / np.float32(DH))).astype(np.float32)
    angle = np.outer(np.arange(T, dtype=np.float32), inverse).astype(np.float32)
    rope = np.zeros((P, 4, T), np.float32)
    for ch in range(DH):
        for h in range(QUAD):
            cos, sin = np.cos(angle[:, ch // 2]), np.sin(angle[:, ch // 2]) * (1 if ch % 2 else -1)
            rope[32 * h + ch] = np.stack([cos * DH ** -0.5, sin * DH ** -0.5, cos, sin])
    o["ra_rope"] = rope
    D = "L1_attn_"
    at = {"q": (0, DH), "k": (0, 2 * DH), "v": (0,), "pk": (DH,), "pq": (2 * DH,)}
    w = np.stack([quads(g[D + "W" + n], *k) for n, k in at.items()], axis=2)
    o["da_W"] = np.concatenate([w, w[:, :1]], axis=1)
    o["da_bias"] = np.stack([quads(g[D + "b" + n], *k)[0].T for n, k in at.items()], axis=2)
    rel = g[D + "rel_emb"].T
    o |= {"da_rel": np.stack([rel, rel[:, ::-1]], axis=1), "da_Wo": g[D + "Wo"].T, "da_bo": columns(g[D + "bo"])}
    eye = np.eye(P, dtype=np.float32)
    o["da_half"] = np.stack([eye * (np.arange(P)[:, None] < 64), eye * (np.arange(P)[:, None] >= 64)], axis=1)
    D = "L0_attn_"
    for n in "kqvag":
        o["dl_W" + n] = g[D + "W" + n].T
    cw = np.stack([g[D + n + "cw"][:, 0, :].T for n in "kqv"])
    o["dl_cw"] = np.broadcast_to(cw, (P, *cw.shape))
    o["dl_Wo"] = rows_in(g[D + "Wo"].T)
    head = np.zeros((2, 2, B, 8), int) + 2 * np.arange(8) + np.arange(2)[:, None, None, None]
    batch = np.zeros((2, 2, B, 8), int) + np.arange(B)[:, None]
    head, batch = head.ravel(), batch.ravel()
    Wb = np.zeros((P, B, P), np.float32)
    for b in range(B):
        Wb[:, b, batch == b] = g[D + "Wb"].T[:, head[batch == b]]
    o["dl_Wb"] = Wb
    o["dl_vec"] = np.concatenate([columns(*(g[D + n] for n in ("kcb", "qcb", "vcb", "ba"))), g[D + "bb"][head][:, None],
                                  np.tile(g[D + "ln_w"], 2)[:, None], np.tile(g[D + "ln_b"], 2)[:, None]], axis=1)
    same = (np.arange(P)[:, None] // 64 == np.arange(P)[None, :] // 64).astype(np.float32)
    o["dl_sums"] = np.stack([same, same / 64, np.eye(P, dtype=np.float32) - same / 64], axis=1)
    o["dl_eye"] = np.concatenate([np.eye(64, dtype=np.float32)] * 2)
    ch = np.arange(P)
    spread = np.zeros((P, 16, P), np.float32)
    for j in range(16):
        spread[(ch // 16) * 16 + j, j, ch] = 1.0
    o["rw_spread"], o["rw_gather"] = spread, spread.transpose(2, 1, 0)
    o["rw_heads"] = (ch[:, None] // 16 == ch[None, :] // 16).astype(np.float32)
    return o


def kernel(**inputs):
    import concourse.bacc as bacc
    from concourse.bass_utils import run_bass_kernel_spmd

    nc = bacc.Bacc("TRN2", target_bir_lowering=False, num_devices=1)
    arrays, dram = {}, {}
    for name, a in laid_out(inputs).items():
        a = np.ascontiguousarray(a)
        arrays[f"in_{name}"] = a
        dram[name] = nc.dram_tensor(f"in_{name}", a.shape, mybir.dt.from_np(a.dtype), kind="ExternalInput").ap()
    dram["outT"] = nc.dram_tensor("outT", (P, B, T), F32, kind="ExternalOutput").ap()
    build(nc, dram)
    r = run_bass_kernel_spmd(nc, [arrays], core_ids=[0])
    return np.ascontiguousarray(r.results[0]["outT"].transpose(1, 2, 0))
```

```python
from contextlib import ExitStack

import numpy as np
import concourse.bass as bass
from concourse import mybir

F32 = mybir.dt.float32
BF16 = mybir.dt.bfloat16
ALU = mybir.AluOpType
ACT = mybir.ActivationFunctionType
AXX = mybir.AxisListType.X

P = 128
B, T = 4, 512
N = B * T
PAD = 3
TAIL = 32
EPS = 1e-5


class Chip:

    def __init__(self, nc, ctx, dram):
        self.nc, self.ctx, self.dram = nc, ctx, dram
        self.X = self.sb("X", [P, B, PAD + T + TAIL])
        self.R = self.sb("R", [P, B, T])
        self.ones_mean = self.sb("ones_mean", [P, P])
        self.ident = self.sb("ident", [P, P])
        self.eps = self.sb("eps", [P, 1])
        self.ps = ctx.enter_context(nc.psum_tensor("ps", [P, 8, 512], F32))
        self.norms = 0
        self.past = self.sem("past")

    def sb(self, name, shape, ctx=None):
        return (ctx or self.ctx).enter_context(self.nc.sbuf_tensor(name, shape, F32))

    def sem(self, name):
        return self.ctx.enter_context(self.nc.semaphore(name))

    def block(self, ctx):
        return ctx.enter_context(self.nc.Block())


def load_start(c):
    loaded = c.sem("start_loaded")
    zeroed = c.sem("start_zeroed")
    with ExitStack() as ctx:
        block = c.block(ctx)

        @block.sync
        def _(eng):
            eng.wait_ge(zeroed, 1)
            for b in range(B):
                eng.dma_start(c.X[:, b, PAD:PAD + T], c.dram["xT"][:, b, :]).then_inc(loaded, 16)
            eng.dma_start(c.ident[:, :], c.dram["identity"]).then_inc(loaded, 16)
            eng.wait_ge(loaded, 16 * (B + 1))

        @block.vector
        def _(eng):
            eng.memset(c.X[:, :, PAD + T:], 0.0)
            eng.memset(c.X[:, :, 0:PAD], 0.0).then_inc(zeroed, 1)
            eng.memset(c.ones_mean[:, :], 1.0 / P)
            eng.memset(c.eps[:, :], EPS)


def layernorm(c):
    base = B * c.norms
    c.norms += 1
    mean, centred, squared, var, log, rstd = (c.ln[n] for n in (
        "ln_mean", "ln_centred", "ln_squared", "ln_var", "ln_log", "ln_rstd"))
    with ExitStack() as ctx:
        D = c.sb(f"ln_D{base}", [P, B, T], ctx)
        Q = c.sb(f"ln_Q{base}", [P, B, T], ctx)
        block = c.block(ctx)

        @block.tensor
        def _(eng):
            for b in range(B):
                eng.matmul(c.ps[:, b, :], c.ones_mean[:, :], c.R[:, b, :], start=True, stop=True).then_inc(mean, 1)
            for b in range(B):
                eng.wait_ge(squared, base + b + 1)
                eng.matmul(c.ps[:, 4 + b, :], c.ones_mean[:, :], Q[:, b, :], start=True, stop=True).then_inc(var, 1)

        @block.vector
        def _(eng):
            for b in range(B):
                eng.wait_ge(mean, base + b + 1)
                eng.tensor_tensor(D[:, b, :], c.R[:, b, :], c.ps[:, b, :], ALU.subtract).then_inc(centred, 1)
            for b in range(B):
                eng.wait_ge(rstd, base + b + 1)
                eng.wait_ge(centred, base + b + 1)
                eng.tensor_tensor(c.X[:, b, PAD:PAD + T], D[:, b, :], Q[:, b, :], ALU.mult)

        @block.scalar
        def _(eng):
            for b in range(B):
                eng.wait_ge(centred, base + b + 1)
                eng.activation(Q[:, b, :], D[:, b, :], ACT.Square).then_inc(squared, 1)
            for b in range(B):
                eng.wait_ge(var, base + b + 1)
                eng.activation(Q[:, b, :], c.ps[:, 4 + b, :], ACT.Ln, bias=c.eps[:, 0:1]).then_inc(log, 1)
            for b in range(B):
                eng.wait_ge(log, base + b + 1)
                eng.activation(Q[:, b, :], Q[:, b, :], ACT.Exp, scale=-0.5).then_inc(rstd, 1)


def store_end(c):
    stored = c.sem("stored")
    with ExitStack() as ctx:
        block = c.block(ctx)

        @block.sync
        def _(eng):
            for b in range(B):
                eng.dma_start(c.dram["outT"][:, b, :], c.X[:, b, PAD:PAD + T]).then_inc(stored, 16)
            eng.wait_ge(stored, 16 * B)


def load_all(eng, sem, pairs):
    for dst, src in pairs:
        eng.dma_start(dst, src).then_inc(sem, 16)
    return 16 * len(pairs)


def ternary_ffn(c):
    d = c.dram
    H = 512
    HT = H // P
    loaded, tiles = c.sem("tf_loaded"), c.sem("tf_tiles")
    act_done, dve_done = c.sem("tf_act_done"), c.sem("tf_dve_done")
    TILES, ACTS, DVES = 2 * HT + 2 * HT + 1, 3 * HT, HT + 1
    with ExitStack() as ctx:
        w1 = c.sb("tf_w1", [P, H], ctx)
        w2 = c.sb("tf_w2", [P, H], ctx)
        h1 = c.sb("tf_h1", [P, HT, H], ctx)
        h2 = c.sb("tf_h2", [P, HT, H], ctx)
        w3 = c.sb("tf_w3", [P, HT, P], ctx)
        s = c.sb("tf_s", [P, 4 * HT + 1], ctx)
        G = c.sb("tf_G", [P, HT, T], ctx)
        H1 = c.sb("tf_H1", [P, HT, T], ctx)
        H2 = c.sb("tf_H2", [P, HT, T], ctx)
        H3 = c.sb("tf_H3", [P, HT, T], ctx)
        pairs = [(w1[:, :], d["tf_w1"]), (w2[:, :], d["tf_w2"]), (s[:, :], d["tf_s"]), (h1[:, :, :], d["tf_h1"]),
                 (h2[:, :, :], d["tf_h2"]), (w3[:, :, :], d["tf_w3"])]
        block = c.block(ctx)

        @block.sync
        def _(eng):
            load_all(eng, loaded, pairs)

        @block.tensor
        def _(eng):
            eng.wait_ge(loaded, 16 * len(pairs))
            with eng.Fori(0, B) as b:
                x = c.X[:, b, PAD:PAD + T]
                eng.wait_ge(dve_done, b * DVES + 1)
                for m in range(HT):
                    cols = slice(m * P, (m + 1) * P)
                    eng.matmul(c.ps[:, 2 * m, :], w1[:, cols], x, start=True, stop=True).then_inc(tiles, 1)
                    eng.matmul(c.ps[:, 2 * m + 1, :], w2[:, cols], x, start=True, stop=True).then_inc(tiles, 1)
                eng.wait_ge(dve_done, b * DVES + HT + 1)
                for layer, (w, hid) in enumerate(((h1, H1), (h2, H2))):
                    if layer:
                        eng.wait_ge(act_done, b * ACTS + 2 * HT)
                    for m in range(HT):
                        for k in range(HT):
                            mm = eng.matmul(c.ps[:, 4 * layer + m, :], w[:, k, m * P:(m + 1) * P], hid[:, k, :],
                                            start=k == 0, stop=k == HT - 1)
                        mm.then_inc(tiles, 1)
                eng.wait_ge(act_done, b * ACTS + 3 * HT)
                for k in range(HT):
                    mm = eng.matmul(c.ps[:, 0, :], w3[:, k, :], H3[:, k, :], start=k == 0, stop=k == HT - 1)
                mm.then_inc(tiles, 1)

        @block.scalar
        def _(eng):
            eng.wait_ge(loaded, 16 * len(pairs))
            with eng.Fori(0, B) as b:
                for m in range(HT):
                    eng.wait_ge(tiles, b * TILES + 2 * m + 1)
                    eng.activation(G[:, m, :], c.ps[:, 2 * m, :], ACT.Silu, scale=s[:, m:m + 1]).then_inc(act_done, 1)
                for layer, out in enumerate((H2, H3)):
                    for m in range(HT):
                        eng.wait_ge(tiles, b * TILES + 2 * HT + layer * HT + m + 1)
                        k = (2 + layer) * HT + m
                        eng.activation(out[:, m, :], c.ps[:, 4 * layer + m, :], ACT.Gelu, scale=s[:, k:k + 1])\
                           .then_inc(act_done, 1)

        @block.vector
        def _(eng):
            eng.sem_inc(dve_done, 1)
            eng.wait_ge(loaded, 16 * len(pairs))
            with eng.Fori(0, B) as b:
                for m in range(HT):
                    eng.wait_ge(tiles, b * TILES + 2 * m + 2)
                    eng.wait_ge(act_done, b * ACTS + m + 1)
                    eng.scalar_tensor_tensor(H1[:, m, :], c.ps[:, 2 * m + 1, :], s[:, HT + m:HT + m + 1], G[:, m, :],
                                             ALU.mult, ALU.mult).then_inc(dve_done, 1)
                eng.wait_ge(tiles, b * TILES + TILES)
                eng.scalar_tensor_tensor(c.R[:, b, :], c.ps[:, 0, :], s[:, 4 * HT:4 * HT + 1], c.X[:, b, PAD:PAD + T],
                                         ALU.mult, ALU.add).then_inc(dve_done, 1)


def hashed_ffn(c):
    d = c.dram
    E, HS = 8, 2
    first = [(r * 11) % E for r in range(E)]
    second = [(r * 11 + 7919) % E for r in range(E)]
    C = T // E
    loaded, tiles, outs = c.sem("hf_loaded"), c.sem("hf_tiles"), c.sem("hf_outs")
    silus, gelus, gated = c.sem("hf_silus"), c.sem("hf_gelus"), c.sem("hf_gated")
    prepared, scaled, chain = c.sem("hf_prepared"), c.sem("hf_scaled"), c.sem("hf_chain")
    with ExitStack() as ctx:
        sw1 = c.sb("hf_sw1", [P, HS * P], ctx)
        sw3 = c.sb("hf_sw3", [P, HS * P], ctx)
        sw2 = c.sb("hf_sw2", [P, HS, P], ctx)
        sw2x2 = c.sb("hf_sw2x2", [P, HS, P], ctx)
        w1 = c.sb("hf_w1", [P, E, P], ctx)
        w2 = c.sb("hf_w2", [P, E, P], ctx)
        bias = c.sb("hf_bias", [P, 2 * HS + 1 + 2 * E], ctx)
        b_out = c.sb("hf_b_out", [P, 3 * E], ctx)
        G = c.sb("hf_G", [P, B, HS, T], ctx)
        SH = c.sb("hf_SH", [P, HS, B, T], ctx)
        EH = c.sb("hf_EH", [P, E, 2, B * C], ctx)
        O = c.sb("hf_O", [P, E, B * C], ctx)
        pairs = [(sw1[:, :], d["hf_sw1"]), (sw3[:, :], d["hf_sw3"]), (sw2[:, :, :], d["hf_sw2"]), (w1[:, :, :], d["hf_w1"]),
                 (w2[:, :, :], d["hf_w2"]), (bias[:, :], d["hf_bias"])]
        SB2, B1, B2 = 2 * HS, 2 * HS + 1, 2 * HS + 1 + E
        block = c.block(ctx)

        def residue(buf, r, pad):
            return buf[:, :, pad + r:pad + r + (C - 1) * E + 1:E]

        @block.sync
        def _(eng):
            load_all(eng, loaded, pairs)

        @block.tensor
        def _(eng):
            eng.wait_ge(loaded, 16 * len(pairs))
            for b in range(B):
                if b >= 2:
                    eng.wait_ge(gated, HS * (b - 1))
                for m in range(HS):
                    for k, w in enumerate((sw1, sw3)):
                        eng.matmul(c.ps[:, 4 * (b % 2) + 2 * m + k, :], w[:, m * P:(m + 1) * P], c.X[:, b, PAD:PAD + T],
                                   start=True, stop=True).then_inc(tiles, 1)
            eng.wait_ge(gated, HS * B)
            for r in range(E):
                for j, e in enumerate((first[r], second[r])):
                    n = 2 * r + j
                    if n >= 8:
                        eng.wait_ge(gelus, n - 7)
                    eng.matmul(c.ps[:, n % 8, 0:B * C], w1[:, e, :], residue(c.X, r, PAD), start=True, stop=True)\
                       .then_inc(tiles, 1)
            eng.wait_ge(prepared, 1)
            eng.wait_ge(gelus, 2 * E)
            for r in range(E):
                eng.matmul(c.ps[:, r, 0:B * C], w2[:, first[r], :], EH[:, r, 0, :], start=True, stop=False)
                eng.matmul(c.ps[:, r, 0:B * C], w2[:, second[r], :], EH[:, r, 1, :], start=False, stop=False)
                for k in range(HS):
                    mm = eng.matmul(c.ps[:, r, 0:B * C], sw2x2[:, k, :], residue(SH[:, k, :, :], r, 0),
                                    start=False, stop=k == HS - 1)
                mm.then_inc(outs, 1)

        @block.scalar
        def _(eng):
            eng.wait_ge(loaded, 16 * len(pairs))
            for b in range(B):
                for m in range(HS):
                    eng.wait_ge(tiles, 4 * b + 2 * m + 1)
                    eng.activation(G[:, b, m, :], c.ps[:, 4 * (b % 2) + 2 * m, :], ACT.Silu,
                                   bias=bias[:, m:m + 1]).then_inc(silus, 1)
            for r in range(E):
                for j, e in enumerate((first[r], second[r])):
                    n = 2 * r + j
                    eng.wait_ge(tiles, 4 * B + n + 1)
                    eng.activation(EH[:, r, j, :], c.ps[:, n % 8, 0:B * C], ACT.Gelu,
                                   bias=bias[:, B1 + e:B1 + e + 1]).then_inc(gelus, 1)
            eng.wait_ge(prepared, 1)
            for r in range(E):
                eng.wait_ge(outs, r + 1)
                eng.activation(O[:, r, :], c.ps[:, r, 0:B * C], ACT.Identity, scale=0.25,
                               bias=b_out[:, 2 * E + r:2 * E + r + 1]).then_inc(scaled, 1)

        @block.vector
        def _(eng):
            eng.wait_ge(loaded, 16 * len(pairs))
            for b in range(B):
                for m in range(HS):
                    eng.wait_ge(tiles, 4 * b + 2 * m + 2)
                    eng.wait_ge(silus, HS * b + m + 1)
                    eng.scalar_tensor_tensor(SH[:, m, b, :], c.ps[:, 4 * (b % 2) + 2 * m + 1, :],
                                             bias[:, HS + m:HS + m + 1], G[:, b, m, :], ALU.add, ALU.mult)\
                       .then_inc(gated, 1)
            for r in range(E):
                eng.tensor_tensor(b_out[:, r:r + 1], bias[:, B2 + first[r]:B2 + first[r] + 1],
                                  bias[:, B2 + second[r]:B2 + second[r] + 1], ALU.add).then_inc(chain, 1)
            eng.tensor_scalar(b_out[:, E:2 * E], bias[:, SB2:SB2 + 1].to_broadcast([P, E]), 0.5, None, ALU.mult).then_inc(chain, 1)
            eng.wait_ge(chain, E + 1)
            eng.scalar_tensor_tensor(b_out[:, 2 * E:3 * E], b_out[:, 0:E], 0.25, b_out[:, E:2 * E],
                                     ALU.mult, ALU.add).then_inc(chain, 1)
            eng.wait_ge(chain, E + 2)
            eng.tensor_scalar(sw2x2[:, :, :], sw2[:, :, :], 2.0, None, ALU.mult).then_inc(prepared, 1)
            for r in range(E):
                eng.wait_ge(scaled, r + 1)
                eng.tensor_tensor(residue(c.R, r, 0), O[:, r, :].rearrange("p (b t) -> p b t", b=B),
                                  residue(c.X, r, PAD), ALU.add)


def lowrank_ffn(c):
    d = c.dram
    RANK = 32
    loaded, merged, weight, tiles = c.sem("lf_loaded"), c.sem("lf_merged"), c.sem("lf_weight"), c.sem("lf_tiles")
    with ExitStack() as ctx:
        W = c.sb("lf_W", [P, P], ctx)
        V = c.sb("lf_V", [RANK, P], ctx)
        C = c.sb("lf_C", [RANK, P], ctx)
        bias = c.sb("lf_b", [P, 1], ctx)
        M = c.sb("lf_M", [P, P], ctx)
        pairs = [(W[:, :], d["lf_W"]), (V[:, :], d["lf_V"]), (C[:, :], d["lf_C"]), (bias[:, :], d["lf_b"])]
        block = c.block(ctx)

        @block.sync
        def _(eng):
            load_all(eng, loaded, pairs)

        @block.tensor
        def _(eng):
            eng.wait_ge(loaded, 16 * len(pairs))
            eng.matmul(c.ps[:, 0, 0:P], V[:, :], C[:, :], start=True, stop=True).then_inc(merged, 1)
            eng.wait_ge(weight, 1)
            for b in range(B):
                eng.matmul(c.ps[:, 1 + b, :], M[:, :], c.X[:, b, PAD:PAD + T], start=True, stop=True).then_inc(tiles, 1)

        @block.vector
        def _(eng):
            eng.wait_ge(loaded, 16 * len(pairs))
            eng.wait_ge(merged, 1)
            eng.tensor_tensor(M[:, :], W[:, :], c.ps[:, 0, 0:P], ALU.add).then_inc(weight, 1)
            for b in range(B):
                eng.wait_ge(tiles, b + 1)
                eng.scalar_tensor_tensor(c.R[:, b, :], c.ps[:, 1 + b, :], bias[:, 0:1], c.X[:, b, PAD:PAD + T],
                                         ALU.add, ALU.add)


def routed_ffn(c):
    d = c.dram
    E, HR, HS = 12, 3, 2
    NT = N // P
    TAU = 1.5
    loaded, logits_done, chain = c.sem("rf_loaded"), c.sem("rf_logits"), c.sem("rf_chain")
    experts_loaded = c.sem("rf_experts_loaded")
    gap, sigmoids = c.sem("rf_gap"), c.sem("rf_sigmoids")
    weights_t, weights_c = c.sem("rf_weights_transposed"), c.sem("rf_weights_copied")
    wide, tiles, outs = c.sem("rf_wide"), c.sem("rf_tiles"), c.sem("rf_outs")
    wide_copied, gelus, weighted, acts, stored = (c.sem("rf_" + n) for n in (
        "wide_copied", "gelus", "weighted", "acts", "residual"))
    with ExitStack() as ctx:
        We1 = c.sb("rf_We1", [P, E, 2 * HR, P], ctx)
        We2 = c.sb("rf_We2", [P, E, HR, P], ctx)
        Ws1 = c.sb("rf_Ws1", [P, 2 * HS, P], ctx)
        Ws2 = c.sb("rf_Ws2", [P, HS, P], ctx)
        Wr = c.sb("rf_Wr", [P, E], ctx)
        br = c.sb("rf_br", [P, E], ctx)
        be2 = c.sb("rf_be2", [P, P], ctx)
        bias = c.sb("rf_bias", [P, E * 2 * HR + 2 * HS + 1], ctx)
        pick = c.sb("rf_pick", [P, E, P], ctx)
        order = c.sb("rf_order", [P, E], ctx)
        logits = c.sb("rf_logits", [P, NT, E], ctx)
        rest = c.sb("rf_rest", [P, NT, E], ctx)
        key = c.sb("rf_key", [P, NT, E], ctx)
        hot = c.sb("rf_hot", [P, 2, NT, E], ctx)
        top = c.sb("rf_top", [P, 2, NT], ctx)
        kmax = c.sb("rf_kmax", [P, 2, NT], ctx)
        part = c.sb("rf_part", [P, 3, NT], ctx)
        weights = c.sb("rf_weights", [P, NT, E], ctx)
        WT = c.sb("rf_WT", [P, B, T], ctx)
        WB = c.sb("rf_WB", [P, 2, T], ctx)
        G = c.sb("rf_G", [P, 2, HR, T], ctx)
        A = c.sb("rf_A", [P, 2, HR, T], ctx)
        pairs = [(Wr[:, :], d["rf_Wr"]), (br[:, :], d["rf_br"]), (order[:, :], d["rf_order"]), (pick[:, :, :], d["rf_pick"]),
                 (be2[:, :], d["rf_be2"]), (bias[:, :], d["rf_bias"]), (Ws1[:, :, :], d["rf_Ws1"]), (Ws2[:, :, :], d["rf_Ws2"])]
        large = [(We1[:, :, :, :], d["rf_We1"]), (We2[:, :, :, :], d["rf_We2"])]
        BS2 = E * 2 * HR + 2 * HS
        with ExitStack() as inner:
            block = c.block(inner)

            @block.sync
            def _(eng):
                load_all(eng, loaded, pairs)
                load_all(eng, experts_loaded, large)

            @block.tensor
            def _(eng):
                eng.wait_ge(loaded, 16 * len(pairs))
                for t in range(NT):
                    b, q = t // (T // P), t % (T // P)
                    mm = eng.matmul(c.ps[:, 0, t * E:(t + 1) * E], c.X[:, b, PAD + q * P:PAD + (q + 1) * P], Wr[:, :],
                                    start=True, stop=True)
                mm.then_inc(logits_done, 1)
                eng.wait_ge(chain, 14)
                for t in range(NT):
                    mm = eng.transpose(c.ps[0:E, 1 + t // 4, (t % 4) * P:(t % 4 + 1) * P], weights[:, t, :], c.ident[:, :])
                    if t % 4 == 3:
                        mm.then_inc(weights_t, 1)

            @block.vector
            def _(eng):
                steps = [0]

                def step(ins):
                    steps[0] += 1
                    ins.then_inc(chain, 1)
                    eng.wait_ge(chain, steps[0])

                def wide_of(x):
                    return x.unsqueeze(2).to_broadcast([P, NT, E])

                def per_expert(x):
                    return x.unsqueeze(1).to_broadcast([P, NT, E])

                eng.wait_ge(loaded, 16 * len(pairs))
                eng.wait_ge(logits_done, 1)
                step(eng.tensor_tensor(logits[:, :, :], c.ps[:, 0, 0:NT * E].rearrange("p (t e) -> p t e", e=E),
                                       per_expert(br[:, :]), ALU.add))
                values = logits
                for k in range(2):
                    step(eng.tensor_reduce(top[:, k, :], values[:, :, :], AXX, ALU.max))
                    step(eng.tensor_tensor(key[:, :, :], values[:, :, :], wide_of(top[:, k, :]), ALU.is_equal))
                    step(eng.tensor_tensor(key[:, :, :], key[:, :, :], per_expert(order[:, :]), ALU.mult))
                    step(eng.tensor_reduce(kmax[:, k, :], key[:, :, :], AXX, ALU.max))
                    step(eng.tensor_tensor(hot[:, k, :, :], key[:, :, :], wide_of(kmax[:, k, :]), ALU.is_equal))
                    if k == 0:
                        step(eng.scalar_tensor_tensor(rest[:, :, :], hot[:, 0, :, :], -3e38, logits[:, :, :], ALU.mult, ALU.add))
                        values = rest
                eng.tensor_tensor(part[:, 0, :], top[:, 1, :], top[:, 0, :], ALU.subtract).then_inc(gap, 1)
                eng.wait_ge(sigmoids, 2)
                step(eng.tensor_tensor(rest[:, :, :], hot[:, 0, :, :], wide_of(part[:, 1, :]), ALU.mult))
                eng.tensor_tensor(key[:, :, :], hot[:, 1, :, :], wide_of(part[:, 2, :]), ALU.mult).then_inc(gap, 1)
                eng.wait_ge(gap, 2)
                step(eng.tensor_tensor(weights[:, :, :], rest[:, :, :], key[:, :, :], ALU.add))
                step(eng.memset(WT[:, :, :], 0.0))
                for b in range(B):
                    eng.wait_ge(weights_t, b + 1)
                    eng.tensor_copy(WT[0:E, b, :], c.ps[0:E, 1 + b, :]).then_inc(weights_c, 1)

            @block.scalar
            def _(eng):
                eng.wait_ge(gap, 1)
                eng.activation(part[:, 1, :], part[:, 0, :], ACT.Sigmoid, scale=-1.0 / TAU).then_inc(sigmoids, 1)
                eng.activation(part[:, 2, :], part[:, 0, :], ACT.Sigmoid, scale=1.0 / TAU).then_inc(sigmoids, 1)

        experts = [(HR, E > 0)] * E + [(HS, False)]
        before = [sum(h for h, _ in experts[:e]) for e in range(E + 2)]
        HB = before[E + 1]
        block = c.block(ctx)

        def w_in(e):
            return (We1[:, e, :, :], We2[:, e, :, :], e * 2 * HR) if e < E else (Ws1[:, :, :], Ws2[:, :, :], E * 2 * HR)

        @block.tensor
        def _(eng):
            eng.wait_ge(experts_loaded, 16 * len(large))
            with eng.Fori(0, B) as b:
                x = c.X[:, b, PAD:PAD + T]

                def second(e):
                    h, w2 = experts[e][0], w_in(e)[1]
                    for m in range(h):
                        eng.wait_ge(acts, b * HB + before[e] + m + 2)
                        mm = eng.matmul(c.ps[:, 7, :], w2[:, m, :], A[:, e % 2, m, :], start=False,
                                        stop=e == E and m == h - 1)
                    mm.then_inc(outs, 1)

                eng.wait_ge(stored, b + 1)
                eng.matmul(c.ps[:, 7, :], be2[:, :], WT[:, b, :], start=True, stop=False)
                for e in range(E + 1):
                    h, _ = experts[e]
                    w1 = w_in(e)[0]
                    if e < E:
                        eng.wait_ge(wide_copied, b * E + e + 1)
                        eng.matmul(c.ps[:, 6, :], pick[:, e, :], WT[:, b, :], start=True, stop=True).then_inc(wide, 1)
                    for m in range(h):
                        seen = before[e - 1] + min(m + 1, experts[e - 1][0]) if e else 0
                        eng.wait_ge(gelus, b * HB + seen + 1)
                        eng.matmul(c.ps[:, m, :], w1[:, h + m, :], x, start=True, stop=True).then_inc(tiles, 1)
                        eng.wait_ge(acts, b * HB + seen + 1)
                        eng.matmul(c.ps[:, 3 + m, :], w1[:, m, :], x, start=True, stop=True).then_inc(tiles, 1)
                    if e:
                        second(e - 1)
                second(E)

        @block.scalar
        def _(eng):
            eng.sem_inc(wide_copied, 1)
            eng.sem_inc(gelus, 1)
            with eng.Fori(0, B) as b:
                for e in range(E + 1):
                    h, _ = experts[e]
                    at = w_in(e)[2]
                    if e < E:
                        eng.wait_ge(wide, b * E + e + 1)
                        if e >= 2:
                            eng.wait_ge(weighted, b * E * HR + (e - 1) * HR)
                        eng.activation(WB[:, e % 2, :], c.ps[:, 6, :], ACT.Copy).then_inc(wide_copied, 1)
                    for m in range(h):
                        eng.wait_ge(tiles, 2 * (b * HB + before[e] + m) + 1)
                        if e >= 2:
                            eng.wait_ge(acts, b * HB + before[e - 2] + m + 2)
                        eng.activation(G[:, e % 2, m, :], c.ps[:, m, :], ACT.Gelu, bias=bias[:, at + h + m:at + h + m + 1])\
                           .then_inc(gelus, 1)

        @block.gpsimd
        def _(eng):
            with eng.Fori(0, B) as b:
                for e in range(E):
                    eng.wait_ge(wide_copied, b * E + e + 2)
                    for m in range(HR):
                        eng.wait_ge(gelus, b * HB + before[e] + m + 2)
                        eng.tensor_tensor(G[:, e % 2, m, :], G[:, e % 2, m, :], WB[:, e % 2, :], ALU.mult).then_inc(weighted, 1)

        @block.vector
        def _(eng):
            eng.sem_inc(acts, 1)
            eng.sem_inc(stored, 1)
            with eng.Fori(0, B) as b:
                for e in range(E + 1):
                    h, _ = experts[e]
                    at = w_in(e)[2]
                    for m in range(h):
                        eng.wait_ge(tiles, 2 * (b * HB + before[e] + m) + 2)
                        if e < E:
                            eng.wait_ge(weighted, b * E * HR + e * HR + m + 1)
                        else:
                            eng.wait_ge(gelus, b * HB + before[e] + m + 2)
                        if e >= 2:
                            eng.wait_ge(outs, b * (E + 1) + e - 1)
                        eng.scalar_tensor_tensor(A[:, e % 2, m, :], c.ps[:, 3 + m, :], bias[:, at + m:at + m + 1],
                                                 G[:, e % 2, m, :], ALU.add, ALU.mult).then_inc(acts, 1)
                eng.wait_ge(outs, (b + 1) * (E + 1))
                eng.scalar_tensor_tensor(c.R[:, b, :], c.ps[:, 7, :], bias[:, BS2:BS2 + 1], c.X[:, b, PAD:PAD + T],
                                         ALU.add, ALU.add).then_inc(stored, 1)


def rwkv_attention(c):
    d = c.dram
    HS = 16
    DEEP = 4
    BEHIND = 3
    loaded, chain = c.sem("rw_loaded"), c.sem("rw_chain")
    pe_done, act_done = c.sem("rw_pe"), c.sem("rw_act")
    vb_ready, kv_ready, scanned, read, summed = (c.sem("rw_" + n) for n in ("vb", "kv", "scanned", "read", "summed"))
    ym, yc, ys, yv, yl, yr, yn, yo = (c.sem("rw_y" + n) for n in "mcsvlrno")
    with ExitStack() as ctx:
        maa = c.sb("rw_maa", [P, 9], ctx)
        w1 = c.sb("rw_w1", [P, P], ctx)
        w2 = c.sb("rw_w2", [P, P], ctx)
        dw1 = c.sb("rw_dw1", [P, 64], ctx)
        dw2 = c.sb("rw_dw2", [64, P], ctx)
        Wrkv = c.sb("rw_Wrkv", [P, 3, P], ctx)
        Wo = c.sb("rw_Wo", [P, P], ctx)
        spread = c.sb("rw_spread", [P, HS, P], ctx)
        gather = c.sb("rw_gather", [P, HS, P], ctx)
        heads = c.sb("rw_heads", [P, P], ctx)
        xx = c.sb("rw_xx", [P, T], ctx)
        xxx = c.sb("rw_xxx", [P, T], ctx)
        m = c.sb("rw_m", [P, T], ctx)
        mix = c.sb("rw_mix", [P, 4, T], ctx)
        rkv = c.sb("rw_rkv", [P, 3, T], ctx)
        wd = c.sb("rw_wd", [P, T], ctx)
        wt = c.sb("rw_wt", [64, T], ctx)
        we = c.sb("rw_we", [P, T], ctx)
        ruk = c.sb("rw_ruk", [P, T], ctx)
        own = c.sb("rw_own", [P, T], ctx)
        kv = c.sb("rw_kv", [P, DEEP, T], ctx)
        S = c.sb("rw_S", [P, DEEP, 1 + T], ctx)
        rS = c.sb("rw_rS", [P, DEEP, T], ctx)
        Y = c.sb("rw_Y", [P, T], ctx)
        Q = c.sb("rw_Q", [P, 2, T], ctx)
        pairs = [(maa[:, :], d["rw_maa"]), (w1[:, :], d["rw_w1"]), (w2[:, :], d["rw_w2"]), (dw1[:, :], d["rw_dw1"]),
                 (dw2[:, :], d["rw_dw2"]), (Wrkv[:, :, :], d["rw_Wrkv"]), (Wo[:, :], d["rw_Wo"]),
                 (spread[:, :, :], d["rw_spread"]), (gather[:, :, :], d["rw_gather"]), (heads[:, :], d["rw_heads"])]
        block = c.block(ctx)
        PES, ACTS, STEPS = 10, 7, 12

        def spread_bank(j):
            return (0, 1, 3, 4)[j % DEEP]

        @block.sync
        def _(eng):
            load_all(eng, loaded, pairs)

        @block.tensor
        def _(eng):
            eng.wait_ge(loaded, 16 * len(pairs))
            with eng.Fori(0, B) as b:
                pe, dv, ac = b * PES, b * STEPS, b * ACTS
                eng.wait_ge(chain, dv + 2)
                eng.matmul(c.ps[:, 7, :], w1[:, :], xxx[:, :], start=True, stop=True).then_inc(pe_done, 1)
                eng.wait_ge(act_done, ac + 1)
                for f in range(4):
                    eng.matmul(c.ps[:, f, :], w2[32 * f:32 * f + 32, :], m[32 * f:32 * f + 32, :], start=True, stop=True)\
                       .then_inc(pe_done, 1)
                eng.wait_ge(chain, dv + 10)
                eng.matmul(c.ps[0:64, 7, :], dw1[:, :], mix[:, 0, :], start=True, stop=True).then_inc(pe_done, 1)
                for n in range(3):
                    mm = eng.matmul(c.ps[:, 4 + n, :], Wrkv[:, n, :], mix[:, 1 + n, :], start=True, stop=True)
                mm.then_inc(pe_done, 1)
                eng.wait_ge(act_done, ac + 2)
                eng.matmul(c.ps[:, 7, :], dw2[:, :], wt[:, :], start=True, stop=True).then_inc(pe_done, 1)
                eng.wait_ge(chain, dv + 11)
                eng.wait_ge(act_done, ac + 4)
                eng.matmul(c.ps[:, 7, :], heads[:, :], ruk[:, :], start=True, stop=True).then_inc(pe_done, 1)
                for j in range(HS + BEHIND):
                    if j < HS:
                        if j >= DEEP:
                            eng.wait_ge(kv_ready, b * HS + j - DEEP + 1)
                        eng.matmul(c.ps[:, spread_bank(j), :], spread[:, j, :], rkv[:, 1, :], start=True, stop=True).then_inc(vb_ready, 1)
                    if j >= BEHIND:
                        k = j - BEHIND
                        eng.wait_ge(read, b * HS + k + 1)
                        eng.matmul(c.ps[:, 2, :], gather[:, k, :], rS[:, k % DEEP, :], start=k == 0, stop=k == HS - 1)\
                           .then_inc(summed, 1)
                eng.wait_ge(yo, 2 * b + 1)
                eng.matmul(c.ps[:, 3, :], c.ones_mean[:, :], Y[:, :], start=True, stop=True).then_inc(ym, 1)
                eng.wait_ge(ys, b + 1)
                eng.matmul(c.ps[:, 4, :], c.ones_mean[:, :], Q[:, 0, :], start=True, stop=True).then_inc(yv, 1)
                eng.wait_ge(yn, 2 * b + 2)
                eng.matmul(c.ps[:, 5, :], Wo[:, :], Y[:, :], start=True, stop=True).then_inc(pe_done, 1)
                eng.wait_ge(yo, 2 * b + 2)

        @block.scalar
        def _(eng):
            eng.wait_ge(loaded, 16 * len(pairs))
            with eng.Fori(0, B) as b:
                pe, dv, ac = b * PES, b * STEPS, b * ACTS
                eng.wait_ge(pe_done, pe + 1)
                eng.activation(m[:, :], c.ps[:, 7, :], ACT.Tanh).then_inc(act_done, 1)
                eng.wait_ge(pe_done, pe + 6)
                eng.activation(wt[:, :], c.ps[0:64, 7, :], ACT.Tanh).then_inc(act_done, 1)
                eng.wait_ge(pe_done, pe + 7)
                for n in range(3):
                    mm = eng.activation(rkv[:, n, :], c.ps[:, 4 + n, :], ACT.Copy)
                mm.then_inc(act_done, 1)
                eng.wait_ge(pe_done, pe + 8)
                eng.activation(we[:, :], c.ps[:, 7, :], ACT.Exp, bias=maa[:, 5:6]).then_inc(act_done, 1)
                eng.wait_ge(act_done, ac + 4)
                eng.activation(wd[:, :], we[:, :], ACT.Exp, scale=-1.0).then_inc(act_done, 1)
                eng.wait_ge(yc, b + 1)
                eng.activation(Q[:, 0, :], xx[:, :], ACT.Square).then_inc(ys, 1)
                eng.wait_ge(yv, b + 1)
                eng.activation(Q[:, 1, :], c.ps[:, 4, :], ACT.Ln, bias=c.eps[:, 0:1]).then_inc(act_done, 1)
                eng.wait_ge(act_done, ac + 6)
                eng.activation(Q[:, 1, :], Q[:, 1, :], ACT.Exp, scale=-0.5).then_inc(act_done, 1)

        @block.gpsimd
        def _(eng):
            with eng.Fori(0, B) as b:
                for j in range(HS):
                    eng.wait_ge(scanned, b * HS + j + 1)
                    if j >= DEEP:
                        eng.wait_ge(summed, b * HS + j - DEEP + 1)
                    eng.tensor_tensor(rS[:, j % DEEP, :], rkv[:, 2, :], S[:, j % DEEP, 0:T], ALU.mult).then_inc(read, 1)

        @block.vector
        def _(eng):
            for n in range(DEEP):
                eng.memset(S[:, n, 0:1], 0.0)
            eng.wait_ge(loaded, 16 * len(pairs))
            with eng.Fori(0, B) as b:
                pe, dv, ac = b * PES, b * STEPS, b * ACTS
                steps = [0]

                def step(ins):
                    steps[0] += 1
                    ins.then_inc(chain, 1)

                def after():
                    eng.wait_ge(chain, dv + steps[0])

                x = c.X[:, b, PAD:PAD + T]
                step(eng.tensor_tensor(xx[:, :], c.X[:, b, PAD - 1:PAD + T - 1], x, ALU.subtract))
                after()
                step(eng.scalar_tensor_tensor(xxx[:, :], xx[:, :], maa[:, 0:1], x, ALU.mult, ALU.add))
                for f in range(4):
                    eng.wait_ge(pe_done, pe + 2 + f)
                    step(eng.scalar_tensor_tensor(mix[:, f, :], c.ps[:, f, :], maa[:, 1 + f:2 + f], xx[:, :], ALU.add, ALU.mult))
                after()
                for f in range(4):
                    step(eng.tensor_tensor(mix[:, f, :], mix[:, f, :], x, ALU.add))
                eng.wait_ge(act_done, ac + 3)
                step(eng.scalar_tensor_tensor(ruk[:, :], rkv[:, 2, :], maa[:, 6:7], rkv[:, 0, :], ALU.mult, ALU.mult))
                eng.wait_ge(act_done, ac + 5)
                eng.wait_ge(pe_done, pe + 9)
                step(eng.tensor_tensor(we[:, :], rkv[:, 1, :], c.ps[:, 7, :], ALU.mult))
                for j in range(HS + 1):
                    if j < HS:
                        eng.wait_ge(vb_ready, b * HS + j + 1)
                        if j >= DEEP:
                            eng.wait_ge(scanned, b * HS + j - DEEP + 1)
                        eng.tensor_tensor(kv[:, j % DEEP, :], rkv[:, 0, :], c.ps[:, spread_bank(j), :], ALU.mult).then_inc(kv_ready, 1)
                    if j >= 1:
                        k = j - 1
                        eng.wait_ge(kv_ready, b * HS + k + 1)
                        if k >= DEEP:
                            eng.wait_ge(read, b * HS + k - DEEP + 1)
                        eng.tensor_tensor_scan(S[:, k % DEEP, 1:], wd[:, :], kv[:, k % DEEP, :], 0.0,
                                               ALU.mult, ALU.add).then_inc(scanned, 1)
                eng.wait_ge(summed, (b + 1) * HS)
                after()
                eng.tensor_tensor(Y[:, :], we[:, :], c.ps[:, 2, :], ALU.add).then_inc(yo, 1)
                eng.wait_ge(ym, b + 1)
                eng.wait_ge(yo, 2 * b + 1)
                eng.tensor_tensor(xx[:, :], Y[:, :], c.ps[:, 3, :], ALU.subtract).then_inc(yc, 1)
                eng.wait_ge(act_done, ac + 7)
                eng.wait_ge(yc, b + 1)
                eng.scalar_tensor_tensor(own[:, :], xx[:, :], maa[:, 7:8], Q[:, 1, :], ALU.mult, ALU.mult).then_inc(yn, 1)
                eng.wait_ge(yn, 2 * b + 1)
                eng.tensor_scalar(Y[:, :], own[:, :], maa[:, 8:9], None, ALU.add).then_inc(yn, 1)
                eng.wait_ge(pe_done, pe + 10)
                eng.tensor_tensor(c.R[:, b, :], x, c.ps[:, 5, :], ALU.add).then_inc(yo, 1)
                assert steps[0] == STEPS


HEADS = 16
DH = P // HEADS
QUAD = 4
GROUPS = HEADS // QUAD
QT = T // P
UNITS = QT * QUAD


def rotary_attention(c):
    d = c.dram
    NW = 4
    TILES = 2
    NPROJ, NMUL, NSIDE = TILES * NW + 1, TILES * NW, TILES * 2
    names = ("loaded", "weights", "projected", "multiplied", "added", "high", "less", "middle", "split", "kept", "values_t",
             "values", "scores", "maxima", "exps", "probs_t", "probs_v", "probs_s", "mixed", "inverted", "wide", "wide_t", "wide_c",
             "taken", "normed", "place", "placed", "added_up")
    s = {n: c.sem("ra_" + n) for n in names}
    with ExitStack() as ctx:
        W = c.sb("ra_W", [P, NPROJ, P], ctx)
        rope = c.sb("ra_rope", [P, NW, T], ctx)
        mask = c.sb("ra_mask", [P, 2, 2], ctx)
        tmp = c.sb("ra_tmp", [P, NMUL, T], ctx)
        F = c.sb("ra_F", [P, NSIDE, T], ctx)
        H = ctx.enter_context(c.nc.sbuf_tensor("ra_H", [P, 2, NSIDE, T], BF16))
        S = ctx.enter_context(c.nc.sbuf_tensor("ra_S", [P, 2, NSIDE, T], BF16))
        VC = c.sb("ra_VC", [P, T], ctx)
        V = c.sb("ra_V", [P, 2, QT, P], ctx)
        bias = c.sb("ra_bias", [P, UNITS], ctx)
        E = c.sb("ra_E", [P, 3, T], ctx)
        PT = c.sb("ra_PT", [P, 2, QUAD, T], ctx)
        total = c.sb("ra_total", [P, UNITS], ctx)
        inverse = c.sb("ra_inverse", [P, UNITS], ctx)
        wide = c.sb("ra_wide", [P, UNITS, 32], ctx)
        IT = c.sb("ra_IT", [P, T], ctx)
        ON = c.sb("ra_ON", [P, T], ctx)
        place = c.sb("ra_place", [P, P], ctx)
        block = c.block(ctx)

        def bank(i):
            return c.ps[:, 6 + i % 2, :]

        def interleaved(units, pieces):
            for u in range(UNITS + 1):
                if u < UNITS:
                    units(u)
                for piece in pieces.get(u, []):
                    piece()

        def merged(one, other):
            return {u: one.get(u, []) + other.get(u, []) for u in {**one, **other}}

        def wide_tile(t):
            return wide[:, t * QUAD:(t + 1) * QUAD, :].rearrange("p h c -> p (h c)")

        def alone(pieces):
            for u in sorted(pieces):
                for piece in pieces[u]:
                    piece()

        def score_bank(b, u):
            return (0, 1, 5)[(b * UNITS + u) % 3]

        def copied(eng, n, u):
            t, h = u // QUAD, u % QUAD
            if h == QUAD - 1:
                eng.wait_ge(s["probs_s"], n * QT + t + 1)
            else:
                eng.wait_ge(s["probs_v"], (n * QT + t) * (QUAD - 1) + h + 1)

        @block.sync
        def _(eng):
            eng.dma_start(mask[:, :, :], d["ra_mask"]).then_inc(s["loaded"], 16)
            eng.dma_start(rope[:, :, :], d["ra_rope"]).then_inc(s["loaded"], 16)
            eng.dma_start(W[:, :, :], d["ra_W"][:, 0, :, :]).then_inc(s["weights"], 16)
            eng.dma_start(place[:, :], d["ra_place"][:, 0, :]).then_inc(s["place"], 16)
            with eng.Fori(0, GROUPS) as g:
                eng.wait_ge(s["projected"], (g + 1) * B * NPROJ)
                eng.dma_start(W[:, :, :], d["ra_W"][:, g + 1, :, :]).then_inc(s["weights"], 16)
                eng.wait_ge(s["placed"], (g + 1) * B)
                eng.dma_start(place[:, :], d["ra_place"][:, g + 1, :]).then_inc(s["place"], 16)
            eng.wait_ge(s["place"], 16 * (GROUPS + 1))

        @block.tensor
        def _(eng):
            def prepare(n, b, first):
                x = c.X[:, b, PAD:PAD + T]

                def project(i):
                    if i == 0 and not first:
                        eng.wait_ge(s["added_up"], n)
                        eng.wait_ge(s["values"], n)
                        eng.wait_ge(s["multiplied"], n * NMUL)
                    if i >= 2:
                        eng.wait_ge(s["multiplied"], n * NMUL + i - 1)
                    eng.matmul(bank(i), W[:, i, :], x, start=True, stop=True).then_inc(s["projected"], 1)

                def transpose_values():
                    eng.wait_ge(s["kept"], n + 1)
                    eng.wait_ge(s["multiplied"], n * NMUL + NMUL)
                    for t in range(QT):
                        mm = eng.transpose(bank(1)[:, t * P:(t + 1) * P], VC[:, t * P:(t + 1) * P], c.ident[:, :])
                    mm.then_inc(s["values_t"], 1)

                pieces = {u: [lambda i=u: project(i)] for u in range(NPROJ)}
                pieces[11] = [transpose_values]
                return pieces

            def divide(n, g):
                def invert():
                    eng.wait_ge(s["wide"], n + 1)
                    eng.wait_ge(s["kept"], n + 2)
                    for t in range(QT):
                        mm = eng.matmul(c.ps[:, 6, t * P:(t + 1) * P], wide_tile(t), c.ident[:, :], start=True, stop=True)
                    mm.then_inc(s["wide_t"], 1)

                def put():
                    eng.wait_ge(s["normed"], n + 1)
                    eng.wait_ge(s["place"], 16 * g + 16)
                    eng.matmul(c.ps[:, 6, :], place[:, :], ON[:, :], start=True, stop=True).then_inc(s["placed"], 1)

                return {10: [invert], 13: [put]}

            def matrix(n, b, u):
                t, h = u // QUAD, u % QUAD
                rows = slice(64 * (h % 2), 64 * (h % 2) + 64)
                side = 2 * (h // 2)
                eng.matmul(c.ps[:, score_bank(b, u), :], S[rows, b % 2, side, t * P:(t + 1) * P], S[rows, b % 2, side + 1, :],
                           start=True, stop=True).then_inc(s["scores"], 1)

            def unit(n, b):
                def first_scores(u):
                    if u == 0:
                        eng.wait_ge(s["split"], (n + 2) * NSIDE)
                        eng.wait_ge(s["exps"], n * UNITS + (UNITS - 2 if b < B - 1 else UNITS))
                    else:
                        eng.wait_ge(s["exps"], n * UNITS + UNITS - 1)
                    matrix(n + 1, (b + 1) % B, u)

                def scores(u):
                    if u >= 3:
                        eng.wait_ge(s["exps"], n * UNITS + u - 2)
                    elif u == 2 and b:
                        eng.wait_ge(s["exps"], n * UNITS)
                    matrix(n, b, u)

                def mix(t):
                    if t == 0:
                        eng.wait_ge(s["taken"], n + 1)
                    copied(eng, n, t * QUAD + QUAD - 2)
                    copied(eng, n, t * QUAD + QUAD - 1)
                    for k in range(QT):
                        for h in range(QUAD):
                            rows = slice(32 * h, 32 * h + 32)
                            mm = eng.matmul(c.ps[rows, 4, t * P:(t + 1) * P], V[:, b % 2, k, rows],
                                            PT[:, t % 2, h, k * P:(k + 1) * P], start=k == 0, stop=k == QT - 1)
                    mm.then_inc(s["mixed"], 1)

                def of(u):
                    if u == 0:
                        eng.wait_ge(s["values"], n + 1)
                    if u + 2 < UNITS:
                        scores(u + 2)
                    else:
                        first_scores(u + 2 - UNITS)
                    eng.wait_ge(s["exps"], n * UNITS + u + 1)
                    if u >= 2:
                        copied(eng, n, u - 2)
                    for k in range(QT):
                        mm = eng.transpose(c.ps[:, 2 + u % 2, k * P:(k + 1) * P], E[:, u % 3, k * P:(k + 1) * P], c.ident[:, :])
                    mm.then_inc(s["probs_t"], 1)
                    if u and u % QUAD == 0:
                        mix(u // QUAD - 1)
                    if u == UNITS - 1:
                        mix(QT - 1)
                return of

            eng.wait_ge(s["weights"], 16)
            alone(prepare(0, 0, True))
            eng.wait_ge(s["split"], NSIDE)
            for u in range(2):
                matrix(0, 0, u)
            with eng.Fori(0, GROUPS) as g:
                for b in range(B):
                    n = g * B + b
                    if b == B - 1:
                        eng.wait_ge(s["weights"], 16 * g + 32)
                    interleaved(unit(n, b), merged(prepare(n + 1, (b + 1) % B, False), divide(n - 1, g) if b else {}))
                alone(divide(n, g))

        @block.scalar
        def _(eng):
            def prepare(n, b):
                def high(j):
                    eng.wait_ge(s["added"], n * NSIDE + j + 1)
                    eng.activation(H[:, 0, j, :], F[:, j, :], ACT.Copy, scale=mask[:, j % 2, 0:1]).then_inc(s["high"], 1)

                def middle(j):
                    eng.wait_ge(s["less"], n * NSIDE + j + 1)
                    eng.activation(H[:, 1, j, :], F[:, j, :], ACT.Copy, scale=mask[:, j % 2, 1:2]).then_inc(s["middle"], 1)

                def keep():
                    eng.wait_ge(s["projected"], (n + 1) * NPROJ)
                    eng.activation(VC[:, :], bank(NPROJ - 1), ACT.Copy).then_inc(s["kept"], 1)

                def values():
                    eng.wait_ge(s["values_t"], n + 1)
                    eng.activation(V[:, b % 2, :, :], bank(1).rearrange("p (t c) -> p t c", t=QT), ACT.Copy).then_inc(s["values"], 1)

                return {4: [lambda: high(0)], 6: [lambda: high(1), lambda: middle(0)], 8: [lambda: high(2), lambda: middle(1)], 9: [keep],
                        10: [lambda: high(3), lambda: middle(2)], 12: [lambda: middle(3)], 14: [values]}

            def unit(n, b):
                def of(u):
                    if u == UNITS:
                        copy(QT - 1)
                        return
                    eng.wait_ge(s["maxima"], n * UNITS + u + 1)
                    if u >= 3:
                        eng.wait_ge(s["probs_t"], n * UNITS + u - 2)
                    eng.activation(E[:, u % 3, :], c.ps[:, score_bank(b, u), :], ACT.Exp, bias=bias[:, u:u + 1],
                                   accum_out=total[:, u:u + 1]).then_inc(s["exps"], 1)
                    if u and u % QUAD == 0:
                        copy(u // QUAD - 1)

                def copy(t):
                    u = t * QUAD + QUAD - 1
                    eng.wait_ge(s["probs_t"], n * UNITS + u + 1)
                    if t >= 2:
                        eng.wait_ge(s["mixed"], n * QT + t - 1)
                    eng.activation(PT[:, t % 2, QUAD - 1, :], c.ps[:, 2 + u % 2, :], ACT.Copy).then_inc(s["probs_s"], 1)
                return of

            def divide(n):
                def keep():
                    eng.wait_ge(s["wide_t"], n + 1)
                    eng.activation(IT[:, :], c.ps[:, 6, :], ACT.Copy).then_inc(s["wide_c"], 1)
                return {11: [keep]}

            eng.wait_ge(s["loaded"], 32)
            alone(prepare(0, 0))
            with eng.Fori(0, GROUPS) as g:
                for b in range(B):
                    n = g * B + b
                    of = unit(n, b)
                    interleaved(of, merged(prepare(n + 1, (b + 1) % B), divide(n - 1) if b else {}))
                    of(UNITS)
                alone(divide(n))

        @block.gpsimd
        def _(eng):
            def prepare(n, b):
                def add(j):
                    eng.wait_ge(s["multiplied"], n * NMUL + 2 * j + 2)
                    eng.tensor_tensor(F[:, j, :], tmp[:, 2 * j, :], tmp[:, 2 * j + 1, :], ALU.add).then_inc(s["added"], 1)

                def less(j):
                    eng.wait_ge(s["high"], n * NSIDE + j + 1)
                    eng.tensor_tensor(F[:, j, :], F[:, j, :], H[:, 0, j, :], ALU.subtract).then_inc(s["less"], 1)

                def last(j):
                    eng.wait_ge(s["middle"], n * NSIDE + j + 1)
                    eng.tensor_tensor(S[:, b % 2, j, :], F[:, j, :], H[:, 1, j, :], ALU.subtract).then_inc(s["split"], 1)

                for j in range(NSIDE + 2):
                    if j < NSIDE:
                        add(j)
                    if 1 <= j <= NSIDE:
                        less(j - 1)
                    if j >= 2:
                        last(j - 2)

            prepare(0, 0)
            with eng.Fori(0, GROUPS) as g:
                for b in range(B):
                    n = g * B + b
                    prepare(n + 1, (b + 1) % B)
                    eng.wait_ge(s["inverted"], n + 1)
                    if b:
                        eng.wait_ge(s["wide_t"], n)
                    eng.sem_inc(c.past, 1)
                    eng.tensor_copy(wide[:, :, :], inverse[:, :].unsqueeze(2).to_broadcast([P, UNITS, 32])).then_inc(s["wide"], 1)

        @block.vector
        def _(eng):
            def prepare(n, b, first):
                def multiply(i):
                    if not first:
                        eng.wait_ge(s["added"], n * NSIDE - NSIDE + i // 2 + 1)
                    eng.wait_ge(s["projected"], n * NPROJ + i + 1)
                    eng.tensor_tensor(tmp[:, i, :], rope[:, i % NW, :], bank(i), ALU.mult).then_inc(s["multiplied"], 1)
                return {i + 1: [lambda i=i: multiply(i)] for i in range(NMUL)}

            def unit(n, b):
                def of(u):
                    if u < UNITS:
                        eng.wait_ge(s["scores"], n * UNITS + u + 1)
                        eng.tensor_reduce(bias[:, u:u + 1], c.ps[:, score_bank(b, u), :], AXX, ALU.max, negate=True).then_inc(s["maxima"], 1)
                    if u and u % QUAD:
                        t, h = (u - 1) // QUAD, (u - 1) % QUAD
                        eng.wait_ge(s["probs_t"], n * UNITS + u)
                        if t >= 2:
                            eng.wait_ge(s["mixed"], n * QT + t - 1)
                        eng.tensor_copy(PT[:, t % 2, h, :], c.ps[:, 2 + (u - 1) % 2, :]).then_inc(s["probs_v"], 1)
                return of

            def divide(n, b):
                def take():
                    eng.wait_ge(s["mixed"], (n + 1) * QT)
                    eng.tensor_copy(ON[:, :], c.ps[:, 4, :]).then_inc(s["taken"], 1)

                def norm():
                    eng.wait_ge(s["wide_c"], n + 1)
                    eng.wait_ge(s["taken"], n + 2)
                    eng.tensor_tensor(ON[:, :], ON[:, :], IT[:, :], ALU.mult).then_inc(s["normed"], 1)

                def add():
                    eng.wait_ge(s["placed"], n + 1)
                    eng.tensor_tensor(c.R[:, b, :], c.R[:, b, :], c.ps[:, 6, :], ALU.add).then_inc(s["added_up"], 1)

                return {1: [take], 12: [norm], 15: [add]}

            eng.sem_inc(s["taken"], 1)
            eng.tensor_copy(c.R[:, :, :], c.X[:, :, PAD:PAD + T]).then_inc(s["added_up"], 1)
            eng.wait_ge(s["added_up"], 1)
            eng.sem_inc(s["added_up"], 1)
            eng.wait_ge(s["loaded"], 32)
            alone(prepare(0, 0, True))
            with eng.Fori(0, GROUPS) as g:
                for b in range(B):
                    n = g * B + b
                    interleaved(unit(n, b), merged(prepare(n + 1, (b + 1) % B, False), divide(n - 1, b - 1) if b else {}))
                    eng.wait_ge(s["exps"], (n + 1) * UNITS)
                    eng.reciprocal(inverse[:, :], total[:, :]).then_inc(s["inverted"], 1)
                alone(divide(n, B - 1))


def relative_attention(c):
    d, nc = c.dram, c.nc
    SPAN, LOW, UP = 64, 192, 64
    BAND = LOW + UP
    ROW = SPAN + BAND
    names = ("loaded", "zeros", "padded", "weights", "tables_ps", "tables", "projected", "kept", "values_t", "qk", "ab",
             "km", "ab_copied", "wrote", "windows", "scores", "complete", "maxima", "exps", "probs_t", "probs_v", "probs_s", "mixed",
             "inverted", "wide", "wide_t", "wide_c", "normed", "place", "placed", "added_up")
    s = {n: c.sem("da_" + n) for n in names}
    scale = (DH * 3) ** -0.5
    Wq, Wk, Wv, Wpk, Wpq = range(5)
    LOW_END, UP_END = range(2)
    scratch = [[nc.dram_tensor(f"da_scratch{i}{j}", (UNITS * P * ROW + SPAN,), F32).ap() for j in range(2)] for i in range(2)]

    def rows_of(buf, offset, row, first, count, width):
        return bass.AP(buf.tensor, buf.offset + offset + first * row, [[row, count], [P * ROW, UNITS], [1, width]])

    with ExitStack() as ctx:
        W = c.sb("da_W", [P, 5, P], ctx)
        place = c.sb("da_place", [P, P], ctx)
        only = c.sb("da_only", [P, 2, QUAD], ctx)
        rel = c.sb("da_rel", [P, 2, P], ctx)
        bias = c.sb("da_bias", [P, GROUPS, 5], ctx)
        bo = c.sb("da_bo", [P, 1], ctx)
        zeros = c.sb("da_zeros", [P, UNITS, SPAN], ctx)
        pk = c.sb("da_pk", [P, P], ctx)
        pq = c.sb("da_pq", [P, P], ctx)
        A_table = c.sb("da_A_table", [P, BAND], ctx)
        B_table = c.sb("da_B_table", [P, BAND], ctx)
        ends = c.sb("da_ends", [P, 5], ctx)
        Q = c.sb("da_Q", [P, 2, 2, QUAD, T], ctx)
        K = c.sb("da_K", [P, 2, 2, T], ctx)
        KA = c.sb("da_KA", [P, QUAD, T], ctx)
        VC = c.sb("da_VC", [P, T], ctx)
        V = c.sb("da_V", [P, 2, QT, P], ctx)
        AB = c.sb("da_AB", [P, UNITS, 2, BAND], ctx)
        window = c.sb("da_window", [P, 2, UNITS, P + 2 * SPAN], ctx)
        diag = c.sb("da_diag", [P, 2, UNITS, P], ctx)
        corner = c.sb("da_corner", [P, 2, UNITS, SPAN], ctx)
        top = c.sb("da_top", [P, UNITS], ctx)
        E = c.sb("da_E", [P, 3, T], ctx)
        PT = c.sb("da_PT", [P, 2, QUAD, T], ctx)
        total = c.sb("da_total", [P, UNITS], ctx)
        inverse = c.sb("da_inverse", [P, UNITS], ctx)
        wide = c.sb("da_wide", [P, UNITS, 32], ctx)
        IT = c.sb("da_IT", [P, T], ctx)
        ON = c.sb("da_ON", [P, T], ctx)
        pairs = [(only[:, :, :], d["da_only"]), (rel[:, :, :], d["da_rel"]), (bias[:, :, :], d["da_bias"]), (bo[:, :], d["da_bo"])]
        COPIES = UNITS + 1
        QKS = 2 * QUAD + 2
        TABLES = 9
        ORDER = [(1, 0), (1, 1), (2, 0), (1, 2), (2, 1), (1, 3), (2, 2), (2, 3)]
        BANDS_BY = [sum(k == 1 for k, _ in ORDER[:ORDER.index((2, b))]) for b in range(B)]
        BANDS_IN = [sum(k == 1 for k, _ in ORDER[:ORDER.index((2, b)) + 2]) for b in range(B)]
        DIVIDED = [sum(k == 2 for k, _ in ORDER[:max(ORDER.index((1, b)) - 1, 0)]) for b in range(B)]
        block = c.block(ctx)

        def phases(bands, scores, divide):
            before = None
            for kind, b in ORDER:
                pieces = divide(before) if before is not None else {}
                (bands if kind == 1 else scores)(b, lambda u: [piece() for piece in pieces.get(u, [])])
                before = b if kind == 2 else None
            for u, pieces in sorted(divide(before).items()):
                for piece in pieces:
                    piece()

        def score_bank(u):
            return (0, 1, 5)[u % 3]

        def wide_tile(t):
            return wide[:, t * QUAD:(t + 1) * QUAD, :].rearrange("p h c -> p (h c)")

        def copied(eng, n, u):
            t, h = u // QUAD, u % QUAD
            eng.wait_ge(s["probs_s" if h % 2 else "probs_v"], (n * QT + t) * (QUAD // 2) + h // 2 + 1)

        @block.sync
        def _(eng):
            load_all(eng, s["loaded"], pairs)
            eng.dma_start(W[:, :, :], d["da_W"][:, 0, :, :]).then_inc(s["weights"], 16)
            eng.dma_start(place[:, :], d["da_place"][:, 0, :]).then_inc(s["place"], 16)
            eng.sem_inc(s["wrote"], 1)
            eng.wait_ge(s["zeros"], 2)
            for pair in scratch:
                for buf in pair:
                    eng.dma_start(rows_of(buf, 0, ROW, 0, P, SPAN), zeros[:, :, :]).then_inc(s["padded"], 16)
                    eng.dma_start(bass.AP(buf.tensor, buf.offset + UNITS * P * ROW, [[SPAN, 1], [1, SPAN]]), zeros[0:1, 0, :])\
                       .then_inc(s["padded"], 16)
            eng.wait_ge(s["padded"], 8 * 16)
            with eng.Fori(0, GROUPS) as g:
                for kind, b in ORDER:
                    if kind == 2:
                        continue
                    n = g * B + b
                    for t in range(QT):
                        eng.wait_ge(s["ab_copied"], n * COPIES + 2 + (t + 1) * QUAD)
                        for side in range(2):
                            buf = scratch[b % 2][side]
                            dst = bass.AP(buf.tensor, buf.offset + t * QUAD * P * ROW + SPAN, [[ROW, P], [P * ROW, QUAD], [1, BAND]])
                            eng.dma_start(dst, AB[:, t * QUAD:(t + 1) * QUAD, side, :]).then_inc(s["wrote"], 16)
                    eng.wait_ge(s["wrote"], (n + 1) * 16 * 2 * QT + 1)
                    A, Bk = scratch[b % 2]
                    par = b % 2
                    for dst, src in (
                            (window[:, par, :, SPAN:SPAN + P], rows_of(A, 2 * SPAN, ROW - 1, 0, P, P)),
                            (window[0:64, par, :, 0:SPAN], rows_of(A, SPAN, ROW - 1, 0, 64, SPAN)),
                            (window[64:128, par, :, SPAN + P:], rows_of(A, SPAN + LOW + 2 * SPAN, ROW - 1, 64, 64, SPAN)),
                            (diag[:, par, :, :], rows_of(Bk, SPAN + UP + P, ROW - 1, 0, P, P)),
                            (corner[0:64, par, :, :], rows_of(Bk, SPAN, ROW - 1, 0, 64, SPAN)),
                            (corner[64:128, par, :, :], rows_of(Bk, SPAN + UP + 2 * P, ROW - 1, 64, 64, SPAN))):
                        eng.dma_start(dst, src).then_inc(s["windows"], 16)
                eng.wait_ge(s["projected"], (g + 1) * B)
                eng.dma_start(W[:, :, :], d["da_W"][:, g + 1, :, :]).then_inc(s["weights"], 16)
                eng.wait_ge(s["placed"], (g + 1) * B)
                eng.dma_start(place[:, :], d["da_place"][:, g + 1, :]).then_inc(s["place"], 16)
            eng.wait_ge(s["weights"], 16 * (GROUPS + 1))
            eng.wait_ge(s["place"], 16 * (GROUPS + 1))

        @block.tensor
        def _(eng):
            eng.wait_ge(s["loaded"], 16 * len(pairs))
            with eng.Fori(0, GROUPS) as g:
                def bands(b, after):
                    n = g * B + b
                    x = c.X[:, b, PAD:PAD + T]
                    eng.wait_ge(s["ab_copied"], n * COPIES + 1)
                    eng.wait_ge(s["qk"], n * QKS + 1)
                    eng.wait_ge(s["added_up"], g * B + DIVIDED[b] + 1)
                    for w in (Wq, Wk, Wv):
                        mm = eng.matmul(c.ps[:, 5 + w, :], W[:, w, :], x, start=True, stop=True)
                    mm.then_inc(s["projected"], 1)
                    eng.wait_ge(s["kept"], n + 1)
                    for t in range(QT):
                        mm = eng.transpose(c.ps[:, 7, t * P:(t + 1) * P], VC[:, t * P:(t + 1) * P], c.ident[:, :])
                    mm.then_inc(s["values_t"], 1)
                    for u in range(UNITS):
                        t, h = u // QUAD, u % QUAD
                        at = slice(t * P, (t + 1) * P)
                        if u < QUAD:
                            eng.wait_ge(s["qk"], n * QKS + 1 + 2 + h + 1)
                            eng.wait_ge(s["km"], n * QUAD + h + 1)
                        if u >= 2:
                            eng.wait_ge(s["ab_copied"], n * COPIES + 1 + u)
                        eng.matmul(c.ps[:, 2 + u % 2, 0:BAND], Q[:, b % 2, LOW_END, h, at], A_table[:, :], start=True, stop=True)
                        eng.matmul(c.ps[:, 2 + u % 2, BAND:2 * BAND], KA[:, h, at], B_table[:, :],
                                   start=True, stop=True).then_inc(s["ab"], 1)
                        after(u)

                def score(b, u):
                    n = g * B + b
                    t, h = u // QUAD, u % QUAD
                    par, ps = b % 2, c.ps[:, score_bank(u), :]
                    lo, hi = c.ps[0:64, score_bank(u), :], c.ps[64:128, score_bank(u), :]
                    at = slice(t * P, (t + 1) * P)
                    if u >= 3:
                        eng.wait_ge(s["exps"], n * UNITS + u - 2)
                    eng.matmul(ps[:, 0:(t + 1) * P], Q[:, par, LOW_END, h, at], K[:, par, LOW_END, 0:(t + 1) * P], start=True, stop=False)
                    if t < QT - 1:
                        eng.matmul(ps[:, (t + 1) * P:], Q[:, par, UP_END, h, at], K[:, par, UP_END, (t + 1) * P:], start=False, stop=False)
                    if t > 0:
                        eng.matmul(lo[:, t * P - SPAN:t * P], corner[:, par, u - QUAD, :], c.ident[:, 64:128], start=False, stop=False)
                    if t < QT - 1:
                        eng.matmul(hi[:, (t + 1) * P:(t + 1) * P + SPAN], corner[:, par, u + QUAD, :], c.ident[:, 0:64],
                                   start=False, stop=False)
                    eng.matmul(ps[:, at], diag[:, par, u, :], c.ident[:, :], start=False, stop=True).then_inc(s["scores"], 1)

                def scores(b, after):
                    n = g * B + b

                    def mix(t):
                        if t == 0:
                            eng.wait_ge(s["normed"], n + 1)
                        copied(eng, n, t * QUAD + QUAD - 2)
                        copied(eng, n, t * QUAD + QUAD - 1)
                        for k in range(QT):
                            for h in range(QUAD):
                                rows = slice(32 * h, 32 * h + 32)
                                mm = eng.matmul(c.ps[rows, 4, t * P:(t + 1) * P], V[:, b % 2, k, rows],
                                                PT[:, t % 2, h, k * P:(k + 1) * P], start=k == 0, stop=k == QT - 1)
                        mm.then_inc(s["mixed"], 1)

                    eng.wait_ge(s["windows"], (n + 1) * 6 * 16)
                    eng.wait_ge(s["ab_copied"], (g * B + BANDS_BY[b]) * COPIES + 1)
                    eng.wait_ge(s["qk"], (g * B + BANDS_BY[b]) * QKS + 1)
                    score(b, 0)
                    score(b, 1)
                    for u in range(UNITS):
                        if u + 2 < UNITS:
                            score(b, u + 2)
                        eng.wait_ge(s["exps"], n * UNITS + u + 1)
                        if u >= 2:
                            copied(eng, n, u - 2)
                        for k in range(QT):
                            mm = eng.transpose(c.ps[:, 2 + u % 2, k * P:(k + 1) * P], E[:, u % 3, k * P:(k + 1) * P], c.ident[:, :])
                        mm.then_inc(s["probs_t"], 1)
                        if u and u % QUAD == 0:
                            mix(u // QUAD - 1)
                        after(u)
                    mix(QT - 1)

                def divide(b):
                    n = g * B + b

                    def invert():
                        eng.wait_ge(s["wide"], n + 1)
                        eng.wait_ge(s["added_up"], n + 1)
                        eng.wait_ge(s["ab_copied"], (g * B + BANDS_IN[b] - 1) * COPIES + 2)
                        for t in range(QT):
                            mm = eng.matmul(c.ps[:, 7, t * P:(t + 1) * P], wide_tile(t), c.ident[:, :], start=True, stop=True)
                        mm.then_inc(s["wide_t"], 1)

                    def put():
                        eng.wait_ge(s["normed"], n + 2)
                        eng.wait_ge(s["place"], 16 * g + 16)
                        eng.matmul(c.ps[:, 7, :], place[:, :], ON[:, :], start=True, stop=True).then_inc(s["placed"], 1)

                    return {1: [invert], 5: [put]}

                eng.wait_ge(s["weights"], 16 * g + 16)
                eng.wait_ge(s["qk"], g * B * QKS + 1)
                eng.matmul(c.ps[:, 5, 0:P], W[:, Wpk, :], rel[:, 0, :], start=True, stop=True)
                eng.matmul(c.ps[:, 6, 0:P], W[:, Wpq, :], rel[:, 1, :], start=True, stop=True).then_inc(s["tables_ps"], 1)
                eng.wait_ge(s["tables"], g * TABLES + TABLES)
                phases(bands, scores, divide)

        @block.scalar
        def _(eng):
            eng.sem_inc(s["ab_copied"], 1)
            eng.wait_ge(s["loaded"], 16 * len(pairs))
            with eng.Fori(0, GROUPS) as g:
                def bands(b, after):
                    n = g * B + b
                    if b == 0:
                        eng.wait_ge(s["tables"], g * TABLES + TABLES)
                    eng.wait_ge(s["projected"], n + 1)
                    eng.activation(VC[:, :], c.ps[:, 5 + Wv, :], ACT.Identity, bias=ends[:, 4:5]).then_inc(s["kept"], 1)
                    eng.wait_ge(s["qk"], n * QKS + 2)
                    for h in range(QUAD):
                        eng.activation(KA[:, h, :], K[:, b % 2, LOW_END, :], ACT.Copy, scale=only[:, 0, h:h + 1]).then_inc(s["km"], 1)
                    eng.wait_ge(s["values_t"], n + 1)
                    eng.activation(V[:, b % 2, :, :], c.ps[:, 7, :].rearrange("p (t c) -> p t c", t=QT), ACT.Copy)\
                       .then_inc(s["ab_copied"], 1)
                    eng.wait_ge(s["wrote"], n * 16 * 2 * QT + 1)
                    for u in range(UNITS):
                        eng.wait_ge(s["ab"], n * UNITS + u + 1)
                        eng.activation(AB[:, u, :, :], c.ps[:, 2 + u % 2, :].rearrange("p (k c) -> p k c", k=2), ACT.Copy)\
                           .then_inc(s["ab_copied"], 1)
                        after(u)

                def scores(b, after):
                    n = g * B + b

                    def copy(u):
                        t, h = u // QUAD, u % QUAD
                        eng.wait_ge(s["probs_t"], n * UNITS + u + 1)
                        if t >= 2:
                            eng.wait_ge(s["mixed"], n * QT + t - 1)
                        eng.activation(PT[:, t % 2, h, :], c.ps[:, 2 + u % 2, :], ACT.Copy).then_inc(s["probs_s"], 1)

                    for u in range(UNITS):
                        eng.wait_ge(s["maxima"], n * UNITS + u + 1)
                        if u >= 3:
                            eng.wait_ge(s["probs_t"], n * UNITS + u - 2)
                        eng.activation(E[:, u % 3, :], c.ps[:, score_bank(u), :], ACT.Exp, bias=top[:, u:u + 1],
                                       accum_out=total[:, u:u + 1]).then_inc(s["exps"], 1)
                        if u and u % 2 == 0:
                            copy(u - 1)
                        after(u)
                    copy(UNITS - 1)

                def divide(b):
                    n = g * B + b

                    def keep():
                        eng.wait_ge(s["wide_t"], n + 2)
                        eng.activation(IT[:, :], c.ps[:, 7, :], ACT.Copy).then_inc(s["wide_c"], 1)
                    return {2: [keep]}

                phases(bands, scores, divide)

        @block.gpsimd
        def _(eng):
            with eng.Fori(0, GROUPS * B) as n:
                eng.wait_ge(s["inverted"], n + 1)
                eng.wait_ge(s["wide_t"], n + 1)
                eng.sem_inc(c.past, 1)
                eng.tensor_copy(wide[:, :, :], inverse[:, :].unsqueeze(2).to_broadcast([P, UNITS, 32])).then_inc(s["wide"], 1)

        @block.vector
        def _(eng):
            eng.memset(zeros[:, :, :], 0.0).then_inc(s["zeros"], 1)
            eng.memset(window[:, :, :, :], 0.0).then_inc(s["zeros"], 1)
            eng.memset(B_table[:, 0:1], 0.0)
            eng.sem_inc(s["normed"], 1)
            eng.sem_inc(s["wide_t"], 1)
            eng.sem_inc(s["qk"], 1)
            eng.wait_ge(s["loaded"], 16 * len(pairs))
            eng.tensor_scalar(c.R[:, :, :], c.X[:, :, PAD:PAD + T], bo[:, 0:1], None, ALU.add).then_inc(s["added_up"], 1)
            eng.wait_ge(s["added_up"], 1)
            with eng.Fori(0, GROUPS) as g:
                def table(ins):
                    ins.then_inc(s["tables"], 1)

                def group_bias(i):
                    return bias[:, bass.ds(g, 1), i]

                eng.wait_ge(s["tables_ps"], g + 1)
                table(eng.tensor_scalar(pk[:, :], c.ps[:, 5, 0:P], group_bias(Wpk), None, ALU.add))
                table(eng.tensor_scalar(pq[:, :], c.ps[:, 6, 0:P], group_bias(Wpq), None, ALU.add))
                eng.wait_ge(s["tables"], g * TABLES + 2)
                pk_low, pk_up, pq_low, pq_up = pk[:, 0:1], pk[:, P - 1:P], pq[:, P - 1:P], pq[:, 0:1]
                table(eng.tensor_scalar(A_table[:, 0:P], pk[:, :], pk_low, None, ALU.subtract))
                table(eng.tensor_scalar(A_table[:, P:LOW], pk_up.to_broadcast([P, LOW - P]), pk_low, None, ALU.subtract))
                table(eng.tensor_scalar(A_table[:, LOW:], pk[:, SPAN:], pk_up, None, ALU.subtract))
                table(eng.tensor_scalar(B_table[:, 1:UP], pq[:, 0:UP - 1], pq_up, scale, ALU.subtract, ALU.mult))
                table(eng.tensor_scalar(B_table[:, UP:2 * UP + 1], pq_up.to_broadcast([P, UP + 1]), pq_low, scale,
                                        ALU.subtract, ALU.mult))
                table(eng.tensor_scalar(B_table[:, 2 * UP + 1:], pq[:, 0:P - 1], pq_low, scale, ALU.subtract, ALU.mult))
                for i, (w, end) in enumerate(((Wq, pq_low), (Wq, pq_up), (Wk, pk_low), (Wk, pk_up))):
                    eng.tensor_tensor(ends[:, i:i + 1], group_bias(w), end, ALU.add)
                table(eng.tensor_copy(ends[:, 4:5], group_bias(Wv)))
                eng.wait_ge(s["tables"], g * TABLES + TABLES)

                def bands(b, after):
                    n = g * B + b
                    eng.wait_ge(s["projected"], n + 1)

                    def queries(end):
                        for h in range(QUAD):
                            eng.tensor_scalar(Q[:, b % 2, end, h, :], c.ps[:, 5 + Wq, :], ends[:, end:end + 1], only[:, 1, h:h + 1],
                                              ALU.add, ALU.mult).then_inc(s["qk"], 1)

                    for end in (LOW_END, UP_END):
                        eng.tensor_scalar(K[:, b % 2, end, :], c.ps[:, 5 + Wk, :], ends[:, 2 + end:3 + end], None, ALU.add)\
                           .then_inc(s["qk"], 1)
                    queries(LOW_END)
                    queries(UP_END)
                    for u in range(UNITS):
                        after(u)

                def scores(b, after):
                    n = g * B + b
                    for u in range(UNITS + 1):
                        if u < UNITS:
                            t, bank = u // QUAD, c.ps[:, score_bank(u), :]
                            first, last = max(t * P - SPAN, 0), min(t * P + P + SPAN, T)
                            skip = first - (t * P - SPAN)
                            eng.wait_ge(s["scores"], n * UNITS + u + 1)
                            eng.tensor_tensor(bank[:, first:last], bank[:, first:last],
                                              window[:, b % 2, u, skip:skip + last - first], ALU.add).then_inc(s["complete"], 1)
                            eng.wait_ge(s["complete"], n * UNITS + u + 1)
                            eng.tensor_reduce(top[:, u:u + 1], bank, AXX, ALU.max, negate=True).then_inc(s["maxima"], 1)
                        if u % 2:
                            t, h = (u - 1) // QUAD, (u - 1) % QUAD
                            eng.wait_ge(s["probs_t"], n * UNITS + u)
                            if t >= 2:
                                eng.wait_ge(s["mixed"], n * QT + t - 1)
                            eng.tensor_copy(PT[:, t % 2, h, :], c.ps[:, 2 + (u - 1) % 2, :]).then_inc(s["probs_v"], 1)
                        after(u)
                    eng.wait_ge(s["exps"], (n + 1) * UNITS)
                    eng.reciprocal(inverse[:, :], total[:, :]).then_inc(s["inverted"], 1)

                def divide(b):
                    n = g * B + b

                    def norm():
                        eng.wait_ge(s["wide_c"], n + 1)
                        eng.wait_ge(s["mixed"], (n + 1) * QT)
                        eng.tensor_tensor(ON[:, :], c.ps[:, 4, :], IT[:, :], ALU.mult).then_inc(s["normed"], 1)

                    def add():
                        eng.wait_ge(s["placed"], n + 1)
                        eng.tensor_tensor(c.R[:, b, :], c.R[:, b, :], c.ps[:, 7, :], ALU.add).then_inc(s["added_up"], 1)

                    return {3: [norm], 7: [add]}

                phases(bands, scores, divide)


def delta_attention(c):
    d = c.dram
    CH = 32
    NC = T // CH
    M = 8
    NP = B * M
    DK = 64
    X2 = 2 * CH
    TAPS = PAD + 1
    I = 32
    ID = 24
    GR, GP = 8, NP // 8
    BEHIND = 3
    names = ("loaded", "staged", "prepared", "beta_ps", "beta", "proj", "evac", "kq", "d0", "g", "gt", "chain",
             "handled", "y", "yt", "pool_chain", "dve_done", "o", "w", "pd", "t", "wc", "ktc", "upd", "decayed",
             "state", "kc", "centred", "gate_ps", "squared", "gate", "var", "log", "rstd", "pool_out", "normed", "wo",
             "wo_copied")
    s = {n: c.sem("dl_" + n) for n in names}
    with ExitStack() as ctx:
        taps = [c.sb(f"dl_taps_{n}", [P, TAPS, M * P], ctx) for n in "kqv"]
        Wa = c.sb("dl_Wa", [P, M * P], ctx)
        Wg = c.sb("dl_Wg", [P, M * P], ctx)
        Wo = c.sb("dl_Wo", [P, M, P], ctx)
        Wb = c.sb("dl_Wb", [P, B, P], ctx)
        vec = c.sb("dl_vec", [P, 4 * M + 3], ctx)
        sums = c.sb("dl_sums", [P, 3, P], ctx)
        eye = c.sb("dl_eye", [P, DK], ctx)
        beta = c.sb("dl_beta", [P, T + CH], ctx)
        bc = c.sb("dl_bc", [P, 2, CH], ctx)
        kkN = c.sb("dl_kkN", [P, NP, 2, CH], ctx)
        kqN = c.sb("dl_kqN", [P, NP, CH, 2], ctx)
        vN = c.sb("dl_vN", [P, NP, CH], ctx)
        aN = c.sb("dl_aN", [P, NP, CH], ctx)
        kc = c.sb("dl_kc", [P, NP, CH], ctx)
        d0 = c.sb("dl_d0", [P, NP, CH], ctx)
        d1 = c.sb("dl_d1", [P, NP, CH], ctx)
        F = c.sb("dl_F", [P, NP, CH], ctx)
        whole = c.sb("dl_whole", [P, NP], ctx)
        Pd = c.sb("dl_Pd", [P, NP, DK], ctx)
        aT = c.sb("dl_aT", [P, CH, I], ctx)
        bv = c.sb("dl_bv", [P, CH, I], ctx)
        G = c.sb("dl_G", [P, X2, CH], ctx)
        Y = c.sb("dl_Y", [P, X2, I], ctx)
        tmp = c.sb("dl_tmp", [P, X2, I], ctx)
        U = c.sb("dl_U", [P, CH, I], ctx)
        UT = tmp[:, CH:, :]
        W = c.sb("dl_W", [P, NP, CH], ctx)
        WT = c.sb("dl_WT", [CH, 2, GP * P], ctx)
        KT = c.sb("dl_KT", [CH, 2, GP * P], ctx)
        ST = c.sb("dl_ST", [P, NP, DK], ctx)
        O = c.sb("dl_O", [P, CH, NP], ctx)
        D = c.sb("dl_D", [P, CH, NP], ctx)
        Q = c.sb("dl_Q", [P, CH * NP], ctx)
        gate = c.sb("dl_gate", [P, CH, NP], ctx)
        back = c.sb("dl_back", [P, B, CH], ctx)
        BB, LW, LB = 4 * M, 4 * M + 1, 4 * M + 2
        pairs = [(taps[i][:, :, :], d["dl_cw"][:, i]) for i in range(3)] + [
            (Wa[:, :], d["dl_Wa"]), (Wg[:, :], d["dl_Wg"]), (Wo[:, :, :], d["dl_Wo"]), (Wb[:, :, :], d["dl_Wb"]),
            (vec[:, :], d["dl_vec"]), (sums[:, :, :], d["dl_sums"]), (eye[:, :], d["dl_eye"])]
        flat = (tmp[:, :, :].rearrange("p x i -> p (x i)"), Y[:, :, :].rearrange("p x i -> p (x i)"))
        plain = [flat[0][:, 0:M * P], flat[0][:, M * P:2 * M * P], flat[1][:, 0:M * P]]
        PROJ = 8
        K, QQ, V, A = range(4)
        ps = c.ps
        state_ps = ps[:, 2:6, :].rearrange("p k (n x) -> p (k n) x", x=X2)
        block = c.block(ctx)

        def chunk_of(buf, n, first=0):
            return buf[:, :, bass.ds(n * CH + first, CH)] if not isinstance(n, int) else buf[:, :, n * CH + first:n * CH + first + CH]


        @block.sync
        def _(eng):
            load_all(eng, s["loaded"], pairs)
            for dst, name in zip(plain, "kqv"):
                eng.dma_start(dst, d[f"dl_W{name}"]).then_inc(s["staged"], 16)

        @block.tensor
        def _(eng):
            def project(n, first):
                if not first:
                    eng.wait_ge(s["handled"], n)
                for i in range(PROJ):
                    if i >= 2 or not first:
                        eng.wait_ge(s["evac"], n * PROJ + i - 1)
                    w, half = i // 2, i % 2
                    for m in range(4 * half, 4 * half + 4):
                        out = ps[:, i % 2, (m % 4) * P:(m % 4 + 1) * P]
                        cols = slice(m * P, (m + 1) * P)
                        if w == A:
                            mm = eng.matmul(out, Wa[:, cols], chunk_of(c.X, n, PAD), start=True, stop=True)
                        else:
                            for tap in range(TAPS):
                                mm = eng.matmul(out, taps[w][:, tap, cols], chunk_of(c.X, n, tap),
                                                start=tap == 0, stop=tap == TAPS - 1)
                    mm.then_inc(s["proj"], 1)

            def products_of_keys(n, first):
                eng.wait_ge(s["kq"], 2 * n + 2)
                if not first:
                    eng.wait_ge(s["yt"], n)
                eng.sem_inc(c.past, 1)
                for pair in range(NP):
                    for h in range(2):
                        rows = slice(DK * h, DK * h + DK)
                        mm = eng.matmul(state_ps[rows, pair, :], kkN[rows, pair, :, :].rearrange("p k t -> p (k t)"), kqN[rows, pair, :, :].rearrange("p t k -> p (t k)"),
                                        start=True, stop=True)
                mm.then_inc(s["g"], 1)

            def start(n, g, first):
                if not first:
                    eng.wait_ge(s["state"], GR * (n - 1) + g + 1)
                if g == 0:
                    eng.wait_ge(s["gt"], n + 1)
                eng.sem_inc(c.past, 1)
                for pair in range(g * GP, (g + 1) * GP):
                    for h in range(2):
                        rows = slice(DK * h, DK * h + DK)
                        mm = eng.matmul(state_ps[rows, pair, :], ST[rows, pair, :], kqN[rows, pair, :, :].rearrange("p t k -> p (t k)"),
                                        start=True, stop=True)
                mm.then_inc(s["y"], 1)

            def end(n):
                def update(g):
                    at = GR * n + g + 1
                    eng.wait_ge(s["wc"], at)
                    eng.wait_ge(s["ktc"], at)
                    if g >= 2:
                        eng.wait_ge(s["state"], at - 2)
                    bank = ps[:, 6 + g % 2, :]
                    eng.matmul(bank[:, GP * DK:2 * GP * DK], sums[:, 0, :],
                               Pd[:, g * GP:(g + 1) * GP, :].rearrange("p n i -> p (n i)"), start=True, stop=True)
                    for j in range(GP):
                        for h in range(2):
                            cols = slice(j * P + DK * h, j * P + DK * h + DK)
                            mm = eng.matmul(bank[DK * h:DK * h + DK, j * DK:(j + 1) * DK], KT[:, g % 2, cols], WT[:, g % 2, cols],
                                            start=True, stop=True)
                    mm.then_inc(s["upd"], 1)

                eng.wait_ge(s["pd"], n + 1)
                eng.wait_ge(s["kc"], n + 1)
                eng.wait_ge(s["w"], n + 1)
                eng.wait_ge(s["evac"], (n + 2) * PROJ)
                for g in range(GR):
                    if g:
                        eng.wait_ge(s["wc"], GR * n + g)
                        eng.wait_ge(s["ktc"], GR * n + g)
                    for bank, src in ((0, W), (1, kc)):
                        for j in range(GP):
                            mm = eng.transpose(ps[0:CH, bank, j * P:(j + 1) * P], src[:, g * GP + j, :], c.ident[:, :])
                    mm.then_inc(s["t"], 1)
                    if g:
                        update(g - 1)
                    if g >= BEHIND:
                        start(n + 1, g - BEHIND, False)
                update(GR - 1)
                for g in range(GR - BEHIND, GR):
                    start(n + 1, g, False)

            def output(n):
                eng.wait_ge(s["o"], n + 1)
                Of = O[:, :, :].rearrange("p t n -> p (t n)")
                for k in range(2):
                    mm = eng.matmul(ps[:, k, :], sums[:, 2, :], Of[:, k * 512:(k + 1) * 512], start=True, stop=True)
                mm.then_inc(s["centred"], 1)
                for m in range(M):
                    mm = eng.matmul(ps[:, 6 + m // 4, (m % 4) * P:(m % 4 + 1) * P], Wg[:, m * P:(m + 1) * P], chunk_of(c.X, n, PAD),
                                    start=True, stop=True)
                mm.then_inc(s["gate_ps"], 1)
                eng.wait_ge(s["squared"], n + 1)
                eng.wait_ge(s["gate"], n + 1)
                for k in range(2):
                    mm = eng.matmul(ps[:, 6 + k, :], sums[:, 1, :], Q[:, k * 512:(k + 1) * 512], start=True, stop=True)
                mm.then_inc(s["var"], 1)
                eng.wait_ge(s["normed"], n + 1)
                Dv = D[:, :, :].rearrange("p t (b m) -> p m b t", m=M)
                for m in range(M):
                    mm = eng.matmul(ps[:, 0, 0:P], Wo[:, m, :], Dv[:, m, :, :], start=m == 0, stop=m == M - 1)
                mm.then_inc(s["wo"], 1)
                eng.wait_ge(s["wo_copied"], n + 1)

            def one_pass(n, first):
                if not first:
                    output(n - 1)
                project(n + 1, False)
                products_of_keys(n + 1, False)
                end(n)

            eng.wait_ge(s["loaded"], 16 * len(pairs))
            for b in range(B):
                mm = eng.matmul(ps[:, 7, :], Wb[:, b, :], c.X[:, b, PAD:PAD + T], start=b == 0, stop=b == B - 1)
            mm.then_inc(s["beta_ps"], 1)
            eng.wait_ge(s["prepared"], 4)
            project(0, True)
            products_of_keys(0, True)
            for g in range(GR):
                start(0, g, True)
            one_pass(0, True)
            with eng.Fori(1, NC) as n:
                one_pass(n, False)
            output(NC - 1)

        @block.scalar
        def _(eng):
            def project(n, first):
                if not first:
                    eng.wait_ge(s["y"], GR * n)
                    eng.wait_ge(s["handled"], n)
                    eng.wait_ge(s["kc"], n)
                for i in range(PROJ):
                    w, half = i // 2, i % 2
                    eng.wait_ge(s["proj"], n * PROJ + i + 1)
                    dst = (kkN[:, :, 0, :], kqN[:, :, :, 1], vN[:, :, :], aN[:, :, :])[w]
                    for m in range(4 * half, 4 * half + 4):
                        ins = eng.activation(dst[:, m:NP:M, :], ps[:, i % 2, (m % 4) * P:(m % 4 + 1) * P].rearrange("p (b t) -> p b t", b=B),
                                             ACT.Sigmoid if w == A else ACT.Silu, bias=vec[:, w * M + m:w * M + m + 1])
                    ins.then_inc(s["evac"], 1)
                    if w == QQ and half == 1:
                        eng.wait_ge(s["evac"], n * PROJ + i + 1)
                        raw, scale = kkN[:, :, 0, :], float(DK) ** -0.5
                        eng.activation(kqN[:, :, :, 0], raw, ACT.Copy, scale=scale)
                        eng.activation(kkN[:, :, 1, :], raw, ACT.Copy, scale=scale).then_inc(s["kq"], 1)
                        eng.wait_ge(s["kq"], 2 * n + 1)
                        eng.activation(raw, raw, ACT.Copy, scale=scale).then_inc(s["kq"], 1)
                eng.wait_ge(s["evac"], (n + 1) * PROJ)
                eng.activation(d0[:, :, 0:CH - 1], aN[:, :, 1:CH], ACT.Copy).then_inc(s["d0"], 1)

            def keep_keys(n):
                eng.wait_ge(s["kq"], 2 * n + 2)
                eng.activation(kc[:, :, :], kqN[:, :, :, 0], ACT.Copy).then_inc(s["kc"], 1)

            def end(n):
                for g in range(GR):
                    at = GR * n + g + 1
                    eng.wait_ge(s["t"], at)
                    if g >= 2:
                        eng.wait_ge(s["upd"], at - 2)
                    eng.activation(WT[:, g % 2, :], ps[0:CH, 0, :], ACT.Copy).then_inc(s["wc"], 1)
                    eng.activation(KT[:, g % 2, :], ps[0:CH, 1, :], ACT.Copy).then_inc(s["ktc"], 1)
                keep_keys(n + 1)

            def output(n):
                eng.wait_ge(s["centred"], n + 1)
                Df = D[:, :, :].rearrange("p t n -> p (t n)")
                for k in range(2):
                    eng.activation(Df[:, k * 512:(k + 1) * 512], ps[:, k, :], ACT.Copy)
                for k in range(2):
                    ins = eng.activation(Q[:, k * 512:(k + 1) * 512], ps[:, k, :], ACT.Square)
                ins.then_inc(s["squared"], 1)
                eng.wait_ge(s["gate_ps"], n + 1)
                gv = gate[:, :, :].rearrange("p t (b m) -> p m b t", m=M)
                for m in range(M):
                    ins = eng.activation(gv[:, m, :, :], ps[:, 6 + m // 4, (m % 4) * P:(m % 4 + 1) * P].rearrange("p (b t) -> p b t", b=B),
                                         ACT.Sigmoid)
                ins.then_inc(s["gate"], 1)
                eng.wait_ge(s["var"], n + 1)
                for k in range(2):
                    ins = eng.activation(Q[:, k * 512:(k + 1) * 512], ps[:, 6 + k, :], ACT.Ln, bias=c.eps[:, 0:1])
                ins.then_inc(s["log"], 1)
                eng.wait_ge(s["log"], n + 1)
                eng.activation(Q[:, :], Q[:, :], ACT.Exp, scale=-0.5).then_inc(s["rstd"], 1)
                eng.wait_ge(s["wo"], n + 1)
                eng.activation(back[:, :, :], ps[:, 0, 0:P].rearrange("p (b t) -> p b t", b=B), ACT.Copy).then_inc(s["wo_copied"], 1)

            def one_pass(n, first):
                if not first:
                    output(n - 1)
                project(n + 1, False)
                end(n)

            eng.wait_ge(s["loaded"], 16 * len(pairs))
            eng.wait_ge(s["prepared"], 4)
            eng.wait_ge(s["beta_ps"], 1)
            eng.activation(beta[:, 0:T], ps[:, 7, :], ACT.Sigmoid, bias=vec[:, BB:BB + 1]).then_inc(s["beta"], 1)
            project(0, True)
            keep_keys(0)
            one_pass(0, True)
            with eng.Fori(1, NC) as n:
                one_pass(n, False)
            output(NC - 1)

        def steps(eng, lo, hi, chain, base, fused, midway):
            count = [0]

            def link(ins):
                count[0] += 1
                ins.then_inc(chain, 1)

            def before(k=0):
                eng.wait_ge(chain, base + count[0] - k)

            n = hi - lo
            for t in range(CH):
                rest = X2 - 1 - 2 * t
                if t:
                    before()
                if fused:
                    link(eng.scalar_tensor_tensor(U[:, t, lo:hi], Y[:, 2 * t, lo:hi], bc[:, 1, t:t + 1], bv[:, t, lo:hi], ALU.mult, ALU.add))
                else:
                    link(eng.tensor_tensor(U[:, t, lo:hi], Y[:, 2 * t, lo:hi], bc[:, 1, t:t + 1].to_broadcast([P, n]), ALU.mult))
                    before()
                    link(eng.tensor_tensor(U[:, t, lo:hi], U[:, t, lo:hi], bv[:, t, lo:hi], ALU.add))
                y = Y[:, 2 * t + 1:, lo:hi]
                link(eng.tensor_tensor(y, y, aT[:, t, lo:hi].unsqueeze(1).to_broadcast([P, rest, n]), ALU.mult))
                before(1)
                link(eng.tensor_tensor(tmp[:, 2 * t + 1:, lo:hi], G[:, 2 * t + 1:, t].unsqueeze(2).to_broadcast([P, rest, n]),
                                       U[:, t, lo:hi].unsqueeze(1).to_broadcast([P, rest, n]), ALU.mult))
                before()
                link(eng.tensor_tensor(y, y, tmp[:, 2 * t + 1:, lo:hi], ALU.add))
                if t in midway:
                    midway[t]()
            return count[0]

        POOL_LINKS, DVE_LINKS = 5 * CH, 4 * CH

        @block.gpsimd
        def _(eng):
            def diagonal(n, first):
                eng.wait_ge(s["handled"], n + 1)
                if not first:
                    eng.wait_ge(s["upd"], GR * n)
                eng.tensor_tensor(Pd[:, :, :], whole[:, :].unsqueeze(2).to_broadcast([P, NP, DK]),
                                  eye[:, :].unsqueeze(1).to_broadcast([P, NP, DK]), ALU.mult).then_inc(s["pd"], 1)

            def norm(n):
                eng.wait_ge(s["rstd"], n + 1)
                Df = D[:, :, :].rearrange("p t n -> p (t n)")
                at = 3 * n
                eng.tensor_tensor(Df, Df, Q[:, :], ALU.mult).then_inc(s["pool_out"], 1)
                eng.wait_ge(s["pool_out"], at + 1)
                eng.sem_inc(c.past, 1)
                eng.tensor_scalar(Df, Df, vec[:, LW:LW + 1], vec[:, LB:LB + 1], ALU.mult, ALU.add).then_inc(s["pool_out"], 1)
                eng.wait_ge(s["pool_out"], at + 2)
                eng.tensor_tensor(D[:, :, :], D[:, :, :], gate[:, :, :], ALU.mult).then_inc(s["normed"], 1)

            def residual(n):
                eng.wait_ge(s["wo_copied"], n + 1)
                eng.tensor_tensor(chunk_of(c.R, n), chunk_of(c.X, n, PAD), back[:, :, :], ALU.add).then_inc(s["pool_out"], 1)

            def one_pass(n, first):
                eng.wait_ge(s["yt"], n + 1)
                midway = {3: lambda: diagonal(n, first)}
                if not first:
                    midway |= {6: lambda: norm(n - 1), 14: lambda: residual(n - 1)}
                assert steps(eng, ID, I, s["pool_chain"], n * POOL_LINKS, False, midway) == POOL_LINKS

            eng.wait_ge(s["loaded"], 16 * len(pairs))
            one_pass(0, True)
            with eng.Fori(1, NC) as n:
                one_pass(n, False)
            norm(NC - 1)
            residual(NC - 1)

        @block.vector
        def _(eng):
            HANDLES = 3

            def handle(n):
                at = HANDLES * n
                vT = tmp[:, 0:CH, :]

                def products():
                    eng.tensor_copy(bc[:, 0, :], beta_chunk(n))
                    eng.tensor_scalar(bc[:, 1, :], beta_chunk(n), -1.0, None, ALU.mult).then_inc(s["chain"], 1)
                    eng.wait_ge(s["g"], n + 1)
                    eng.transpose(G[:, :, :], state_ps.rearrange("p n x -> p x n")).then_inc(s["gt"], 1)

                def values():
                    eng.wait_ge(s["evac"], (n + 1) * PROJ)
                    eng.transpose(vT, vN[:, :, :].rearrange("p n t -> p t n")).then_inc(s["chain"], 1)

                def decays():
                    eng.transpose(aT[:, :, :], aN[:, :, :].rearrange("p n t -> p t n"))

                def scaled_values():
                    eng.wait_ge(s["chain"], at + 2)
                    eng.tensor_tensor(bv[:, :, :], vT, bc[:, 0, :].unsqueeze(2).to_broadcast([P, CH, I]), ALU.mult)

                def to_the_end():
                    eng.wait_ge(s["d0"], n + 1)
                    eng.tensor_tensor_scan(F[:, :, :].rearrange("p n t -> p (n t)")[:, ::-1], d0[:, :, :].rearrange("p n t -> p (n t)")[:, ::-1],
                                           d1[:, :, :].rearrange("p n t -> p (n t)")[:, ::-1], 0.0, ALU.mult, ALU.add).then_inc(s["chain"], 1)

                def whole_decay():
                    eng.wait_ge(s["chain"], at + 3)
                    eng.tensor_tensor(whole[:, :], F[:, :, 0], aN[:, :, 0], ALU.mult).then_inc(s["handled"], 1)

                return [products, values, decays, scaled_values, to_the_end, whole_decay]

            def beta_chunk(n):
                return beta[:, n * CH:(n + 1) * CH] if isinstance(n, int) else beta[:, bass.ds(n * CH, CH)]

            def start(n):
                eng.wait_ge(s["y"], GR * (n + 1))
                eng.transpose(Y[:, :, :], state_ps.rearrange("p n x -> p x n")).then_inc(s["yt"], 1)

            def end(n, first):
                eng.wait_ge(s["pool_chain"], (n + 1) * POOL_LINKS)
                eng.wait_ge(s["dve_done"], (n + 1) * DVE_LINKS)
                eng.transpose(UT, U[:, :, :]).then_inc(s["decayed"], 1)
                eng.wait_ge(s["decayed"], (n + 1) * (GR + 1) - GR)
                eng.tensor_tensor(W[:, :, :], UT.rearrange("p t n -> p n t"), F[:, :, :], ALU.mult).then_inc(s["w"], 1)

                def outputs():
                    if not first:
                        eng.wait_ge(s["centred"], n)
                    eng.transpose(O[:, :, :], Y[:, 1::2, :]).then_inc(s["o"], 1)

                pieces = handle(n + 1)
                pieces.insert(1, outputs)

                def update(g):
                    at = GR * n + g + 1
                    eng.wait_ge(s["upd"], at)
                    mine = ST[:, g * GP:(g + 1) * GP, :]
                    bank = ps[:, 6 + g % 2, :].rearrange("p (k n i) -> p k n i", k=2, i=DK)
                    eng.tensor_tensor(mine, mine, bank[:, 1, :, :], ALU.mult).then_inc(s["decayed"], 1)
                    eng.wait_ge(s["decayed"], (n + 1) * (GR + 1) - GR + g + 1)
                    eng.tensor_tensor(mine, mine, bank[:, 0, :, :], ALU.add).then_inc(s["state"], 1)

                for g in range(GR):
                    if g:
                        update(g - 1)
                    if g < len(pieces):
                        pieces[g]()
                update(GR - 1)

            def one_pass(n, first):
                assert steps(eng, 0, ID, s["dve_done"], n * DVE_LINKS, True, {}) == DVE_LINKS
                end(n, first)
                start(n + 1)

            for i in range(3):
                eng.wait_ge(s["loaded"], 16 * len(pairs))
                eng.wait_ge(s["staged"], 16 * 3)
                eng.tensor_tensor(taps[i][:, :, :], taps[i][:, :, :], plain[i].unsqueeze(1).to_broadcast([P, TAPS, M * P]), ALU.mult)\
                   .then_inc(s["prepared"], 1)
            eng.memset(ST[:, :, :], 0.0)
            eng.memset(beta[:, T:], 0.0)
            eng.memset(d0[:, :, CH - 1:], 0.0)
            eng.memset(d1[:, :, 0:CH - 1], 0.0)
            eng.memset(d1[:, :, CH - 1:], 1.0).then_inc(s["prepared"], 1)
            eng.wait_ge(s["prepared"], 4)
            eng.wait_ge(s["beta"], 1)
            for piece in handle(0):
                piece()
            start(0)
            eng.wait_ge(s["yt"], 1)
            one_pass(0, True)
            with eng.Fori(1, NC) as n:
                eng.wait_ge(s["yt"], n + 1)
                one_pass(n, False)


LAYERS = [delta_attention, ternary_ffn, relative_attention, hashed_ffn, rwkv_attention, lowrank_ffn, rotary_attention, routed_ffn]


def build(nc, dram):
    with ExitStack() as ctx:
        c = Chip(nc, ctx, dram)
        c.ln = {n: c.sem(n) for n in ("ln_mean", "ln_centred", "ln_squared", "ln_var", "ln_log", "ln_rstd")}
        load_start(c)
        for layer in LAYERS:
            layer(c)
            layernorm(c)
        store_end(c)


def columns(*vectors):
    return np.concatenate([np.asarray(v).reshape(-1, P).T for v in vectors], axis=1)


def rows_in(w):
    w = np.asarray(w)
    return w.reshape(-1, P, w.shape[1]).transpose(1, 0, 2)


def quads(w, *at):
    w = np.asarray(w)
    w = w.reshape(GROUPS, QUAD, DH, w.size // P)
    out = np.zeros((w.shape[3], GROUPS, QUAD, 32), w.dtype)
    for offset in at or (0,):
        out[..., offset:offset + DH] = w.transpose(3, 0, 1, 2)
    return out.reshape(w.shape[3], GROUPS, P)


def placed_rows(w):
    w = np.asarray(w).reshape(GROUPS, QUAD, DH, -1)
    out = np.zeros((QUAD, 32, GROUPS + 1, w.shape[3]), w.dtype)
    out[:, :DH, :GROUPS] = w.transpose(1, 2, 0, 3)
    out[:, :DH, GROUPS] = out[:, :DH, 0]
    return out.reshape(P, GROUPS + 1, -1)


PAIRINGS = ((1, 1), (1, 2), (2, 1), (1, 3), (3, 1), (2, 2), (2, 3), (3, 2))


def eights(w):
    w = np.asarray(w).reshape(GROUPS, 2, 2, 1, DH, P)
    return np.broadcast_to(w, (GROUPS, 2, 2, len(PAIRINGS), DH, P)).reshape(GROUPS, 2, P, P).transpose(3, 0, 1, 2)


def part_masks():
    rows = np.repeat(np.array(PAIRINGS), DH, axis=0)
    rows = np.concatenate([rows, rows])
    return np.stack([rows > 1, rows > 2], axis=2).astype(np.float32)


def laid_out(a):
    g = {k: np.asarray(v) for k, v in a.items()}
    L0, L1 = "L0_ffn_", "L1_ffn_"
    o = {
        "xT": g["L0_attn_x"].transpose(2, 0, 1),
        "identity": np.eye(P, dtype=np.float32),
        "tf_w1": g[L0 + "w1_w"].T, "tf_w2": g[L0 + "w2_w"].T, "tf_h1": rows_in(g[L0 + "h1_w"].T),
        "tf_h2": rows_in(g[L0 + "h2_w"].T), "tf_w3": rows_in(g[L0 + "w3_w"].T),
        "tf_s": columns(*(g[L0 + n] for n in ("w1_s", "w2_s", "h1_s", "h2_s", "w3_s"))),
        "hf_sw1": g[L1 + "sw1"], "hf_sw3": g[L1 + "sw3"], "hf_sw2": rows_in(g[L1 + "sw2"]),
        "hf_w1": g[L1 + "w1"].transpose(1, 0, 2), "hf_w2": g[L1 + "w2"].transpose(1, 0, 2),
        "hf_bias": columns(*(g[L1 + n] for n in ("sb1", "sb3", "sb2", "b1", "b2"))),
        "lf_W": g["L2_ffn_W"].T, "lf_V": g["L2_ffn_V_r"].T, "lf_C": g["L2_ffn_C"].T, "lf_b": columns(g["L2_ffn_b"]),
    }
    L3, R6 = "L3_ffn_", "L2_attn_"
    E = 12
    o |= {
        "rf_Wr": g[L3 + "Wr"], "rf_br": np.broadcast_to(g[L3 + "br"], (P, E)),
        "rf_order": np.broadcast_to(100.0 - np.arange(E, dtype=np.float32), (P, E)),
        "rf_pick": np.broadcast_to(np.eye(P, E, dtype=np.float32)[:, :, None], (P, E, P)),
        "rf_be2": np.concatenate([g[L3 + "be2"], np.zeros((P - E, P), np.float32)]), "rf_bias": columns(*(g[L3 + n] for n in ("be1", "bs1", "bs2"))),
        "rf_Ws1": g[L3 + "Ws1"].reshape(P, -1, P), "rf_Ws2": rows_in(g[L3 + "Ws2"]),
        "rf_We1": g[L3 + "We1"].reshape(E, P, -1, P).transpose(1, 0, 2, 3),
        "rf_We2": g[L3 + "We2"].reshape(E, -1, P, P).transpose(2, 0, 1, 3),
        "rw_maa": columns(*(g[R6 + n] for n in ("time_maa_x", "time_maa_w", "time_maa_k", "time_maa_v", "time_maa_r",
                                                "time_decay", "time_faaaa", "ln_g", "ln_b"))),
        "rw_w1": g[R6 + "time_maa_w1"], "rw_w2": g[R6 + "time_maa_w2"].reshape(P, P),
        "rw_dw1": g[R6 + "time_decay_w1"], "rw_dw2": g[R6 + "time_decay_w2"],
        "rw_Wrkv": np.stack([g[R6 + n] for n in ("W_k", "W_v", "W_r")], axis=1), "rw_Wo": g[R6 + "W_o"],
    }
    swap = np.arange(P) ^ 1
    wq, wk, wv = (g["L3_attn_" + n] for n in ("wq", "wk", "wv"))
    two = np.stack([eights(w) for w in (wq, wq[swap], wk, wk[swap])], axis=3)
    w = np.concatenate([two.reshape(P, GROUPS, -1, P), quads(wv)[:, :, None]], axis=2)
    o["ra_W"] = np.concatenate([w, w[:, :1]], axis=1)
    inverse = (1.0 / np.float32(10000.0) ** (np.arange(0, DH, 2, dtype=np.float32) / np.float32(DH))).astype(np.float32)
    angle = np.outer(np.arange(T, dtype=np.float32), inverse).astype(np.float32)
    ch = np.arange(P) % DH
    cos, sin = np.cos(angle).T[ch // 2], np.sin(angle).T[ch // 2] * np.where(ch % 2, 1, -1)[:, None]
    o["ra_rope"] = np.stack([cos * DH ** -0.5, sin * DH ** -0.5, cos, sin], axis=1).astype(np.float32)
    o["ra_mask"] = part_masks()
    o["ra_place"] = placed_rows(np.eye(P, dtype=np.float32))
    D = "L1_attn_"
    at = {"q": (0, DH), "k": (0, 2 * DH), "v": (0,), "pk": (DH,), "pq": (2 * DH,)}
    w = np.stack([quads(g[D + "W" + n], *k) for n, k in at.items()], axis=2)
    o["da_W"] = np.concatenate([w, w[:, :1]], axis=1)
    o["da_bias"] = np.stack([quads(g[D + "b" + n], *k)[0].T for n, k in at.items()], axis=2)
    rel = g[D + "rel_emb"].T
    o |= {"da_rel": np.stack([rel, rel[:, ::-1]], axis=1), "da_bo": columns(g[D + "bo"])}
    o["da_place"] = placed_rows(g[D + "Wo"].T)
    only = (np.arange(P)[:, None] // 32 == np.arange(QUAD)).astype(np.float32)
    o["da_only"] = np.stack([only, only * np.float32((DH * 3) ** -0.5)], axis=1)
    D = "L0_attn_"
    for n in "kqvag":
        o["dl_W" + n] = g[D + "W" + n].T
    cw = np.stack([g[D + n + "cw"][:, 0, :].T for n in "kqv"])
    o["dl_cw"] = np.broadcast_to(cw, (P, *cw.shape))
    o["dl_Wo"] = rows_in(g[D + "Wo"].T)
    head = np.zeros((2, 2, B, 8), int) + 2 * np.arange(8) + np.arange(2)[:, None, None, None]
    batch = np.zeros((2, 2, B, 8), int) + np.arange(B)[:, None]
    head, batch = head.ravel(), batch.ravel()
    Wb = np.zeros((P, B, P), np.float32)
    for b in range(B):
        Wb[:, b, batch == b] = g[D + "Wb"].T[:, head[batch == b]]
    o["dl_Wb"] = Wb
    o["dl_vec"] = np.concatenate([columns(*(g[D + n] for n in ("kcb", "qcb", "vcb", "ba"))), g[D + "bb"][head][:, None],
                                  np.tile(g[D + "ln_w"], 2)[:, None], np.tile(g[D + "ln_b"], 2)[:, None]], axis=1)
    same = (np.arange(P)[:, None] // 64 == np.arange(P)[None, :] // 64).astype(np.float32)
    o["dl_sums"] = np.stack([same, same / 64, np.eye(P, dtype=np.float32) - same / 64], axis=1)
    o["dl_eye"] = np.concatenate([np.eye(64, dtype=np.float32)] * 2)
    ch = np.arange(P)
    spread = np.zeros((P, 16, P), np.float32)
    for j in range(16):
        spread[(ch // 16) * 16 + j, j, ch] = 1.0
    o["rw_spread"], o["rw_gather"] = spread, spread.transpose(2, 1, 0)
    o["rw_heads"] = (ch[:, None] // 16 == ch[None, :] // 16).astype(np.float32)
    return o


def kernel(**inputs):
    import concourse.bacc as bacc
    from concourse.bass_utils import run_bass_kernel_spmd

    nc = bacc.Bacc("TRN2", target_bir_lowering=False, num_devices=1)
    arrays, dram = {}, {}
    for name, a in laid_out(inputs).items():
        a = np.ascontiguousarray(a)
        arrays[f"in_{name}"] = a
        dram[name] = nc.dram_tensor(f"in_{name}", a.shape, mybir.dt.from_np(a.dtype), kind="ExternalInput").ap()
    dram["outT"] = nc.dram_tensor("outT", (P, B, T), F32, kind="ExternalOutput").ap()
    build(nc, dram)
    r = run_bass_kernel_spmd(nc, [arrays], core_ids=[0])
    return np.ascontiguousarray(r.results[0]["outT"].transpose(1, 2, 0))
```
